# Optimizing a Trainium2 kernel written in Bass

```python
import numpy as np
import jax
import jax.numpy as jnp

def _softmax(x, axis=-1):
    return jax.nn.softmax(x, axis=axis)

def _gelu(x):
    return jax.nn.gelu(x, approximate=True)

def _silu(x):
    return jax.nn.silu(x)

def _sigmoid(x):
    return jax.nn.sigmoid(x)

def _layernorm(x, axis=-1, eps=1e-05):
    m = jnp.mean(x, axis=axis, keepdims=True)
    v = jnp.var(x, axis=axis, keepdims=True)
    return (x - m) / jnp.sqrt(v + eps)

def _scatter_add(tgt, idx, src, axis=0):
    return tgt.at[idx].add(src)

def _segment_sum(src, seg, n):
    return jax.ops.segment_sum(src, seg, n)
kernel_name = 'mk_seq_postln_d2_jaxref_r4_bee1ac'

def setup_inputs(seed: int=0):
    np.random.seed(seed)
    _w = jnp.asarray

    def _L0_attn_setup():
        import jax, jax.numpy as jnp
        import numpy as np
        NUM_HEADS = 16
        key = jax.random.key(seed)
        ks = jax.random.split(key, 6)
        B, S, D = (2, 512, 512)
        scale = 1.0 / np.sqrt(D)
        return {'x': jax.random.normal(ks[0], (B, S, D), dtype=jnp.float32), 'wq': jax.random.normal(ks[1], (D, D), dtype=jnp.float32) * scale, 'wk': jax.random.normal(ks[2], (D, D), dtype=jnp.float32) * scale, 'wv': jax.random.normal(ks[3], (D, D), dtype=jnp.float32) * scale, 'wo': jax.random.normal(ks[4], (D, D), dtype=jnp.float32) * scale, 'bo': jax.random.normal(ks[5], (D,), dtype=jnp.float32) * 0.01}
    _L0_attn_in = _L0_attn_setup()

    def _L0_ffn_setup():
        import jax, jax.numpy as jnp
        import numpy as np
        THRESHOLD = 0.05
        ACT_BITS = 4
        QMAX = 2 ** (ACT_BITS - 1) - 1
        EPS = 1e-08

        def ternarize(W, threshold):
            absW = jnp.abs(W)
            delta = threshold * jnp.max(absW)
            mask = absW > delta
            n = jnp.maximum(jnp.sum(mask), 1)
            alpha = jnp.sum(jnp.where(mask, absW, 0.0)) / n
            Wt = alpha * jnp.sign(W) * mask
            return W + jax.lax.stop_gradient(Wt - W)

        def ternary_linear(x, W, b, threshold=THRESHOLD):
            Wq = ternarize(W, threshold)
            return jnp.einsum('bsd,hd->bsh', x, Wq) + b

        def fp4_activation(x):
            scale = jnp.max(jnp.abs(x)) / QMAX + EPS
            q = jnp.clip(jnp.round(x / scale), -QMAX, QMAX) * scale
            return x + jax.lax.stop_gradient(q - x)
        key = jax.random.key(seed)
        k1, k2, k3, k4, k5 = jax.random.split(key, 5)
        B, S, D, H = (2, 1024, 512, 2048)
        x = jax.random.normal(k1, (B, S, D), dtype=jnp.float32)
        W1 = jax.random.normal(k2, (H, D), dtype=jnp.float32) * (1.0 / np.sqrt(D))
        b1 = jax.random.normal(k3, (H,), dtype=jnp.float32) * 0.02
        W2 = jax.random.normal(k4, (D, H), dtype=jnp.float32) * (1.0 / np.sqrt(H))
        b2 = jax.random.normal(k5, (D,), dtype=jnp.float32) * 0.02
        return {'x': x, 'W1': W1, 'b1': b1, 'W2': W2, 'b2': b2}
    _L0_ffn_in = _L0_ffn_setup()

    def _L1_attn_setup():
        import jax, jax.numpy as jnp
        import numpy as np
        D_MODEL = 512
        N_HEADS = 16
        D_K = D_MODEL // N_HEADS
        EPS = 1e-06
        key = jax.random.key(seed)
        ks = jax.random.split(key, 9)
        s = 1.0 / np.sqrt(D_MODEL)
        return {'x': jax.random.normal(ks[0], (4, 1024, D_MODEL), dtype=jnp.float32), 'Wq': jax.random.normal(ks[1], (D_MODEL, D_MODEL), dtype=jnp.float32) * s, 'bq': jnp.zeros((D_MODEL,), dtype=jnp.float32), 'Wk': jax.random.normal(ks[2], (D_MODEL, D_MODEL), dtype=jnp.float32) * s, 'bk': jnp.zeros((D_MODEL,), dtype=jnp.float32), 'Wv': jax.random.normal(ks[3], (D_MODEL, D_MODEL), dtype=jnp.float32) * s, 'bv': jnp.zeros((D_MODEL,), dtype=jnp.float32), 'Wo': jax.random.normal(ks[4], (D_MODEL, D_MODEL), dtype=jnp.float32) * s, 'bo': jnp.zeros((D_MODEL,), dtype=jnp.float32)}
    _L1_attn_in = _L1_attn_setup()

    def _L1_ffn_setup():
        import jax, jax.numpy as jnp
        import numpy as np
        key = jax.random.key(seed)
        k1, k2, k3, k4, k5 = jax.random.split(key, 5)
        B, L, H, N = (2, 512, 512, 2048)
        x = jax.random.normal(k1, (B, L, H), dtype=jnp.float32)
        W0 = jax.random.normal(k2, (N, H), dtype=jnp.float32) * (1.0 / np.sqrt(H))
        bias0 = jax.random.normal(k3, (N,), dtype=jnp.float32) * 0.02
        W1 = jax.random.normal(k4, (H, N), dtype=jnp.float32) * (1.0 / np.sqrt(N))
        bias1 = jax.random.normal(k5, (H,), dtype=jnp.float32) * 0.02
        return {'x': x, 'W0': W0, 'bias0': bias0, 'W1': W1, 'bias1': bias1}
    _L1_ffn_in = _L1_ffn_setup()
    _d = {'L0_attn_x': _L0_attn_in['x'], 'L0_attn_wq': _L0_attn_in['wq'], 'L0_attn_wk': _L0_attn_in['wk'], 'L0_attn_wv': _L0_attn_in['wv'], 'L0_attn_wo': _L0_attn_in['wo'], 'L0_attn_bo': _L0_attn_in['bo'], 'L0_ffn_W1': _L0_ffn_in['W1'], 'L0_ffn_b1': _L0_ffn_in['b1'], 'L0_ffn_W2': _L0_ffn_in['W2'], 'L0_ffn_b2': _L0_ffn_in['b2'], 'L1_attn_Wq': _L1_attn_in['Wq'], 'L1_attn_bq': _L1_attn_in['bq'], 'L1_attn_Wk': _L1_attn_in['Wk'], 'L1_attn_bk': _L1_attn_in['bk'], 'L1_attn_Wv': _L1_attn_in['Wv'], 'L1_attn_bv': _L1_attn_in['bv'], 'L1_attn_Wo': _L1_attn_in['Wo'], 'L1_attn_bo': _L1_attn_in['bo'], 'L1_ffn_W0': _L1_ffn_in['W0'], 'L1_ffn_bias0': _L1_ffn_in['bias0'], 'L1_ffn_W1': _L1_ffn_in['W1'], 'L1_ffn_bias1': _L1_ffn_in['bias1']}
    _x0 = _d['L0_attn_x']
    _d['L0_attn_x'] = jax.random.normal(jax.random.fold_in(jax.random.key(seed), 1), (4, 1024, 512), dtype=_x0.dtype)
    del _x0
    return _d

def reference(L0_attn_x, L0_attn_wq, L0_attn_wk, L0_attn_wv, L0_attn_wo, L0_attn_bo, L0_ffn_W1, L0_ffn_b1, L0_ffn_W2, L0_ffn_b2, L1_attn_Wq, L1_attn_bq, L1_attn_Wk, L1_attn_bk, L1_attn_Wv, L1_attn_bv, L1_attn_Wo, L1_attn_bo, L1_ffn_W0, L1_ffn_bias0, L1_ffn_W1, L1_ffn_bias1):

    def _L0_attn_ref(x, wq, wk, wv, wo, bo):
        import jax, jax.numpy as jnp
        import numpy as np
        NUM_HEADS = 16
        B, S, D = x.shape
        H = NUM_HEADS
        hd = D // H
        q = (x @ wq).reshape(B, S, H, hd).transpose(0, 2, 1, 3)
        k = (x @ wk).reshape(B, S, H, hd).transpose(0, 2, 1, 3)
        v = (x @ wv).reshape(B, S, H, hd).transpose(0, 2, 1, 3)
        scores = jnp.einsum('bhqd,bhkd->bhqk', q, k) / jnp.sqrt(jnp.asarray(hd, x.dtype))
        causal = jnp.tril(jnp.ones((S, S), dtype=bool))
        scores = jnp.where(causal, scores, jnp.finfo(x.dtype).min)
        attn = jax.nn.softmax(scores, axis=-1)
        ctx = jnp.einsum('bhqk,bhkd->bhqd', attn, v)
        ctx = ctx.transpose(0, 2, 1, 3).reshape(B, S, D)
        return ctx @ wo + bo

    def _L0_ffn_ref(x, W1, b1, W2, b2):
        import jax, jax.numpy as jnp
        import numpy as np
        THRESHOLD = 0.05
        ACT_BITS = 4
        QMAX = 2 ** (ACT_BITS - 1) - 1
        EPS = 1e-08

        def ternarize(W, threshold):
            absW = jnp.abs(W)
            delta = threshold * jnp.max(absW)
            mask = absW > delta
            n = jnp.maximum(jnp.sum(mask), 1)
            alpha = jnp.sum(jnp.where(mask, absW, 0.0)) / n
            Wt = alpha * jnp.sign(W) * mask
            return W + jax.lax.stop_gradient(Wt - W)

        def ternary_linear(x, W, b, threshold=THRESHOLD):
            Wq = ternarize(W, threshold)
            return jnp.einsum('bsd,hd->bsh', x, Wq) + b

        def fp4_activation(x):
            scale = jnp.max(jnp.abs(x)) / QMAX + EPS
            q = jnp.clip(jnp.round(x / scale), -QMAX, QMAX) * scale
            return x + jax.lax.stop_gradient(q - x)
        h = ternary_linear(x, W1, b1)
        h = jax.nn.gelu(h, approximate=False)
        y = ternary_linear(h, W2, b2)
        return fp4_activation(y)

    def _L1_attn_ref(x, Wq, bq, Wk, bk, Wv, bv, Wo, bo):
        import jax, jax.numpy as jnp
        import numpy as np
        D_MODEL = 512
        N_HEADS = 16
        D_K = D_MODEL // N_HEADS
        EPS = 1e-06
        b, n, _ = x.shape
        h, d = (N_HEADS, D_K)

        def proj(W, bias):
            y = jnp.einsum('bnm,dm->bnd', x, W) + bias
            return y.reshape(b, n, h, d).transpose(0, 2, 1, 3)
        Q = jax.nn.relu(proj(Wq, bq))
        K = jax.nn.relu(proj(Wk, bk))
        V = proj(Wv, bv)
        pos = jnp.arange(n, dtype=x.dtype)
        decay = jnp.exp(-pos / n)[None, None, :, None]
        Q = Q * decay
        K = K * decay
        KV = jnp.einsum('bhnd,bhne->bhde', K, V)
        Ksum = K.sum(axis=2)
        Z = 1.0 / (jnp.einsum('bhnd,bhd->bhn', Q, Ksum)[..., None] + EPS)
        out = jnp.einsum('bhnd,bhde->bhne', Q, KV) * Z
        out = out.transpose(0, 2, 1, 3).reshape(b, n, h * d)
        return jnp.einsum('bnm,dm->bnd', out, Wo) + bo

    def _L1_ffn_ref(x, W0, bias0, W1, bias1):
        import jax, jax.numpy as jnp
        import numpy as np
        B, L, H = x.shape
        X = x.reshape(-1, H).astype(jnp.float16)
        D = jnp.dot(X.astype(jnp.float32), W0.T) + bias0
        D = jax.nn.gelu(D, approximate=False).astype(jnp.float16)
        E = jnp.dot(D.astype(jnp.float32), W1.T) + bias1
        return E.astype(jnp.float16).reshape(B, L, H)
    x = L0_attn_x
    x = _layernorm(x + _L0_attn_ref(x, L0_attn_wq, L0_attn_wk, L0_attn_wv, L0_attn_wo, L0_attn_bo), axis=-1)
    x = _layernorm(x + _L0_ffn_ref(x, L0_ffn_W1, L0_ffn_b1, L0_ffn_W2, L0_ffn_b2), axis=-1)
    x = _layernorm(x + _L1_attn_ref(x, L1_attn_Wq, L1_attn_bq, L1_attn_Wk, L1_attn_bk, L1_attn_Wv, L1_attn_bv, L1_attn_Wo, L1_attn_bo), axis=-1)
    x = _layernorm(x + _L1_ffn_ref(x, L1_ffn_W0, L1_ffn_bias0, L1_ffn_W1, L1_ffn_bias1), axis=-1)
    return x

_drawn_inputs = setup_inputs


def setup_inputs(seed=0):
    import zlib

    import numpy as np

    out = dict(_drawn_inputs(seed))
    spreads = {'L1_attn_bq': (0.0, 0.8),
     'L1_attn_bk': (0.0, 0.8),
     'L1_attn_bv': (0.0, 0.1),
     'L1_attn_bo': (0.0, 0.1)}
    factors = {'L1_attn_Wq': 3.423, 'L1_attn_Wk': 2.792, 'L1_ffn_bias0': 5.683, 'L1_ffn_bias1': 4.015}
    for name, (base, spread) in spreads.items():
        noise = np.random.default_rng([zlib.crc32(name.encode()), seed]).standard_normal(out[name].shape)
        drawn = base * np.exp(spread * noise) if base else spread * noise
        out[name] = jnp.asarray(drawn.astype(out[name].dtype))
    for name, factor in factors.items():
        out[name] = (out[name] * factor).astype(out[name].dtype)
    return out
```

```python
from contextlib import ExitStack

import numpy as np

import concourse.bass as bass
from concourse import mybir

F32 = mybir.dt.float32
F32R = mybir.dt.float32r
F16 = mybir.dt.float16
ALU = mybir.AluOpType
ACT = mybir.ActivationFunctionType
AX = mybir.AxisListType

P = 128
BATCH, SEQ, D, HID = 4, 1024, 512, 2048
HEADS = 16
HD = D // HEADS
KT = D // P
HT = HID // P
CH = 512
NCH = BATCH * SEQ // CH
CT = CH // P
GROUPS = D // P
HPG = P // HD
SM_SCALE = 1.0 / float(np.sqrt(np.float32(HD)))
LN_EPS = 1e-5
FP4_EPS = 1e-8
QMAX = 7.0
LIN_EPS = 1e-6
TERN = 0.05
ROUND = 12582912.0
FLOOR = -3.0e38


class Phase(ExitStack):

    def __init__(self, nc):
        super().__init__()
        self.nc, self.semaphores = nc, []

    def semaphore(self, name):
        handle = self.nc.alloc_semaphore(name=name)
        self.semaphores.append(handle)
        return handle

    def __exit__(self, *exc):
        self.nc.clear_and_free_semaphores(self.semaphores)
        self.nc.all_engine_barrier()
        return super().__exit__(*exc)


def f32(ap):
    return ap.bitcast(F32)


def split_loader(nc, ctx, name, stage, jobs):
    loaded = [ctx.semaphore(f"{name}_loaded{k}") for k in range(2)]
    hi_done = ctx.semaphore(f"{name}_hi")
    lo_done = ctx.semaphore(f"{name}_lo")

    def load(sp):
        for n, (src, _, _) in enumerate(jobs):
            if n >= 2:
                sp.wait_ge(lo_done, n - 1)
            sp.dma_start(stage[:, n % 2, :], src).then_inc(loaded[n % 2], 16)

    def split_hi(act):
        for n, (_, hi, _) in enumerate(jobs):
            act.wait_ge(loaded[n % 2], 16 * (n // 2 + 1))
            act.activation(hi, stage[:, n % 2, :], ACT.Copy).then_inc(hi_done, 1)

    def split_lo(dve):
        for n, (_, hi, lo) in enumerate(jobs):
            dve.wait_ge(hi_done, n + 1)
            dve.tensor_tensor(lo, stage[:, n % 2, :], f32(hi), ALU.subtract).then_inc(lo_done, 1)

    return load, split_hi, split_lo, lo_done, len(jobs)


def build_constants(nc, ctx):
    ident = ctx.enter_context(nc.sbuf_tensor("ident", [P, P], F32))
    zeroed = ctx.semaphore("ident_zeroed")
    with nc.Block() as block:
        @block.gpsimd
        def _(pool):
            pool.memset(ident[:, :], 0.0).then_inc(zeroed, 1)
            pool.wait_ge(zeroed, 1)
            pool.affine_select(out=ident[:, :], in_=ident[:, :], compare_op=ALU.not_equal, fill=1.0,
                               base=0, pattern=[[-1, P]], channel_multiplier=1).then_inc(zeroed, 1)
            pool.wait_ge(zeroed, 2)
    return ident


def phase_qkv0(nc, psum, ident, x, wq, wk, wv, q_dram, k_dram, v_dram):
    OUTS = 2 * GROUPS + CT
    with Phase(nc) as ctx:
        sb = lambda n, s, d: ctx.enter_context(nc.sbuf_tensor(n, s, d))
        sem = lambda n: ctx.semaphore(n)
        stage = sb("p1_stage", [P, 2, KT * D], F32)
        w_hi = sb("p1_w_hi", [P, 3, KT, D], F32R)
        w_lo = sb("p1_w_lo", [P, 3, KT, D], F32R)
        xs = sb("p1_x", [P, CT, D], F32)
        xT_hi = sb("p1_xT_hi", [P, 2, KT, CH], F32R)
        xT_lo = sb("p1_xT_lo", [P, 2, KT, CH], F32R)
        qk_out = sb("p1_qk_out", [P, 4, 2, CH], F32R)
        v_out = sb("p1_v_out", [P, CT, D], F32)
        jobs = [(w.rearrange("(k p) n -> p k n", p=P),
                 w_hi[:, n, :, :].rearrange("p k n -> p (k n)"), w_lo[:, n, :, :].rearrange("p k n -> p (k n)"))
                for n, w in enumerate((wq, wk, wv))]
        stage_v = stage[:, :, :]
        load_w, split_hi, split_lo, w_done, n_w = split_loader(nc, ctx, "p1_w", stage_v, jobs)
        x_loaded = sem("p1_x_loaded")
        xt_ready = sem("p1_xt_ready")
        xt_hi = sem("p1_xt_hi")
        xt_lo = sem("p1_xt_lo")
        proj = sem("p1_proj")
        qk_hi = sem("p1_qk_hi")
        qk_lo = sem("p1_qk_lo")
        v_copied = sem("p1_v_copied")
        qk_stored = [sem(f"p1_qk_stored{k}") for k in range(4)]
        v_stored = [sem(f"p1_v_stored{t}") for t in range(CT)]
        x_v = x.rearrange("b (c t p) d -> b c p t d", c=2, p=P)

        with nc.Block() as block:
            @block.gpsimd
            def _(pool):
                with pool.Fori(0, BATCH) as b:
                    for c in range(2):
                        pool.wait_ge(xt_ready, 8 * b + 4 * c)
                        pool.dma_start(xs[:, :, :], x_v[b, c]).then_inc(x_loaded, 16)

            @block.sync
            def _(sp):
                load_w(sp)
                with sp.Fori(0, BATCH) as b:
                    for c in range(2):
                        for j in range(2 * GROUPS):
                            dst = (q_dram, k_dram)[j % 2]
                            dst_v = dst[bass.ds(4 * b + j // 2, 1), :, :, c * CH:(c + 1) * CH].rearrange("o s p t -> p (o s) t")
                            sp.wait_ge(qk_lo, 8 + 16 * b + 8 * c + j + 1)
                            sp.dma_start(dst_v, f32(qk_out[:, j % 4, :, :])).then_inc(qk_stored[j % 4], 16)
                        for t in range(CT):
                            r0 = c * CH + t * P
                            dst_v = v_dram[bass.ds(4 * b, 4), r0:r0 + P, :].rearrange("g p e -> p g e")
                            sp.wait_ge(v_copied, 4 + 8 * b + 4 * c + t + 1)
                            sp.dma_start(dst_v, v_out[:, t, :].rearrange("p (g e) -> p g e", g=GROUPS)).then_inc(v_stored[t], 16)
                for k in range(4):
                    sp.wait_ge(qk_stored[k], 16 * 4 * BATCH)
                for t in range(CT):
                    sp.wait_ge(v_stored[t], 16 * 2 * BATCH)

            @block.tensor
            def _(pe):
                pe.sem_inc(proj, 2 * OUTS)
                with pe.Fori(0, BATCH) as b:
                    for c in range(2):
                        pe.wait_ge(x_loaded, 32 * b + 16 * c + 16)
                        for kt in range(KT):
                            pe.wait_ge(xt_lo, 8 * b + 4 * c + kt + 1)
                            for t in range(CT):
                                mm = pe.transpose(psum[:, kt % 2, t * P:(t + 1) * P], xs[:, t, kt * P:(kt + 1) * P], ident[:, :])
                            mm.then_inc(xt_ready, 1)
                        pe.wait_ge(xt_lo, 2 + 8 * b + 4 * c + 4)
                        pe.wait_ge(w_done, n_w)
                        for o in range(OUTS):
                            if o < 2:
                                pe.wait_ge(qk_lo, 16 * b + 8 * c + 7 + o)
                            elif o < 6:
                                pe.wait_ge(v_copied, 8 * b + 4 * c + o - 1)
                            else:
                                pe.wait_ge(qk_lo, 8 + 16 * b + 8 * c + o - 5)
                            bank = psum[:, 2 + o % 6, :]
                            n = 0
                            for kt in range(KT):
                                for part in range(3):
                                    xp = (xT_hi, xT_lo, xT_hi)[part]
                                    wp = (w_hi, w_hi, w_lo)[part]
                                    if o < 2 * GROUPS:
                                        g = o // 2
                                        lhsT, rhs = wp[:, o % 2, kt, g * P:(g + 1) * P], xp[:, c, kt, :]
                                    else:
                                        t = o - 2 * GROUPS
                                        lhsT, rhs = xp[:, c, kt, t * P:(t + 1) * P], wp[:, 2, kt, :]
                                    mm = pe.matmul(bank, lhsT, rhs, start=(n == 0), stop=(n == 3 * KT - 1))
                                    n += 1
                            mm.then_inc(proj, 1)

            @block.scalar
            def _(act):
                split_hi(act)
                act.sem_inc(v_copied, 4)
                with act.Fori(0, BATCH) as b:
                    for c in range(2):
                        for kt in range(KT):
                            if kt == 0:
                                act.wait_ge(proj, 24 * b + 12 * c + 12)
                            act.wait_ge(xt_ready, 8 * b + 4 * c + kt + 1)
                            act.activation(xT_hi[:, c, kt, :], psum[:, kt % 2, :], ACT.Copy).then_inc(xt_hi, 1)
                        for o in range(OUTS):
                            bank = psum[:, 2 + o % 6, :]
                            act.wait_ge(proj, 2 * OUTS + 24 * b + 12 * c + o + 1)
                            if o < 2 * GROUPS:
                                act.wait_ge(qk_stored[o % 4], 64 * b + 32 * c + 16 * (o // 4))
                                act.activation(qk_out[:, o % 4, 0, :], bank, ACT.Copy).then_inc(qk_hi, 1)
                            else:
                                t = o - 2 * GROUPS
                                act.wait_ge(v_stored[t], 32 * b + 16 * c)
                                act.activation(v_out[:, t, :], bank, ACT.Copy).then_inc(v_copied, 1)

            @block.vector
            def _(dve):
                dve.sem_inc(xt_lo, 2)
                dve.sem_inc(qk_lo, 8)
                split_lo(dve)
                with dve.Fori(0, BATCH) as b:
                    for c in range(2):
                        for kt in range(KT):
                            dve.wait_ge(xt_hi, 8 * b + 4 * c + kt + 1)
                            dve.tensor_tensor(xT_lo[:, c, kt, :], psum[:, kt % 2, :], f32(xT_hi[:, c, kt, :]),
                                              ALU.subtract).then_inc(xt_lo, 1)
                        for j in range(2 * GROUPS):
                            dve.wait_ge(qk_hi, 16 * b + 8 * c + j + 1)
                            dve.tensor_tensor(qk_out[:, j % 4, 1, :], psum[:, 2 + j % 6, :], f32(qk_out[:, j % 4, 0, :]),
                                              ALU.subtract).then_inc(qk_lo, 1)


def phase_attention(nc, psum, ident, q_dram, k_dram, v_dram, o_dram):
    NU = BATCH * GROUPS
    DOWN = SEQ // P
    PER_UNIT = HPG * CT
    S_PER_GROUP = 2 * (PER_UNIT + 1)
    STEPS = [CT, 2 * CT]
    ST_PER_GROUP = HPG * sum(STEPS)
    J_PER_GROUP = sum(STEPS)
    KEY_STEPS = [(0, j) for j in range(STEPS[0])] + [(1, j) for j in range(STEPS[1])]
    LOADS = 6 * 16
    with Phase(nc) as ctx:
        sb = lambda n, s, d: ctx.enter_context(nc.sbuf_tensor(n, s, d))
        sem = lambda n: ctx.semaphore(n)
        kst = [sb(f"p2_kst{s}", [P, HPG, SEQ], F32R) for s in range(2)]
        qst = [sb(f"p2_qst{s}", [P, HPG, SEQ], F32R) for s in range(2)]
        vs = [sb(f"p2_v{s}", [P, DOWN, P], F32) for s in range(2)]
        probs = sb("p2_probs", [P, 2, HPG, CH], F32)
        junk = sb("p2_junk", [P, 2, SEQ], F32)
        rowmax = sb("p2_rowmax", [P, 2, PER_UNIT], F32)
        negmax = sb("p2_negmax", [P, 2, 2, PER_UNIT], F32R)
        causal = sb("p2_causal", [P, SEQ], F32)
        pick = sb("p2_pick", [2 * PER_UNIT, PER_UNIT], F32)
        ones = sb("p2_ones", [P, HD], F32)
        o_raw = sb("p2_o_raw", [P, 2, CH], F32)
        recip = sb("p2_recip", [P, CH], F32)
        o_out = sb("p2_o_out", [P, 2, CH], F32)

        const_done = sem("p2_const_done")
        CONSTS = 8
        loaded = [[sem(f"p2_loaded{s}_{c}") for c in range(2)] for s in range(2)]
        v_loaded = [sem(f"p2_v_loaded{s}") for s in range(2)]
        s_ready = sem("p2_s_ready")
        s_used = sem("p2_s_used")
        rm_done = sem("p2_rm_done")
        nm_ready = sem("p2_nm_ready")
        st_ready = sem("p2_st_ready")
        p_ready = sem("p2_p_ready")
        p_masked = sem("p2_p_masked")
        pv_done = sem("p2_pv_done")
        rec_done = sem("p2_rec_done")
        o_read = sem("p2_o_read")
        o_normed = sem("p2_o_normed")
        passed = sem("p2_passed")
        o_stored = [sem(f"p2_o_stored{c}") for c in range(2)]

        ENTRIES = [(0, e // HPG, e % HPG) for e in range(PER_UNIT)] + [(1, e // HPG, e % HPG) for e in range(PER_UNIT)]
        ENTRIES.insert(PER_UNIT + 3, (0, None, None))
        ENTRIES.append((1, None, None))
        BUILT = [PER_UNIT + 4, S_PER_GROUP]
        NORM0 = 4 * (STEPS[0] + 1)
        QUARTER = list(range(NORM0 - 10, NORM0)) + list(range(NORM0 + 4, 4 * J_PER_GROUP))
        assert len(QUARTER) == S_PER_GROUP
        BESIDE_C0 = sum(q < NORM0 for q in QUARTER)

        S_BANKS = [psum[:, 0:2, :].rearrange("p a n -> p (a n)"), psum[:, 2:4, :].rearrange("p a n -> p (a n)")]
        ST_BANKS = [psum[:, 4, :], psum[:, 5, :]]
        O_BANK, SUM_BANK = psum[:, 6, :], psum[:, 7, :]

        def half(eng, body):
            with eng.Fori(0, NU // 2 - 1) as i:
                body(i, False)
            body(NU // 2 - 1, True)

        with nc.Block() as block:
            @block.gpsimd
            def _(pool):
                def build(n, ins):
                    ins.then_inc(const_done, 1)
                    pool.wait_ge(const_done, n)
                build(1, pool.memset(causal[:, :], 0.0))
                build(2, pool.memset(pick[:, :], 0.0))
                build(3, pool.memset(ones[:, :], 1.0))
                for s in range(2):
                    build(4 + s, pool.memset(f32(kst[s][96:128, :, :]), 1.0))
                tri = causal[:, SEQ - P:SEQ]
                build(6, pool.affine_select(out=tri, in_=tri, compare_op=ALU.is_ge, fill=FLOOR, base=0,
                                            pattern=[[-1, P]], channel_multiplier=1))
                for k in range(2):
                    build(7 + k, pool.affine_select(out=pick[:, :], in_=pick[:, :], compare_op=ALU.not_equal, fill=1.0,
                                                    base=-PER_UNIT * k, pattern=[[-1, PER_UNIT]], channel_multiplier=1))

                def body(i, last):
                    for s in range(2):
                        for step, (c, j) in enumerate(KEY_STEPS):
                            for g in range(HPG):
                                if j >= CT * c:
                                    at = ST_PER_GROUP * s + HPG * step + g + 1
                                    q0 = P * j - CH * c
                                    blk = probs[:, step % 2, g, q0:q0 + P]
                                    pool.wait_ge(p_ready, 2 + 2 * ST_PER_GROUP * i + at)
                                    pool.sem_inc(passed, 1)
                                    pool.affine_select(out=blk, in_=blk, compare_op=ALU.is_ge, fill=0.0, base=0,
                                                       pattern=[[1, P]], channel_multiplier=-1).then_inc(p_masked, 1)
                half(pool, body)

            @block.sync
            def _(sp):
                def load(u, s, k):
                    for c in range(2):
                        cols = slice(c * CH, (c + 1) * CH)
                        for dst, src, rows in ((qst, q_dram, (0, 0, 1)), (kst, k_dram, (0, 1, 0))):
                            for r, part in enumerate(rows):
                                view = src[u, part].rearrange("(h d) t -> d h t", d=HD)[:, :, cols]
                                sp.dma_start(f32(dst[s][r * HD:(r + 1) * HD, :, cols]), view).then_inc(loaded[s][c], 16)
                    sp.dma_start(vs[s][:, :, :], v_dram[u].rearrange("(t p) e -> p t e", p=P)).then_inc(v_loaded[s], 16)

                def store(u, c, n):
                    sp.wait_ge(o_normed, n + 1)
                    sp.dma_start(o_dram[u, :, c * CH:(c + 1) * CH], o_out[:, c, :]).then_inc(o_stored[c], 16)

                load(0, 0, 0)
                load(1, 1, 0)

                def body(i, last):
                    for s in range(2):
                        store(2 * i + s, 0, 4 * i + 2 * s)
                        if not last:
                            sp.wait_ge(pv_done, 2 + J_PER_GROUP * (2 * i + s + 1))
                            load(2 * i + 2 + s, s, i + 1)
                        store(2 * i + s, 1, 4 * i + 2 * s + 1)
                half(sp, body)
                for c in range(2):
                    sp.wait_ge(o_stored[c], 16 * NU)

            @block.tensor
            def _(pe):
                def score_entry(u, s, m):
                    c, tile, g = ENTRIES[m]
                    bank = S_BANKS[m % 2]
                    pe.wait_ge(s_used, S_PER_GROUP * u + m + 1)
                    if tile is None:
                        pe.wait_ge(nm_ready, 2 * u + c + 1)
                        pe.transpose(bank[0:2 * PER_UNIT, 0:P], f32(negmax[:, c, :, :]).rearrange("p a n -> p (a n)"),
                                     ident[:, :]).then_inc(s_ready, 1)
                        return
                    t = CT * c + tile
                    n = P * (t + 1)
                    for k0 in range(0, n, CH):
                        k1 = min(n, k0 + CH)
                        mm = pe.matmul(bank[:, k0:k1], qst[s][0:96, g, t * P:(t + 1) * P],
                                       kst[s][0:96, g, k0:k1], start=True, stop=True)
                    mm.then_inc(s_ready, 1)

                def scores_T(u, s, c, j, st):
                    q0, g = max(0, P * j - CH * c), st % HPG
                    pe.wait_ge(p_ready, ST_PER_GROUP * u + st + 1)
                    if j == 0 and g == 0:
                        pe.wait_ge(s_used, 2 + S_PER_GROUP * u + BUILT[c])
                    pe.matmul(ST_BANKS[st % 2][:, q0:CH], kst[s][:, g, j * P:(j + 1) * P],
                              qst[s][:, g, c * CH + q0:(c + 1) * CH], start=True, stop=True).then_inc(st_ready, 1)

                def with_v(u, s, c, j, step, use_ones):
                    q0 = max(0, P * j - CH * c)
                    if not use_ones:
                        if (c, j) == (0, 0):
                            pe.wait_ge(v_loaded[s], 8 * u + 16 - 8 * s)
                        if j == 0:
                            pe.wait_ge(o_read, 2 * u + c + 1)
                        pe.wait_ge(p_ready, 2 + ST_PER_GROUP * u + HPG * (step + 1))
                        if j >= CT * c:
                            pe.wait_ge(p_masked, PER_UNIT * (2 * u + c) + HPG * (j - CT * c + 1))
                    bank = SUM_BANK if use_ones else O_BANK
                    for g in range(HPG):
                        lhsT = ones[:, :] if use_ones else vs[s][:, j, g * HD:(g + 1) * HD]
                        mm = pe.matmul(bank[g * HD:(g + 1) * HD, q0:CH], lhsT, probs[:, step % 2, g, q0:CH],
                                       start=(j == 0), stop=(j == STEPS[c] - 1))
                    if use_ones:
                        mm.then_inc(pv_done, 1)

                def second_pass(i, last):
                    before = None
                    for s in range(2):
                        u = 2 * i + s
                        entries = [] if last and s == 1 else list(range(S_PER_GROUP))
                        for step, (c, j) in enumerate(KEY_STEPS):
                            for quarter in range(4):
                                if quarter % 2 == 0:
                                    scores_T(u, s, c, j, HPG * step + quarter)
                                    scores_T(u, s, c, j, HPG * step + quarter + 1)
                                elif before:
                                    with_v(*before, use_ones=(quarter == 3))
                                if entries and QUARTER[entries[0]] == 4 * step + quarter:
                                    if entries[0] in (0, PER_UNIT):
                                        pe.wait_ge(loaded[1 - s][entries[0] // PER_UNIT], LOADS * (i + 1 + s))
                                    score_entry(u + 1, 1 - s, entries.pop(0))
                            before = (u, s, c, j, step)
                    with_v(*before, use_ones=False)
                    with_v(*before, use_ones=True)

                pe.sem_inc(pv_done, 2)
                pe.wait_ge(const_done, CONSTS)
                pe.wait_ge(loaded[0][0], LOADS)
                pe.wait_ge(loaded[0][1], LOADS)
                for m in range(S_PER_GROUP):
                    score_entry(0, 0, m)

                half(pe, second_pass)

            @block.scalar
            def _(act):
                act.sem_inc(p_ready, 2)
                act.sem_inc(o_read, 1)

                def evacuate(u, c):
                    act.wait_ge(pv_done, 2 + J_PER_GROUP * u + sum(STEPS[:c + 1]))
                    act.wait_ge(o_normed, 2 * u + c)
                    act.activation(o_raw[:, 0, :], O_BANK, ACT.Copy)
                    act.activation(o_raw[:, 1, :], SUM_BANK, ACT.Copy).then_inc(o_read, 1)

                def body(i, last):
                    before = None
                    for s in range(2):
                        u = 2 * i + s
                        for step, (c, j) in enumerate(KEY_STEPS):
                            q0 = max(0, P * j - CH * c)
                            act.wait_ge(pv_done, J_PER_GROUP * u + step + 1)
                            for g in range(HPG):
                                st = HPG * step + g
                                act.wait_ge(st_ready, ST_PER_GROUP * u + st + 1)
                                act.activation(probs[:, step % 2, g, q0:CH], ST_BANKS[st % 2][:, q0:CH], ACT.Exp,
                                               scale=SM_SCALE).then_inc(p_ready, 1)
                            if j == 0 and before:
                                evacuate(*before)
                            before = (u, c)
                    evacuate(*before)
                half(act, body)

            @block.vector
            def _(dve):
                dve.sem_inc(s_used, 2)
                dve.wait_ge(const_done, CONSTS)

                def maximum(u, s, m):
                    c, tile, g = ENTRIES[m]
                    base = S_PER_GROUP * u
                    dve.wait_ge(s_ready, base + m + 1)
                    dve.wait_ge(s_used, base + m + 1)
                    dve.sem_inc(passed, 1)
                    if tile is not None:
                        n = P * (CT * c + tile + 1)
                        col = g * CT + tile
                        dve.tensor_tensor_reduce(junk[:, m % 2, 0:n], S_BANKS[m % 2][:, 0:n], causal[:, SEQ - n:SEQ], 1.0, FLOOR,
                                                 ALU.add, ALU.max, rowmax[:, c, col:col + 1]).then_inc(s_used, 1)
                        if (tile, g) == (CT - 1, HPG - 1):
                            dve.wait_ge(s_used, 2 + base + m + 1)
                            dve.tensor_scalar(negmax[:, c, 0, :], rowmax[:, c, :], -1.0, None, ALU.mult).then_inc(rm_done, 1)
                            dve.wait_ge(rm_done, 2 * u + c + 1)
                            dve.scalar_tensor_tensor(out=negmax[:, c, 1, :], in0=rowmax[:, c, :], scalar=-1.0,
                                                     in1=f32(negmax[:, c, 0, :]), op0=ALU.mult, op1=ALU.subtract).then_inc(nm_ready, 1)
                        return
                    rows = [2 * PER_UNIT, HPG, CT, P]
                    dve.tensor_tensor(
                        qst[s][96:128, :, c * CH:(c + 1) * CH].rearrange("p g (t q) -> p g t q", q=P),
                        S_BANKS[m % 2][0:2 * PER_UNIT, 0:P][:, None, None, :].to_broadcast(rows),
                        pick[:, :].rearrange("p (g t) -> p g t", g=HPG)[:, :, :, None].to_broadcast(rows),
                        ALU.mult).then_inc(s_used, 1)

                def normalize(u, c):
                    dve.wait_ge(o_read, 1 + 2 * u + c + 1)
                    dve.wait_ge(o_stored[c], 16 * u)
                    dve.reciprocal(recip[:, :], o_raw[:, 1, :]).then_inc(rec_done, 1)
                    dve.wait_ge(rec_done, 2 * u + c + 1)
                    dve.tensor_tensor(o_out[:, c, :], o_raw[:, 0, :], recip[:, :], ALU.mult).then_inc(o_normed, 1)

                for m in range(S_PER_GROUP):
                    maximum(0, 0, m)

                def body(i, last):
                    for s in range(2):
                        u = 2 * i + s
                        if not (last and s == 1):
                            for m in range(BESIDE_C0):
                                maximum(u + 1, 1 - s, m)
                        normalize(u, 0)
                        if not (last and s == 1):
                            for m in range(BESIDE_C0, S_PER_GROUP):
                                maximum(u + 1, 1 - s, m)
                        normalize(u, 1)
                half(dve, body)


class Banks:

    def __init__(self, nc, ctx, name, psum, first, size, per_iter):
        assert per_iter % size == 0
        self.psum, self.first, self.size, self.turns = psum, first, size, per_iter // size
        self.filled = [ctx.semaphore(f"{name}_filled{k}") for k in range(size)]
        self.freed = [ctx.semaphore(f"{name}_freed{k}") for k in range(size)]

    def bank(self, m):
        return self.psum[:, self.first + m % self.size, :]

    def wait_free(self, pe, it, m):
        pe.wait_ge(self.freed[m % self.size], it * self.turns + m // self.size)

    def wait_full(self, eng, it, m):
        eng.wait_ge(self.filled[m % self.size], it * self.turns + m // self.size + 1)

    def fill(self, ins, m):
        return ins.then_inc(self.filled[m % self.size], 1)

    def free(self, ins, m):
        return ins.then_inc(self.freed[m % self.size], 1)


def partials(pe, bank, terms):
    for n, (lhsT, rhs) in enumerate(terms):
        mm = pe.matmul(bank, lhsT, rhs, start=(n == 0), stop=(n == len(terms) - 1))
    return mm


class LayerNorm:
    FROM = 2 * CT

    def __init__(self, nc, ctx, name):
        sem = lambda k: ctx.semaphore(f"{name}_{k}")
        self.stats = ctx.enter_context(nc.sbuf_tensor(f"{name}_stats", [P, CT, 6], F32))
        self.meanvar = ctx.enter_context(nc.sbuf_tensor(f"{name}_meanvar", [P, CT, 2], F32))
        self.vareps = ctx.enter_context(nc.sbuf_tensor(f"{name}_vareps", [P, CT], F32))
        self.rstd = ctx.enter_context(nc.sbuf_tensor(f"{name}_rstd", [P, CT], F32))
        self.power = ctx.enter_context(nc.sbuf_tensor(f"{name}_power", [P, CT], F32))
        self.summed, self.got_stats, self.got_mean = sem("summed"), sem("got_stats"), sem("got_mean")
        self.passed = sem("passed")
        self.ready, self.eps_added, self.got_rstd, self.normed = sem("ready"), sem("eps_added"), sem("got_rstd"), sem("normed")

    def setup(self, pool):
        pool.memset(self.power[:, :], -0.5).then_inc(self.ready, 1)
        pool.wait_ge(self.ready, 1)

    def pool_part(self, pool, n):
        pool.wait_ge(self.got_mean, n * CT + CT)
        pool.sem_inc(self.passed, 1)
        pool.tensor_scalar(self.vareps[:, :], self.meanvar[:, :, 1], LN_EPS, None, ALU.add).then_inc(self.eps_added, 1)
        pool.wait_ge(self.eps_added, n + 1)
        pool.tensor_tensor(self.rstd[:, :], self.vareps[:, :], self.power[:, :], ALU.pow).then_inc(self.got_rstd, 1)

    def vector_part(self, dve, n, src, dst):
        for t in range(CT):
            dve.wait_ge(self.summed, self.FROM + n * CT + t + 1)
            dve.bn_stats(self.stats[:, t, :], src(t)).then_inc(self.got_stats, 1)
        dve.wait_ge(self.got_stats, n * CT + CT)
        dve.sem_inc(self.passed, 1)
        for t in range(CT):
            dve.bn_aggr(self.meanvar[:, t, :], self.stats[:, t, :]).then_inc(self.got_mean, 1)
        dve.wait_ge(self.got_rstd, n + 1)
        for t in range(CT):
            dve.tensor_scalar(dst(t), src(t), self.meanvar[:, t, 0:1], self.rstd[:, t:t + 1],
                              ALU.subtract, ALU.mult).then_inc(self.normed, 1)


def rows(vec):
    return vec.rearrange("(o n) -> o n", o=1).to_broadcast([P, vec.shape[0]])


def phase_out0(nc, psum, x, wo, bo, o_dram, x1_dram):
    with Phase(nc) as ctx:
        sb = lambda n, s, d: ctx.enter_context(nc.sbuf_tensor(n, s, d))
        sem = lambda n: ctx.semaphore(n)
        stage = sb("p3_stage", [P, 2, KT * D], F32)
        w_hi = sb("p3_w_hi", [P, KT, D], F32R)
        w_lo = sb("p3_w_lo", [P, KT, D], F32R)
        o_in = sb("p3_o", [P, 2, GROUPS, CH], F32)
        o_hi = sb("p3_o_hi", [P, 2, GROUPS, CH], F32R)
        o_lo = sb("p3_o_lo", [P, 2, GROUPS, CH], F32R)
        xs = sb("p3_x", [P, 2, CT, D], F32)
        s_in = sb("p3_sum", [P, 2, CT, D], F32)
        x1 = sb("p3_x1", [P, 2, CT, D], F32)
        bias = sb("p3_bias", [P, D], F32)
        flat = lambda ap: ap.rearrange("p k n -> p (k n)")
        load_w, split_hi, split_lo, w_done, n_w = split_loader(
            nc, ctx, "p3_w", stage[:, :, :], [(wo.rearrange("(k p) n -> p k n", p=P), flat(w_hi[:, :, :]), flat(w_lo[:, :, :]))])
        ln = LayerNorm(nc, ctx, "p3_ln")
        banks = Banks(nc, ctx, "p3_bank", psum, 0, 8, 2 * CT)
        bias_loaded = sem("p3_bias_loaded")
        o_loaded = [sem(f"p3_o_loaded{c}") for c in range(2)]
        x_loaded = [sem(f"p3_x_loaded{c}") for c in range(2)]
        o_hi_done, o_lo_done = sem("p3_o_hi_done"), sem("p3_o_lo_done")
        x_biased = sem("p3_x_biased")
        stored = [sem(f"p3_stored{c}") for c in range(2)]
        x_v = x.rearrange("b (c t p) d -> b c p t d", c=2, p=P)

        with nc.Block() as block:
            @block.sync
            def _(sp):
                load_w(sp)
                sp.dma_start(bias[:, :], rows(bo)).then_inc(bias_loaded, 16)
                with sp.Fori(0, BATCH) as b:
                    for c in range(2):
                        sp.wait_ge(o_lo_done, 2 * b)
                        sp.dma_start(o_in[:, c, :, :], o_dram[bass.ds(4 * b, GROUPS), :, c * CH:(c + 1) * CH].rearrange("g p t -> p g t")).then_inc(o_loaded[c], 16)
                        sp.wait_ge(ln.summed, ln.FROM + 8 * b)
                        sp.dma_start(xs[:, c, :, :], x_v[b, c]).then_inc(x_loaded[c], 16)
                    for c in range(2):
                        sp.wait_ge(ln.normed, 8 * b + 4 * c + 4)
                        sp.dma_start(x1_dram[2 * b + c].rearrange("(t p) d -> p t d", p=P), x1[:, c, :, :]).then_inc(stored[c], 16)
                for c in range(2):
                    sp.wait_ge(stored[c], 16 * BATCH)

            @block.gpsimd
            def _(pool):
                ln.setup(pool)
                pool.wait_ge(bias_loaded, 16)
                with pool.Fori(0, BATCH) as b:
                    for c in range(2):
                        pool.wait_ge(o_hi_done, 2 * b + c + 1)
                        pool.tensor_tensor(o_lo[:, c, :, :], o_in[:, c, :, :], f32(o_hi[:, c, :, :]), ALU.subtract).then_inc(o_lo_done, 1)
                        pool.wait_ge(x_loaded[c], 16 * b + 16)
                        pool.tensor_tensor(xs[:, c, :, :], xs[:, c, :, :], bias[:, None, :].to_broadcast([P, CT, D]), ALU.add).then_inc(x_biased, 1)
                    for c in range(2):
                        ln.pool_part(pool, 2 * b + c)

            @block.scalar
            def _(act):
                split_hi(act)
                with act.Fori(0, BATCH) as b:
                    for c in range(2):
                        act.wait_ge(o_loaded[c], 16 * b + 16)
                        act.wait_ge(banks.filled[CT * c + CT - 1], b)
                        act.activation(o_hi[:, c, :, :], o_in[:, c, :, :], ACT.Copy).then_inc(o_hi_done, 1)

            @block.tensor
            def _(pe):
                pe.wait_ge(w_done, n_w)
                with pe.Fori(0, BATCH) as b:
                    for c in range(2):
                        pe.wait_ge(o_lo_done, 2 * b + c + 1)
                        for t in range(CT):
                            m = CT * c + t
                            tok = slice(t * P, (t + 1) * P)
                            pe.wait_ge(ln.summed, 8 * b + m + 1)
                            banks.fill(partials(pe, banks.bank(m), [
                                (o[:, c, k, tok], w[:, k, :]) for k in range(KT)
                                for o, w in ((o_hi, w_hi), (o_lo, w_hi), (o_hi, w_lo))]), m)

            @block.vector
            def _(dve):
                split_lo(dve)
                dve.sem_inc(ln.summed, ln.FROM)
                with dve.Fori(0, BATCH) as b:
                    for c in range(2):
                        dve.wait_ge(x_biased, 2 * b + c + 1)
                        dve.wait_ge(ln.normed, 8 * b)
                        for t in range(CT):
                            m = CT * c + t
                            banks.wait_full(dve, b, m)
                            dve.tensor_tensor(s_in[:, c, t, :], banks.bank(m), xs[:, c, t, :], ALU.add).then_inc(ln.summed, 1)
                        dve.wait_ge(stored[c], 16 * b)
                        ln.vector_part(dve, 2 * b + c, lambda t: s_in[:, c, t, :], lambda t: x1[:, c, t, :])


def phase_ffn0(nc, psum, ident, w1, b1, w2, b2, x1_dram, y_dram, y_max):
    NT = KT * HID
    with Phase(nc) as ctx:
        sb = lambda n, s, d: ctx.enter_context(nc.sbuf_tensor(n, s, d))
        sem = lambda n: ctx.semaphore(n)
        raw = sb("p4_raw", [P, NT], F32)
        below = sb("p4_below", [P, NT], F16)
        tern1 = sb("p4_tern1", [P, KT, HID], F32R)
        tern2 = sb("p4_tern2", [P, HT, D], F32R)
        amax = sb("p4_amax", [P, 2], F32)
        delta = sb("p4_delta", [P, 2, 3], F32)
        sums = sb("p4_sums", [P, 2, 2], F32)
        totals = sb("p4_totals", [P, 2], F32)
        totals_all = sb("p4_totals_all", [P, 2], F32)
        alpha = sb("p4_alpha", [P, 2], F32)
        b1c = sb("p4_b1", [P, HT], F32)
        b2r = sb("p4_b2", [P, D], F32)
        x1 = sb("p4_x1", [P, CT, D], F32)
        xT_hi = sb("p4_xT_hi", [P, 2, KT, CH], F32R)
        xT_lo = sb("p4_xT_lo", [P, 2, KT, CH], F32R)
        h = sb("p4_h", [P, 2, CH], F32)
        h_hi = sb("p4_h_hi", [P, 2, CH], F32R)
        h_lo = sb("p4_h_lo", [P, 2, CH], F32R)
        ys = sb("p4_y", [P, CT, D], F32)
        y_abs = sb("p4_y_abs", [P, CT + 2], F32)

        Y = Banks(nc, ctx, "p4_ybank", psum, 0, CT, 2 * CT)
        H = Banks(nc, ctx, "p4_hbank", psum, 4, 2, 2 * HT)
        T = Banks(nc, ctx, "p4_tbank", psum, 6, 2, 2 * KT)
        raw_loaded, bias_loaded, x_loaded = sem("p4_raw_loaded"), sem("p4_bias_loaded"), sem("p4_x_loaded")
        prep, reduced = sem("p4_prep"), sem("p4_reduced")
        xt_hi, xt_lo = sem("p4_xt_hi"), sem("p4_xt_lo")
        gelu_done, hh_done, hl_done = sem("p4_gelu"), sem("p4_h_hi_done"), sem("p4_h_lo_done")
        h_used = sem("p4_h_used")
        y_done, y_maxed, run_max = sem("p4_y_done"), sem("p4_y_maxed"), sem("p4_run_max")
        y_stored = sem("p4_y_stored")
        PREP_STEPS = 13

        with nc.Block() as block:
            @block.sync
            def _(sp):
                sp.dma_start(raw[:, :].rearrange("p (k n) -> p k n", k=KT), w1.rearrange("(k p) n -> p k n", p=P)).then_inc(raw_loaded, 16)
                sp.dma_start(b1c[:, :], b1).then_inc(bias_loaded, 16)
                sp.dma_start(b2r[:, :], rows(b2)).then_inc(bias_loaded, 16)
                sp.wait_ge(prep, PREP_STEPS)
                sp.dma_start(raw[:, :].rearrange("p (k n) -> p k n", k=HT), w2.rearrange("(k p) n -> p k n", p=P)).then_inc(raw_loaded, 16)
                with sp.Fori(0, BATCH) as b:
                    for c in range(2):
                        for k in range(2):
                            sp.wait_ge(T.filled[k], 4 * b + 2 * c)
                        sp.dma_start(x1[:, :, :], x1_dram[2 * b + c].rearrange("(t p) d -> p t d", p=P)).then_inc(x_loaded, 16)
                        if c == 1:
                            sp.wait_ge(y_maxed, 8 * b + 4)
                            sp.dma_start(y_dram[2 * b].rearrange("(t p) d -> p t d", p=P), ys[:, :, :]).then_inc(y_stored, 16)
                    sp.wait_ge(y_maxed, 8 * b + 8)
                    sp.dma_start(y_dram[2 * b + 1].rearrange("(t p) d -> p t d", p=P), ys[:, :, :]).then_inc(y_stored, 16)
                sp.wait_ge(y_stored, 16 * NCH)

            @block.gpsimd
            def _(pool):
                for n in range(2):
                    pool.wait_ge(prep, PREP_STEPS * n + 1)
                    pool.partition_all_reduce(delta[:, n, 0:1], amax[:, n:n + 1], P, bass.bass_isa.ReduceOp.max).then_inc(reduced, 1)
                    pool.wait_ge(prep, PREP_STEPS * n + PREP_STEPS - 3)
                    pool.partition_all_reduce(totals_all[:, :], totals[:, :], P, bass.bass_isa.ReduceOp.add).then_inc(reduced, 1)

            @block.scalar
            def _(act):
                act.preload_act_table(ACT.Gelu)
                act.wait_ge(prep, 2 * PREP_STEPS)
                act.wait_ge(bias_loaded, 32)
                with act.Fori(0, BATCH) as b:
                    def x_hi(c):
                        for k in range(KT):
                            T.wait_full(act, b, KT * c + k)
                            act.activation(xT_hi[:, c, k, :], T.bank(KT * c + k), ACT.Copy).then_inc(xt_hi, 1)
                    x_hi(0)
                    for c in range(2):
                        for t in range(HT):
                            m = HT * c + t
                            H.wait_full(act, b, m)
                            act.wait_ge(hl_done, 2 * HT * b + m - 1) if m else act.wait_ge(hl_done, 2 * HT * b)
                            H.free(act.activation(h[:, t % 2, :], H.bank(m), ACT.Gelu, bias=b1c[:, t:t + 1], scale=alpha[:, 0:1]), m)
                            if c == 0 and t == HT // 2:
                                x_hi(1)

            @block.tensor
            def _(pe):
                with pe.Fori(0, BATCH) as b:
                    def transposes(c):
                        pe.wait_ge(x_loaded, 32 * b + 16 * c + 16)
                        for k in range(KT):
                            m = KT * c + k
                            pe.wait_ge(xt_lo, 8 * b + m + 1)
                            for t in range(CT):
                                mm = pe.transpose(T.bank(m)[:, t * P:(t + 1) * P], x1[:, t, k * P:(k + 1) * P], ident[:, :])
                            T.fill(mm, m)

                    def to_y(c, t):
                        pe.wait_ge(hl_done, 2 * HT * b + HT * c + t + 1)
                        for a in range(CT):
                            m = CT * c + a
                            if t == 0:
                                Y.wait_free(pe, b, m)
                            tok = slice(a * P, (a + 1) * P)
                            for part, src in enumerate((h_hi, h_lo)):
                                mm = pe.matmul(Y.bank(m), src[:, t % 2, tok], tern2[:, t, :], start=(t == 0 and part == 0),
                                               stop=(t == HT - 1 and part == 1))
                            if t == HT - 1:
                                Y.fill(mm, m)
                        if t < HT - 1:
                            mm.then_inc(h_used, 1)

                    transposes(0)
                    pe.wait_ge(prep, 2 * PREP_STEPS)
                    for c in range(2):
                        pe.wait_ge(xt_lo, 2 + 8 * b + 4 * c + 4)
                        for t in range(HT + 1):
                            if t < HT:
                                m = HT * c + t
                                H.wait_free(pe, b, m)
                                H.fill(partials(pe, H.bank(m), [
                                    (tern1[:, k, t * P:(t + 1) * P], xp[:, c, k, :]) for k in range(KT) for xp in (xT_hi, xT_lo)]), m)
                            if t > 0:
                                to_y(c, t - 1)
                            if c == 0 and t == HT // 2:
                                transposes(1)

            @block.vector
            def _(dve):
                step = [0]

                def link(ins):
                    step[0] += 1
                    ins.then_inc(prep, 1)
                    dve.wait_ge(prep, step[0])

                for n, tern in enumerate((tern1, tern2)):
                    out = tern[:, :, :].rearrange("p k n -> p (k n)")
                    dve.wait_ge(raw_loaded, 16 * n + 16)
                    link(dve.tensor_reduce(amax[:, n:n + 1], raw[:, :], AX.X, ALU.max, apply_absolute_value=True))
                    dve.wait_ge(reduced, 2 * n + 1)
                    link(dve.tensor_scalar(delta[:, n, 1:2], delta[:, n, 0:1], TERN, None, ALU.mult))
                    link(dve.tensor_scalar(delta[:, n, 2:3], delta[:, n, 1:2], -1.0, None, ALU.mult))
                    link(dve.tensor_scalar(below[:, :], raw[:, :], delta[:, n, 2:3], None, ALU.is_lt))
                    link(dve.scalar_tensor_tensor(out=out, in0=raw[:, :], scalar=delta[:, n, 1:2], in1=below[:, :],
                                                  op0=ALU.is_gt, op1=ALU.subtract))
                    for q in range(2):
                        part = slice(q * NT // 2, (q + 1) * NT // 2)
                        link(dve.tensor_tensor_reduce(below[:, part], raw[:, part], f32(out[:, part]), 1.0, 0.0, ALU.mult,
                                                      ALU.add, sums[:, 0, q:q + 1]))
                        link(dve.tensor_tensor_reduce(below[:, part], f32(out[:, part]), f32(out[:, part]), 1.0, 0.0, ALU.mult,
                                                      ALU.add, sums[:, 1, q:q + 1]))
                    link(dve.tensor_tensor(totals[:, :], sums[:, :, 0], sums[:, :, 1], ALU.add))
                    dve.wait_ge(reduced, 2 * n + 2)
                    link(dve.tensor_scalar(totals_all[:, 1:2], totals_all[:, 1:2], 1.0, None, ALU.max))
                    link(dve.reciprocal(totals[:, 1:2], totals_all[:, 1:2]))
                    link(dve.tensor_tensor(alpha[:, n:n + 1], totals_all[:, 0:1], totals[:, 1:2], ALU.mult))
                    assert step[0] == PREP_STEPS * (n + 1), step[0]
                link(dve.memset(y_abs[:, :], 0.0))
                dve.sem_inc(xt_lo, 2)
                dve.wait_ge(bias_loaded, 32)
                with dve.Fori(0, BATCH) as b:
                    def x_lo(c):
                        for k in range(KT):
                            m = KT * c + k
                            dve.wait_ge(xt_hi, 8 * b + m + 1)
                            dve.tensor_tensor(xT_lo[:, c, k, :], T.bank(m), f32(xT_hi[:, c, k, :]), ALU.subtract).then_inc(xt_lo, 1)
                    x_lo(0)
                    for c in range(2):
                        for t in range(HT):
                            m = HT * c + t
                            dve.wait_ge(H.freed[m % 2], HT * b + m // 2 + 1)
                            if t == 1:
                                dve.wait_ge(Y.filled[CT - 1], 2 * b + c)
                            else:
                                dve.wait_ge(h_used, (HT - 1) * (2 * b + c) + max(0, t - 1))
                            dve.tensor_copy(h_hi[:, t % 2, :], h[:, t % 2, :]).then_inc(hh_done, 1)
                            dve.wait_ge(hh_done, 2 * HT * b + m + 1)
                            dve.tensor_tensor(h_lo[:, t % 2, :], h[:, t % 2, :], f32(h_hi[:, t % 2, :]), ALU.subtract).then_inc(hl_done, 1)
                            if c == 0 and t == HT // 2:
                                x_lo(1)
                        dve.wait_ge(y_stored, 32 * b + 16 * c)
                        for a in range(CT):
                            m = CT * c + a
                            Y.wait_full(dve, b, m)
                            Y.free(dve.scalar_tensor_tensor(out=ys[:, a, :], in0=Y.bank(m), scalar=alpha[:, 1:2], in1=b2r[:, :],
                                                            op0=ALU.mult, op1=ALU.add), m)
                        for a in range(CT):
                            m = CT * c + a
                            dve.wait_ge(Y.freed[a], 2 * b + c + 1)
                            dve.tensor_reduce(y_abs[:, a:a + 1], ys[:, a, :], AX.X, ALU.max, apply_absolute_value=True).then_inc(y_maxed, 1)
                        dve.wait_ge(y_maxed, 8 * b + 4 * c + 4)
                        dve.tensor_reduce(y_abs[:, CT + c:CT + c + 1], y_abs[:, :], AX.X, ALU.max).then_inc(run_max, 1)
                        dve.wait_ge(run_max, 2 * b + c + 1)
                dve.tensor_copy(y_max[:, :], y_abs[:, CT + 1:CT + 2]).then_inc(run_max, 1)


def phase_linear_attention(nc, psum, ident, y_max, y_dram, x1_dram, wq, wk, wv, wo, bq, bk, bv, bo, decay_row, decay_col, x3_dram):
    TT = SEQ // P
    EXT = P + HPG
    with Phase(nc) as ctx:
        sb = lambda n, s, d: ctx.enter_context(nc.sbuf_tensor(n, s, d))
        sem = lambda n: ctx.semaphore(n)
        w_hi = sb("p5_w_hi", [P, 4, KT, D], F32R)
        w_lo = sb("p5_w_lo", [P, 4, KT, D], F32R)
        ys = sb("p5_y", [P, 2, CT * D], F32)
        x1 = sb("p5_x1", [P, CT * D], F32)
        x2 = sb("p5_x2", [P, TT, D], F32)
        aT_hi = sb("p5_aT_hi", [P, 2, KT, CH], F32R)
        aT_lo = sb("p5_aT_lo", [P, 2, KT, CH], F32R)
        qT = sb("p5_qT", [P, GROUPS, SEQ], F32)
        ks = sb("p5_k", [P, TT, D], F32)
        vs = sb("p5_v", [P, TT, GROUPS, P + 2], F32)
        kv = sb("p5_kv", [P, GROUPS, EXT], F32)
        o_tok = ks
        den = sb("p5_den", [P, 2, HEADS], F32)
        rden = sb("p5_rden", [P, 2, HEADS], F32)
        same_head = sb("p5_same_head", [P, EXT], F32)
        quant = sb("p5_quant", [P, 3], F32)
        bq_c = sb("p5_bq", [P, GROUPS], F32)
        bias = sb("p5_bias", [P, 3, D], F32)
        dec_r = sb("p5_decay_row", [P, SEQ], F32)
        dec_c = sb("p5_decay_col", [P, TT], F32)

        flat = lambda ap: ap.rearrange("p k n -> p (k n)")
        load_w, split_hi, split_lo, w_done, n_w = split_loader(
            nc, ctx, "p5_w", ys[:, :, :], [(w.rearrange("(k p) n -> p k n", p=P), flat(w_hi[:, n, :, :]), flat(w_lo[:, n, :, :]))
                                           for n, w in enumerate((wq, wk, wv, wo))])
        ln_a = LayerNorm(nc, ctx, "p5_ln_a")
        ln_b = LayerNorm(nc, ctx, "p5_ln_b")
        A = Banks(nc, ctx, "p5_abank", psum, 0, 4, 4 + 2 * TT + 4 * KT)
        B = Banks(nc, ctx, "p5_bbank", psum, 4, 4, 2 * (GROUPS + 2 * CT) + TT)
        a_x = lambda c, k: KT * c + k
        a_kv = lambda g: 2 * KT + g
        a_o = lambda t, half: 2 * KT + GROUPS + 2 * t + half
        a_oT = lambda c, k: 2 * KT + GROUPS + 2 * TT + KT * c + k
        b_q = lambda c, g: 3 * CT * c + g
        b_k = lambda c, t: 3 * CT * c + CT + t
        b_v = lambda c, t: 3 * CT * c + 2 * CT + t
        b_out = lambda t: 6 * CT + t

        built, consts_loaded = sem("p5_built"), sem("p5_consts_loaded")
        y_loaded = [sem(f"p5_y_loaded{c}") for c in range(2)]
        x1_loaded = sem("p5_x1_loaded")
        max_all, quant_ready = sem("p5_max_all"), sem("p5_quant_ready")
        rounding = sem("p5_rounding")
        t_hi, t_lo = sem("p5_t_hi"), sem("p5_t_lo")
        q_relu, q_done = sem("p5_q_relu"), sem("p5_q_done")
        k_biased, k_done = sem("p5_k_biased"), sem("p5_k_done")
        v_done, kv_done = sem("p5_v_done"), sem("p5_kv_done")
        den_eps, den_inv, o_done = sem("p5_den_eps"), sem("p5_den_inv"), sem("p5_o_done")
        x2_biased = sem("p5_x2_biased")
        x3_stored = [sem(f"p5_x3_stored{c}") for c in range(2)]
        tok = lambda t: slice(t * P, (t + 1) * P)

        with nc.Block() as block:
            @block.sync
            def _(sp):
                load_w(sp)
                sp.dma_start(bq_c[:, :], bq).then_inc(consts_loaded, 16)
                for n, vec in enumerate((bk, bv, bo)):
                    sp.dma_start(bias[:, n, :], rows(vec)).then_inc(consts_loaded, 16)
                sp.dma_start(dec_r[:, :], rows(decay_row)).then_inc(consts_loaded, 16)
                sp.dma_start(dec_c[:, :], decay_col).then_inc(consts_loaded, 16)
                sp.wait_ge(w_done, n_w)
                with sp.Fori(0, BATCH) as b:
                    for c in range(2):
                        sp.wait_ge(x3_stored[c], 16 * b)
                        sp.dma_start(ys[:, c, :].rearrange("p (t d) -> p t d", t=CT),
                                     y_dram[2 * b + c].rearrange("(t p) d -> p t d", p=P)).then_inc(y_loaded[c], 16)
                    for c in range(2):
                        sp.wait_ge(ln_a.summed, ln_a.FROM + 8 * b + 4 * c)
                        sp.dma_start(x1[:, :].rearrange("p (t d) -> p t d", t=CT),
                                     x1_dram[2 * b + c].rearrange("(t p) d -> p t d", p=P)).then_inc(x1_loaded, 16)
                    for c in range(2):
                        sp.wait_ge(ln_b.normed, 8 * b + 4 * c + 4)
                        sp.dma_start(x3_dram[2 * b + c].rearrange("(t p) d -> p t d", p=P),
                                     ys[:, c, :].rearrange("p (t d) -> p t d", t=CT)).then_inc(x3_stored[c], 16)
                for c in range(2):
                    sp.wait_ge(x3_stored[c], 16 * BATCH)

            @block.gpsimd
            def _(pool):
                def build(n, ins):
                    ins.then_inc(built, 1)
                    pool.wait_ge(built, n)
                build(1, pool.memset(same_head[:, :], 0.0))
                for g in range(HPG):
                    build(2 + 2 * g, pool.memset(same_head[g * HD:(g + 1) * HD, g * HD:(g + 1) * HD], 1.0))
                    build(3 + 2 * g, pool.memset(same_head[g * HD:(g + 1) * HD, P + g:P + g + 1], 1.0))
                build(10, pool.memset(vs[:, :, :, P:P + 2], 1.0))
                ln_a.setup(pool)
                ln_b.setup(pool)
                pool.partition_all_reduce(quant[:, 0:1], y_max[:, :], P, bass.bass_isa.ReduceOp.max).then_inc(max_all, 1)
                pool.wait_ge(consts_loaded, 16 * 6)
                with pool.Fori(0, BATCH) as b:
                    for c in range(2):
                        ln_a.pool_part(pool, 2 * b + c)
                    for c in range(2):
                        for g in range(GROUPS):
                            n = GROUPS * c + g
                            q = qT[:, g, c * CH:(c + 1) * CH]
                            pool.wait_ge(q_relu, 8 * b + n + 1)
                            pool.tensor_tensor(q, q, dec_r[:, c * CH:(c + 1) * CH], ALU.mult).then_inc(q_done, 1)
                        for t in range(CT * c, CT * c + CT):
                            pool.wait_ge(k_biased, 8 * b + t + 1)
                            pool.sem_inc(ln_a.passed, 1)
                            pool.tensor_scalar(ks[:, t, :], ks[:, t, :], 0.0, dec_c[:, t:t + 1], ALU.max, ALU.mult).then_inc(k_done, 1)
                    for c in range(2):
                        pool.wait_ge(t_lo, 16 * b + 4 * c + 4)
                        part = x2[:, CT * c:CT * c + CT, :]
                        pool.tensor_tensor(part, part, bias[:, 2:3, :].to_broadcast([P, CT, D]), ALU.add).then_inc(x2_biased, 1)
                    for c in range(2):
                        ln_b.pool_part(pool, 2 * b + c)

            @block.scalar
            def _(act):
                split_hi(act)
                act.wait_ge(consts_loaded, 16 * 6)
                with act.Fori(0, BATCH) as b:
                    def part_hi(c, entry):
                        for k in range(KT):
                            A.wait_full(act, b, entry(c, k))
                            act.activation(aT_hi[:, c, k, :], A.bank(entry(c, k)), ACT.Copy).then_inc(t_hi, 1)
                    for c in range(2):
                        part_hi(c, a_x)
                        for g in range(GROUPS):
                            m = b_q(c, g)
                            B.wait_full(act, b, m)
                            act.activation(qT[:, g, c * CH:(c + 1) * CH], B.bank(m), ACT.Relu, bias=bq_c[:, g:g + 1]).then_inc(q_relu, 1)
                    for c in range(2):
                        part_hi(c, a_oT)

            @block.tensor
            def _(pe):
                pe.wait_ge(w_done, n_w)
                with pe.Fori(0, BATCH) as b:
                    def free_b(m):
                        prev = m - 4
                        if prev < 0:
                            pe.wait_ge(ln_b.summed, 8 * b + 4 + m + 1)
                        elif prev < b_out(0):
                            c, kind, n = prev // (3 * CT), prev % (3 * CT) // CT, prev % CT
                            pe.wait_ge((q_relu, k_biased, v_done)[kind], 8 * b + CT * c + n + 1)
                        else:
                            pe.wait_ge(ln_b.summed, ln_b.FROM + 8 * b + prev - b_out(0) + 1)

                    def transposes(c, entry, src):
                        for k in range(KT):
                            m = entry(c, k)
                            free_a(m)
                            for t in range(CT):
                                mm = pe.transpose(A.bank(m)[:, tok(t)], src(t)[:, tok(k)], ident[:, :])
                            A.fill(mm, m)

                    def free_a(m):
                        prev = m - 4
                        if prev < 0:
                            pe.wait_ge(t_lo, 16 * b)
                        elif prev < a_kv(0):
                            pe.wait_ge(t_lo, 16 * b + prev + 1)
                        elif prev < a_o(0, 0):
                            pe.wait_ge(kv_done, 4 * b + prev - a_kv(0) + 1)
                        elif prev < a_oT(0, 0):
                            pe.wait_ge(o_done, 16 * b + prev - a_o(0, 0) + 1)
                        else:
                            pe.wait_ge(t_lo, 16 * b + 8 + prev - a_oT(0, 0) + 1)

                    def product(c, n, a_cols, w_cols, a_is_lhs):
                        terms = []
                        for k in range(KT):
                            for a, w in ((aT_hi, w_hi), (aT_lo, w_hi), (aT_hi, w_lo)):
                                pair = (a[:, c, k, a_cols], w[:, n, k, w_cols])
                                terms.append(pair if a_is_lhs else pair[::-1])
                        return terms

                    everything = slice(0, D)
                    for c in range(2):
                        pe.wait_ge(ln_a.normed, 8 * b + 4 * c + 4)
                        transposes(c, a_x, lambda t: x2[:, CT * c + t, :])
                        pe.wait_ge(t_lo, 16 * b + 4 * c + 4)
                        for g in range(GROUPS):
                            free_b(b_q(c, g))
                            B.fill(partials(pe, B.bank(b_q(c, g)), product(c, 0, everything, tok(g), False)), b_q(c, g))
                        for n, entry in ((1, b_k), (2, b_v)):
                            for t in range(CT):
                                free_b(entry(c, t))
                                B.fill(partials(pe, B.bank(entry(c, t)), product(c, n, tok(t), everything, True)), entry(c, t))
                    pe.wait_ge(k_done, 8 * b + 8)
                    pe.wait_ge(v_done, 8 * b + 8)
                    for g in range(GROUPS):
                        m = a_kv(g)
                        free_a(m)
                        A.fill(partials(pe, A.bank(m)[:, 0:P + 2], [(ks[:, t, tok(g)], vs[:, t, g, :]) for t in range(TT)]), m)
                    pe.wait_ge(q_done, 8 * b + 8)
                    for t in range(TT):
                        for half in range(2):
                            m = a_o(t, half)
                            free_a(m)
                            if t == 0:
                                pe.wait_ge(kv_done, 4 * b + 2 * half + 2)
                            for g in (2 * half, 2 * half + 1):
                                mm = pe.matmul(A.bank(m)[:, (g % 2) * EXT:(g % 2 + 1) * EXT], qT[:, g, tok(t)], kv[:, g, :],
                                               start=True, stop=True)
                            A.fill(mm, m)
                    for c in range(2):
                        pe.wait_ge(o_done, 16 * b + 8 * c + 8)
                        transposes(c, a_oT, lambda t: o_tok[:, CT * c + t, :])
                    for c in range(2):
                        pe.wait_ge(t_lo, 16 * b + 8 + 4 * c + 4)
                        for t in range(CT):
                            m = b_out(CT * c + t)
                            free_b(m)
                            B.fill(partials(pe, B.bank(m), product(c, 3, tok(t), everything, True)), m)

            @block.vector
            def _(dve):
                split_lo(dve)
                dve.sem_inc(ln_a.summed, ln_a.FROM)
                dve.sem_inc(ln_b.summed, ln_b.FROM)
                dve.wait_ge(max_all, 1)
                dve.tensor_scalar(quant[:, 1:2], quant[:, 0:1], 1.0 / QMAX, FP4_EPS, ALU.mult, ALU.add).then_inc(quant_ready, 1)
                dve.wait_ge(quant_ready, 1)
                dve.reciprocal(quant[:, 2:3], quant[:, 1:2]).then_inc(quant_ready, 1)
                dve.wait_ge(quant_ready, 2)
                dve.wait_ge(built, 10)
                dve.wait_ge(consts_loaded, 16 * 6)
                with dve.Fori(0, BATCH) as b:
                    def quantized_norm(c):
                        y = ys[:, c, :]
                        dve.wait_ge(y_loaded[c], 16 * b + 16)
                        dve.tensor_scalar(y, y, quant[:, 2:3], ROUND, ALU.mult, ALU.add).then_inc(rounding, 1)
                        dve.wait_ge(rounding, 6 * b + 3 * c + 1)
                        dve.tensor_scalar(y, y, -ROUND, QMAX, ALU.add, ALU.min).then_inc(rounding, 1)
                        dve.wait_ge(rounding, 6 * b + 3 * c + 2)
                        dve.tensor_scalar(y, y, -QMAX, quant[:, 1:2], ALU.max, ALU.mult).then_inc(rounding, 1)
                        dve.wait_ge(rounding, 6 * b + 3 * c + 3)
                        dve.wait_ge(x1_loaded, 32 * b + 16 * c + 16)
                        for t in range(CT):
                            cols = slice(t * D, (t + 1) * D)
                            dve.tensor_tensor(x2[:, CT * c + t, :], y[:, cols], x1[:, cols], ALU.add).then_inc(ln_a.summed, 1)
                        ln_a.vector_part(dve, 2 * b + c, lambda t: x2[:, CT * c + t, :], lambda t: x2[:, CT * c + t, :])

                    def part_lo(c, entry, first):
                        for k in range(KT):
                            dve.wait_ge(t_hi, 16 * b + first + KT * c + k + 1)
                            dve.tensor_tensor(aT_lo[:, c, k, :], A.bank(entry(c, k)), f32(aT_hi[:, c, k, :]), ALU.subtract).then_inc(t_lo, 1)

                    def keys_values(c):
                        for t in range(CT):
                            B.wait_full(dve, b, b_k(c, t))
                            dve.tensor_tensor(ks[:, CT * c + t, :], B.bank(b_k(c, t)), bias[:, 0, :], ALU.add).then_inc(k_biased, 1)
                        for t in range(CT):
                            B.wait_full(dve, b, b_v(c, t))
                            heads = lambda ap: ap.rearrange("p (g e) -> p g e", g=GROUPS)
                            dve.tensor_tensor(vs[:, CT * c + t, :, 0:P], heads(B.bank(b_v(c, t))), heads(bias[:, 1, :]), ALU.add).then_inc(v_done, 1)

                    quantized_norm(0)
                    part_lo(0, a_x, 0)
                    quantized_norm(1)
                    keys_values(0)
                    part_lo(1, a_x, 0)
                    keys_values(1)
                    for g in range(GROUPS):
                        bank = A.bank(a_kv(g))
                        A.wait_full(dve, b, a_kv(g))
                        dve.tensor_tensor(kv[:, g, 0:P], bank[:, 0:P], same_head[:, 0:P], ALU.mult)
                        dve.tensor_scalar(kv[:, g, P:EXT], same_head[:, P:EXT], bank[:, P:P + 1], None, ALU.mult).then_inc(kv_done, 1)
                    for t in range(TT):
                        halves = [A.bank(a_o(t, half))[:, 0:2 * EXT].rearrange("p (g e) -> p g e", g=2) for half in range(2)]
                        slot = lambda ap: ap[:, t % 2, :]
                        for half in range(2):
                            A.wait_full(dve, b, a_o(t, half))
                            dve.tensor_scalar(slot(den)[:, half * 2 * HPG:(half + 1) * 2 * HPG].rearrange("p (g h) -> p g h", g=2),
                                              halves[half][:, :, P:EXT], LIN_EPS, None, ALU.add).then_inc(den_eps, 1)
                        dve.wait_ge(den_eps, 16 * b + 2 * t + 2)
                        dve.reciprocal(slot(rden), slot(den)).then_inc(den_inv, 1)
                        dve.wait_ge(den_inv, 8 * b + t + 1)
                        for half in range(2):
                            for g in range(2):
                                at = (2 * half + g) * P
                                heads = lambda ap: ap.rearrange("p (h e) -> p h e", h=HPG)
                                inv = slot(rden)[:, (2 * half + g) * HPG:(2 * half + g + 1) * HPG]
                                ins = dve.tensor_tensor(heads(o_tok[:, t, at:at + P]), heads(halves[half][:, g, 0:P]),
                                                        inv[:, :, None].to_broadcast([P, HPG, HD]), ALU.mult)
                            ins.then_inc(o_done, 1)
                    for c in range(2):
                        part_lo(c, a_oT, 8)
                    for c in range(2):
                        dve.wait_ge(x2_biased, 2 * b + c + 1)
                        for t in range(CT):
                            m = b_out(CT * c + t)
                            B.wait_full(dve, b, m)
                            dve.tensor_tensor(x2[:, CT * c + t, :], B.bank(m), x2[:, CT * c + t, :], ALU.add).then_inc(ln_b.summed, 1)
                        ln_b.vector_part(dve, 2 * b + c, lambda t: x2[:, CT * c + t, :], lambda t: ys[:, c, t * D:(t + 1) * D])


def phase_ffn1(nc, psum, w0, b0, w1, b1, x3_dram, out):
    with Phase(nc) as ctx:
        sb = lambda n, s, d: ctx.enter_context(nc.sbuf_tensor(n, s, d))
        sem = lambda n: ctx.semaphore(n)
        w0_hi = sb("p6_w0_hi", [P, KT, HID], F32R)
        w0_lo = sb("p6_w0_lo", [P, KT, HID], F32R)
        w1_hi = sb("p6_w1_hi", [P, HT, D], F32R)
        w1_lo = sb("p6_w1_lo", [P, HT, D], F32R)
        x3 = sb("p6_x3", [P, 2, CT * D], F32)
        x16 = sb("p6_x16", [P, CT, D], F16)
        xT = sb("p6_xT", [P, 2, KT, CH], F32R)
        h16 = sb("p6_h16", [P, 2, CH], F16)
        h = sb("p6_h", [P, 2, CH], F32R)
        e16 = sb("p6_e16", [P, CT, D], F16)
        res = sb("p6_out", [P, CT, D], F32)
        ident16 = sb("p6_ident16", [P, P], F16)
        b0c = sb("p6_b0", [P, HT], F32)
        b1r = sb("p6_b1", [P, D], F32)
        jobs = [(w0[k * P:(k + 1) * P, :], w0_hi[:, k, :], w0_lo[:, k, :]) for k in range(KT)]
        w1_v = w1.rearrange("(t p) n -> p t n", p=P)
        for q in range(4):
            part = slice(4 * q, 4 * q + 4)
            jobs.append((w1_v[:, part, :], w1_hi[:, part, :].rearrange("p t n -> p (t n)"), w1_lo[:, part, :].rearrange("p t n -> p (t n)")))
        load_w, split_hi, split_lo, w_done, n_w = split_loader(nc, ctx, "p6_w", x3[:, :, :], jobs)
        ln = LayerNorm(nc, ctx, "p6_ln")
        Y = Banks(nc, ctx, "p6_ybank", psum, 0, CT, 2 * CT)
        H = Banks(nc, ctx, "p6_hbank", psum, 4, 2, 2 * HT)
        T = Banks(nc, ctx, "p6_tbank", psum, 6, 2, 2 * KT)
        built, bias_loaded = sem("p6_built"), sem("p6_bias_loaded")
        x_loaded = [sem(f"p6_x_loaded{c}") for c in range(2)]
        x_cast, h_done, h_used = sem("p6_x_cast"), sem("p6_h_done"), sem("p6_h_used")
        stored = sem("p6_stored")

        with nc.Block() as block:
            @block.sync
            def _(sp):
                load_w(sp)
                sp.dma_start(b0c[:, :], b0).then_inc(bias_loaded, 16)
                sp.dma_start(b1r[:, :], rows(b1)).then_inc(bias_loaded, 16)
                sp.wait_ge(w_done, n_w)
                tiles = lambda ap: ap.rearrange("(t p) d -> p t d", p=P)
                with sp.Fori(0, BATCH) as b:
                    for c in range(2):
                        sp.wait_ge(ln.summed, 8 * b + 4 * c + 4)
                        sp.dma_start(x3[:, c, :].rearrange("p (t d) -> p t d", t=CT), tiles(x3_dram[2 * b + c])).then_inc(x_loaded[c], 16)
                    for c in range(2):
                        sp.wait_ge(ln.normed, 8 * b + 4 * c + 4)
                        sp.dma_start(tiles(out[2 * b + c]), res[:, :, :]).then_inc(stored, 16)
                sp.wait_ge(stored, 16 * NCH)

            @block.gpsimd
            def _(pool):
                pool.memset(ident16[:, :], 0.0).then_inc(built, 1)
                pool.wait_ge(built, 1)
                pool.affine_select(out=ident16[:, :], in_=ident16[:, :], compare_op=ALU.not_equal, fill=1.0, base=0,
                                   pattern=[[-1, P]], channel_multiplier=1).then_inc(built, 1)
                pool.wait_ge(built, 2)
                ln.setup(pool)
                with pool.Fori(0, BATCH) as b:
                    for c in range(2):
                        ln.pool_part(pool, 2 * b + c)

            @block.scalar
            def _(act):
                split_hi(act)
                act.preload_act_table(ACT.Gelu)
                act.wait_ge(bias_loaded, 32)
                with act.Fori(0, BATCH) as b:
                    def x_T(c):
                        for k in range(KT):
                            m = KT * c + k
                            T.wait_full(act, b, m)
                            T.free(act.activation(xT[:, c, k, :], T.bank(m).bitcast(F16)[:, 0:CH], ACT.Copy), m)
                    x_T(0)
                    for c in range(2):
                        for t in range(HT):
                            m = HT * c + t
                            H.wait_full(act, b, m)
                            act.wait_ge(h_done, 2 * HT * b + max(0, m - 1))
                            H.free(act.activation(h16[:, t % 2, :], H.bank(m), ACT.Gelu, bias=b0c[:, t:t + 1]), m)
                            if c == 0 and t == HT // 2:
                                x_T(1)

            @block.tensor
            def _(pe):
                pe.wait_ge(built, 2)
                with pe.Fori(0, BATCH) as b:
                    def transposes(c):
                        pe.wait_ge(x_cast, 2 * b + c + 1)
                        for k in range(KT):
                            m = KT * c + k
                            T.wait_free(pe, b, m)
                            for t in range(CT):
                                mm = pe.transpose(T.bank(m).bitcast(F16)[:, t * P:(t + 1) * P], x16[:, t, k * P:(k + 1) * P], ident16[:, :])
                            T.fill(mm, m)

                    def to_y(c, t):
                        pe.wait_ge(h_done, 2 * HT * b + HT * c + t + 1)
                        for a in range(CT):
                            m = CT * c + a
                            if t == 0:
                                Y.wait_free(pe, b, m)
                            for part, w in enumerate((w1_hi, w1_lo)):
                                mm = pe.matmul(Y.bank(m), h[:, t % 2, a * P:(a + 1) * P], w[:, t, :], start=(t == 0 and part == 0),
                                               stop=(t == HT - 1 and part == 1))
                            if t == HT - 1:
                                Y.fill(mm, m)
                        if t < HT - 1:
                            mm.then_inc(h_used, 1)

                    transposes(0)
                    pe.wait_ge(w_done, n_w)
                    for c in range(2):
                        for k in range(2):
                            pe.wait_ge(T.freed[k], 4 * b + 2 * c + 2)
                        for t in range(HT + 1):
                            if t < HT:
                                m = HT * c + t
                                H.wait_free(pe, b, m)
                                H.fill(partials(pe, H.bank(m), [
                                    (w[:, k, t * P:(t + 1) * P], xT[:, c, k, :]) for k in range(KT) for w in (w0_hi, w0_lo)]), m)
                            if t > 0:
                                to_y(c, t - 1)
                            if c == 0 and t == HT // 2:
                                transposes(1)

            @block.vector
            def _(dve):
                split_lo(dve)
                dve.sem_inc(ln.summed, ln.FROM)
                dve.wait_ge(bias_loaded, 32)
                with dve.Fori(0, BATCH) as b:
                    def cast(c):
                        dve.wait_ge(x_loaded[c], 16 * b + 16)
                        for k in range(2):
                            dve.wait_ge(T.filled[k], 4 * b + 2 * c)
                        dve.tensor_copy(x16[:, :, :].rearrange("p t d -> p (t d)"), x3[:, c, :]).then_inc(x_cast, 1)

                    cast(0)
                    for c in range(2):
                        for t in range(HT):
                            m = HT * c + t
                            dve.wait_ge(H.freed[m % 2], HT * b + m // 2 + 1)
                            if t == 1:
                                dve.wait_ge(Y.filled[CT - 1], 2 * b + c)
                            else:
                                dve.wait_ge(h_used, (HT - 1) * (2 * b + c) + max(0, t - 1))
                            dve.tensor_copy(h[:, t % 2, :], h16[:, t % 2, :]).then_inc(h_done, 1)
                            if c == 0 and t == HT // 2 - 1:
                                cast(1)
                        for a in range(CT):
                            m = CT * c + a
                            Y.wait_full(dve, b, m)
                            Y.free(dve.tensor_tensor(e16[:, a, :], Y.bank(m), b1r[:, :], ALU.add), m)
                        dve.wait_ge(stored, 32 * b + 16 * c)
                        for a in range(CT):
                            dve.wait_ge(Y.freed[a], 2 * b + c + 1)
                            dve.tensor_tensor(res[:, a, :], x3[:, c, a * D:(a + 1) * D], e16[:, a, :], ALU.add).then_inc(ln.summed, 1)
                        ln.vector_part(dve, 2 * b + c, lambda t: res[:, t, :], lambda t: res[:, t, :])


def build_program(nc, x, l0_wq, l0_wk, l0_wv, l0_wo, l0_bo, f0_w1, f0_b1, f0_w2, f0_b2,
                  l1_wq, l1_bq, l1_wk, l1_bk, l1_wv, l1_bv, l1_wo, l1_bo, f1_w0, f1_b0, f1_w1, f1_b1,
                  decay_row, decay_col, out):
    groups = BATCH * GROUPS
    q_dram = nc.dram_tensor("q_parts", [groups, 2, P, SEQ], F32)
    k_dram = nc.dram_tensor("k_parts", [groups, 2, P, SEQ], F32)
    v_dram = nc.dram_tensor("v_rows", [groups, SEQ, P], F32)
    o_dram = nc.dram_tensor("attention_out", [groups, P, SEQ], F32)
    x1_dram = nc.dram_tensor("x1", [NCH, CH, D], F32)
    y_dram = nc.dram_tensor("ffn0_out", [NCH, CH, D], F32)
    x3_dram = nc.dram_tensor("x3", [NCH, CH, D], F32)
    with Phase(nc) as ctx:
        psum = ctx.enter_context(nc.psum_tensor("psum", [P, 8, CH], F32))
        y_max = ctx.enter_context(nc.sbuf_tensor("y_max", [P, 1], F32))
        ident = build_constants(nc, ctx)
        phase_qkv0(nc, psum, ident, x, l0_wq, l0_wk, l0_wv, q_dram, k_dram, v_dram)
        phase_attention(nc, psum, ident, q_dram, k_dram, v_dram, o_dram)
        phase_out0(nc, psum, x, l0_wo, l0_bo, o_dram, x1_dram)
        phase_ffn0(nc, psum, ident, f0_w1, f0_b1, f0_w2, f0_b2, x1_dram, y_dram, y_max)
        phase_linear_attention(nc, psum, ident, y_max, y_dram, x1_dram, l1_wq, l1_wk, l1_wv, l1_wo,
                               l1_bq, l1_bk, l1_bv, l1_bo, decay_row, decay_col, x3_dram)
        phase_ffn1(nc, psum, f1_w0, f1_b0, f1_w1, f1_b1, x3_dram, out.rearrange("b (c t) d -> (b c) t d", c=2))


def kernel(**inputs):
    import concourse.bacc as bacc
    from concourse.bass_utils import run_bass_kernel_spmd

    i = {k: np.ascontiguousarray(v) for k, v in inputs.items()}
    by_partition = lambda v: np.ascontiguousarray(v.reshape(-1, P).T)
    transposed = lambda w: np.ascontiguousarray(w.T)
    decay = np.exp(-np.arange(SEQ, dtype=np.float32) / np.float32(SEQ)).astype(np.float32)
    arrays = {
        "x": i["L0_attn_x"], "l0_wq": i["L0_attn_wq"], "l0_wk": i["L0_attn_wk"], "l0_wv": i["L0_attn_wv"],
        "l0_wo": i["L0_attn_wo"], "l0_bo": i["L0_attn_bo"],
        "f0_w1": transposed(i["L0_ffn_W1"]), "f0_b1": by_partition(i["L0_ffn_b1"]),
        "f0_w2": transposed(i["L0_ffn_W2"]), "f0_b2": i["L0_ffn_b2"],
        "l1_wq": transposed(i["L1_attn_Wq"]), "l1_bq": by_partition(i["L1_attn_bq"]),
        "l1_wk": transposed(i["L1_attn_Wk"]), "l1_bk": i["L1_attn_bk"],
        "l1_wv": transposed(i["L1_attn_Wv"]), "l1_bv": i["L1_attn_bv"],
        "l1_wo": transposed(i["L1_attn_Wo"]), "l1_bo": i["L1_attn_bo"],
        "f1_w0": transposed(i["L1_ffn_W0"]), "f1_b0": by_partition(i["L1_ffn_bias0"]),
        "f1_w1": transposed(i["L1_ffn_W1"]), "f1_b1": i["L1_ffn_bias1"],
        "decay_row": decay, "decay_col": by_partition(decay),
    }
    nc = bacc.Bacc("TRN2", target_bir_lowering=False, num_devices=1)
    args = [nc.dram_tensor(f"in_{n}", a.shape, mybir.dt.from_np(a.dtype), kind="ExternalInput").ap() for n, a in arrays.items()]
    out = nc.dram_tensor("out", (BATCH, SEQ, D), F32, kind="ExternalOutput").ap()
    build_program(nc, *args, out)
    result = run_bass_kernel_spmd(nc, [{f"in_{n}": a for n, a in arrays.items()}], core_ids=[0])
    return result.results[0]["out"]
```

```python
from contextlib import ExitStack

import numpy as np

import concourse.bass as bass
from concourse import mybir

F32 = mybir.dt.float32
F32R = mybir.dt.float32r
F16 = mybir.dt.float16
ALU = mybir.AluOpType
ACT = mybir.ActivationFunctionType
AX = mybir.AxisListType

P = 128
BATCH, SEQ, D, HID = 4, 1024, 512, 2048
HEADS = 16
HD = D // HEADS
KT = D // P
HT = HID // P
CH = 512
NCH = BATCH * SEQ // CH
CT = CH // P
GROUPS = D // P
HPG = P // HD
SM_SCALE = 1.0 / float(np.sqrt(np.float32(HD)))
LN_EPS = 1e-5
FP4_EPS = 1e-8
QMAX = 7.0
LIN_EPS = 1e-6
TERN = 0.05
ROUND = 12582912.0
FLOOR = -3.0e38


class Phase(ExitStack):

    def __init__(self, nc):
        super().__init__()
        self.nc, self.semaphores = nc, []

    def semaphore(self, name, start=0):
        handle = self.nc.alloc_semaphore(name=name)
        self.semaphores.append(handle)
        if start:
            self.nc.gpsimd.sem_inc(handle, start)
        return handle

    def __exit__(self, *exc):
        self.nc.clear_and_free_semaphores(self.semaphores)
        self.nc.all_engine_barrier()
        return super().__exit__(*exc)


def f32(ap):
    return ap.bitcast(F32)


def split_loader(nc, ctx, name, stage, jobs):
    slots = stage.shape[1]
    loaded = [ctx.semaphore(f"{name}_loaded{k}") for k in range(slots)]
    hi_done = ctx.semaphore(f"{name}_hi")
    lo_done = ctx.semaphore(f"{name}_lo")

    def load(sp):
        for n, (src, _, _) in enumerate(jobs):
            if n >= slots:
                sp.wait_ge(lo_done, n - slots + 1)
            sp.dma_start(stage[:, n % slots, :], src).then_inc(loaded[n % slots], 16)

    def split_hi(act):
        for n, (_, hi, _) in enumerate(jobs):
            act.wait_ge(loaded[n % slots], 16 * (n // slots + 1))
            act.activation(hi, stage[:, n % slots, :], ACT.Copy).then_inc(hi_done, 1)

    def split_lo(dve, first=0, last=len(jobs)):
        for n, (_, hi, lo) in list(enumerate(jobs))[first:last]:
            dve.wait_ge(hi_done, n + 1)
            dve.tensor_tensor(lo, stage[:, n % slots, :], f32(hi), ALU.subtract).then_inc(lo_done, 1)

    return load, split_hi, split_lo, lo_done, len(jobs)


def halves(w, hi, lo):
    flat = lambda ap: ap.rearrange("p k n -> p (k n)")
    view = w.rearrange("(k p) n -> p k n", p=P)
    return [(view[:, k:k + KT // 2, :], flat(hi[:, k:k + KT // 2, :]), flat(lo[:, k:k + KT // 2, :])) for k in (0, KT // 2)]


def build_constants(nc, ctx):
    ident = ctx.enter_context(nc.sbuf_tensor("ident", [P, P], F32))
    zeroed = ctx.semaphore("ident_zeroed")
    with nc.Block() as block:
        @block.gpsimd
        def _(pool):
            pool.memset(ident[:, :], 0.0).then_inc(zeroed, 1)
            pool.wait_ge(zeroed, 1)
            pool.affine_select(out=ident[:, :], in_=ident[:, :], compare_op=ALU.not_equal, fill=1.0,
                               base=0, pattern=[[-1, P]], channel_multiplier=1).then_inc(zeroed, 1)
            pool.wait_ge(zeroed, 2)
    return ident


def phase_qkv0(nc, psum, ident, x, wq, wk, wv, q_dram, k_dram, v_dram, ffn_w, w_max):
    OUTS = 2 * GROUPS + CT
    with Phase(nc) as ctx:
        sb = lambda n, s, d: ctx.enter_context(nc.sbuf_tensor(n, s, d))
        sem = ctx.semaphore
        stage = sb("p1_stage", [P, 4, KT * D // 2], F32)
        w_hi = sb("p1_w_hi", [P, 3, KT, D], F32R)
        w_lo = sb("p1_w_lo", [P, 3, KT, D], F32R)
        xs = sb("p1_x", [P, CT, D], F32)
        xT_hi = sb("p1_xT_hi", [P, 2, KT, CH], F32R)
        xT_lo = sb("p1_xT_lo", [P, 2, KT, CH], F32R)
        qk_out = sb("p1_qk_out", [P, 4, 2, CH], F32R)
        v_out = sb("p1_v_out", [P, CT, D], F32)
        raw = sb("p1_raw", [P, 2, KT * D], F32)
        piece_max = sb("p1_piece_max", [P, 2, BATCH], F32)
        jobs = [job for n, w in enumerate((wq, wk, wv)) for job in halves(w, w_hi[:, n, :, :], w_lo[:, n, :, :])]
        stage_v = stage[:, :, :]
        load_w, split_hi, split_lo, w_done, n_w = split_loader(nc, ctx, "p1_w", stage_v, jobs)
        x_loaded = sem("p1_x_loaded")
        xt_ready = sem("p1_xt_ready", 1)
        xt_hi = sem("p1_xt_hi")
        xt_lo = sem("p1_xt_lo")
        proj = sem("p1_proj")
        qk_hi = sem("p1_qk_hi")
        qk_lo = sem("p1_qk_lo")
        v_copied = sem("p1_v_copied")
        qk_stored = [sem(f"p1_qk_stored{k}", 1) for k in range(4)]
        v_stored = [sem(f"p1_v_stored{t}", 1) for t in range(CT)]
        raw_loaded = [sem(f"p1_raw_loaded{n}") for n in range(2)]
        passed = sem("p1_passed")
        piece_done = sem("p1_piece_done", 2)
        x_v = x.rearrange("b (c t p) d -> b c p t d", c=2, p=P)
        raw_v = [w.rearrange("(q k p) n -> q p k n", q=BATCH, p=P) for w in ffn_w]

        with nc.Block() as block:
            @block.gpsimd
            def _(pool):
                with pool.Fori(0, BATCH) as b:
                    for c in range(2):
                        pool.wait_ge(piece_done, 2 * b + c + 1)
                        pool.sem_inc(passed, 1)
                        n = raw_v[c].shape[2]
                        pool.dma_start(raw[:, c, :].rearrange("p (k n) -> p k n", k=n), raw_v[c][b]).then_inc(raw_loaded[c], 16)
                        pool.wait_ge(xt_ready, 1 + 8 * b + 4 * c)
                        pool.sem_inc(passed, 1)
                        pool.dma_start(xs[:, :, :], x_v[b, c]).then_inc(x_loaded, 16)

            @block.sync
            def _(sp):
                load_w(sp)
                with sp.Fori(0, BATCH) as b:
                    for c in range(2):
                        for j in range(2 * GROUPS):
                            dst = (q_dram, k_dram)[j % 2]
                            dst_v = dst[bass.ds(4 * b + j // 2, 1), :, :, c * CH:(c + 1) * CH].rearrange("o s p t -> p (o s) t")
                            sp.wait_ge(qk_lo, 8 + 16 * b + 8 * c + j + 1)
                            sp.dma_start(dst_v, f32(qk_out[:, j % 4, :, :])).then_inc(qk_stored[j % 4], 16)
                        for t in range(CT):
                            r0 = c * CH + t * P
                            dst_v = v_dram[bass.ds(4 * b, 4), r0:r0 + P, :].rearrange("g p e -> p g e")
                            sp.wait_ge(v_copied, 4 + 8 * b + 4 * c + t + 1)
                            sp.dma_start(dst_v, v_out[:, t, :].rearrange("p (g e) -> p g e", g=GROUPS)).then_inc(v_stored[t], 16)
                for k in range(4):
                    sp.wait_ge(qk_stored[k], 1 + 16 * 4 * BATCH)
                for t in range(CT):
                    sp.wait_ge(v_stored[t], 1 + 16 * 2 * BATCH)

            @block.tensor
            def _(pe):
                pe.sem_inc(proj, 2 * OUTS)
                with pe.Fori(0, BATCH) as b:
                    for c in range(2):
                        pe.wait_ge(x_loaded, 32 * b + 16 * c + 16)
                        for kt in range(KT):
                            pe.wait_ge(xt_lo, 8 * b + 4 * c + kt + 1)
                            for t in range(CT):
                                mm = pe.transpose(psum[:, kt % 2, t * P:(t + 1) * P], xs[:, t, kt * P:(kt + 1) * P], ident[:, :])
                            mm.then_inc(xt_ready, 1)
                        pe.wait_ge(xt_lo, 2 + 8 * b + 4 * c + 4)
                        pe.wait_ge(w_done, n_w)
                        for o in range(OUTS):
                            if o < 2:
                                pe.wait_ge(qk_lo, 16 * b + 8 * c + 7 + o)
                            elif o < 6:
                                pe.wait_ge(v_copied, 8 * b + 4 * c + o - 1)
                            else:
                                pe.wait_ge(qk_lo, 8 + 16 * b + 8 * c + o - 5)
                            bank = psum[:, 2 + o % 6, :]
                            n = 0
                            for kt in range(KT):
                                for part in range(3):
                                    xp = (xT_hi, xT_lo, xT_hi)[part]
                                    wp = (w_hi, w_hi, w_lo)[part]
                                    if o < 2 * GROUPS:
                                        g = o // 2
                                        lhsT, rhs = wp[:, o % 2, kt, g * P:(g + 1) * P], xp[:, c, kt, :]
                                    else:
                                        t = o - 2 * GROUPS
                                        lhsT, rhs = xp[:, c, kt, t * P:(t + 1) * P], wp[:, 2, kt, :]
                                    mm = pe.matmul(bank, lhsT, rhs, start=(n == 0), stop=(n == 3 * KT - 1))
                                    n += 1
                            mm.then_inc(proj, 1)

            @block.scalar
            def _(act):
                split_hi(act)
                act.sem_inc(v_copied, 4)
                with act.Fori(0, BATCH) as b:
                    for c in range(2):
                        for kt in range(KT):
                            if kt == 0:
                                act.wait_ge(proj, 24 * b + 12 * c + 12)
                            act.wait_ge(xt_ready, 1 + 8 * b + 4 * c + kt + 1)
                            act.activation(xT_hi[:, c, kt, :], psum[:, kt % 2, :], ACT.Copy).then_inc(xt_hi, 1)
                        for o in range(OUTS):
                            bank = psum[:, 2 + o % 6, :]
                            act.wait_ge(proj, 2 * OUTS + 24 * b + 12 * c + o + 1)
                            if o < 2 * GROUPS:
                                act.wait_ge(qk_stored[o % 4], 1 + 64 * b + 32 * c + 16 * (o // 4))
                                act.activation(qk_out[:, o % 4, 0, :], bank, ACT.Copy).then_inc(qk_hi, 1)
                            else:
                                t = o - 2 * GROUPS
                                act.wait_ge(v_stored[t], 1 + 32 * b + 16 * c)
                                act.activation(v_out[:, t, :], bank, ACT.Copy).then_inc(v_copied, 1)

            @block.vector
            def _(dve):
                dve.sem_inc(xt_lo, 2)
                dve.sem_inc(qk_lo, 8)
                split_lo(dve)
                with dve.Fori(0, BATCH) as b:
                    for c in range(2):
                        for kt in range(KT):
                            dve.wait_ge(xt_hi, 8 * b + 4 * c + kt + 1)
                            dve.tensor_tensor(xT_lo[:, c, kt, :], psum[:, kt % 2, :], f32(xT_hi[:, c, kt, :]),
                                              ALU.subtract).then_inc(xt_lo, 1)
                        for j in range(2 * GROUPS):
                            dve.wait_ge(qk_hi, 16 * b + 8 * c + j + 1)
                            dve.tensor_tensor(qk_out[:, j % 4, 1, :], psum[:, 2 + j % 6, :], f32(qk_out[:, j % 4, 0, :]),
                                              ALU.subtract).then_inc(qk_lo, 1)
                            if j == GROUPS:
                                dve.wait_ge(raw_loaded[c], 16 * b + 16)
                                dve.tensor_reduce(piece_max[:, c, bass.ds(b, 1)], raw[:, c, :], AX.X, ALU.max,
                                                  apply_absolute_value=True).then_inc(piece_done, 1)
                dve.wait_ge(piece_done, 2 + 2 * BATCH)
                dve.tensor_reduce(w_max[:, :], piece_max[:, :, :], AX.X, ALU.max).then_inc(piece_done, 1)


def phase_attention(nc, psum, ident, q_dram, k_dram, v_dram, o_dram, ffn_w, w_max, tern, kept):
    NU = BATCH * GROUPS
    DOWN = SEQ // P
    PER_UNIT = HPG * CT
    S_PER_GROUP = 2 * (PER_UNIT + 1)
    STEPS = [CT, 2 * CT]
    ST_PER_GROUP = HPG * sum(STEPS)
    J_PER_GROUP = sum(STEPS)
    KEY_STEPS = [(0, j) for j in range(STEPS[0])] + [(1, j) for j in range(STEPS[1])]
    LOADS = 6 * 16
    with Phase(nc) as ctx:
        sb = lambda n, s, d: ctx.enter_context(nc.sbuf_tensor(n, s, d))
        sem = ctx.semaphore
        kst = [sb(f"p2_kst{s}", [P, HPG, SEQ], F32R) for s in range(2)]
        qst = [sb(f"p2_qst{s}", [P, HPG, SEQ], F32R) for s in range(2)]
        vs = [sb(f"p2_v{s}", [P, DOWN, P], F32) for s in range(2)]
        probs = sb("p2_probs", [P, 2, HPG, CH], F32)
        junk = sb("p2_junk", [P, 2, SEQ], F32)
        rowmax = sb("p2_rowmax", [P, 2, PER_UNIT], F32)
        negmax = sb("p2_negmax", [P, 2, 2, PER_UNIT], F32R)
        causal = sb("p2_causal", [P, SEQ], F32)
        pick = sb("p2_pick", [2 * PER_UNIT, PER_UNIT], F32)
        ones = sb("p2_ones", [P, HD], F32)
        o_raw = sb("p2_o_raw", [P, 2, CH], F32)
        recip = sb("p2_recip", [P, CH], F32)
        o_out = sb("p2_o_out", [P, 2, CH], F32)

        TW = tern.shape[2] // (NU // 2)
        KEPT = kept.shape[3]
        raw = sb("p2_raw", [P, 2, TW], F32)
        below = sb("p2_below", [P, 2, TW], F32)
        above = sb("p2_above", [P, 2, TW], F32)
        bound = sb("p2_bound", [P, 2, 3], F32)
        raw_loaded = [sem(f"p2_raw_loaded{n}") for n in range(2)]
        bound_done = sem("p2_bound_done")
        tern_step = sem("p2_tern_step")
        TERN_STEPS = 7
        raw_v = [ffn_w[0].rearrange("(k p) n -> p k n", p=P), ffn_w[1].rearrange("(k p) n -> p k n", p=P)]
        n_rows = [v.shape[1] for v in raw_v]

        def eighth(ap, n, i):
            if n == 0:
                return ap[:, :, bass.ds(TW // KT * i, TW // KT)]
            return ap[:, bass.ds(TW // D * i, TW // D), :]

        const_done = sem("p2_const_done")
        CONSTS = 8
        loaded = [[sem(f"p2_loaded{s}_{c}") for c in range(2)] for s in range(2)]
        v_loaded = [sem(f"p2_v_loaded{s}") for s in range(2)]
        s_ready = sem("p2_s_ready")
        s_used = sem("p2_s_used")
        rm_done = sem("p2_rm_done")
        nm_ready = sem("p2_nm_ready")
        st_ready = sem("p2_st_ready")
        p_ready = sem("p2_p_ready")
        p_masked = sem("p2_p_masked")
        pv_done = sem("p2_pv_done")
        rec_done = sem("p2_rec_done")
        o_read = sem("p2_o_read")
        o_normed = sem("p2_o_normed", 1)
        passed = sem("p2_passed")
        o_stored = [sem(f"p2_o_stored{c}", 1) for c in range(2)]

        ENTRIES = [(0, e // HPG, e % HPG) for e in range(PER_UNIT)] + [(1, e // HPG, e % HPG) for e in range(PER_UNIT)]
        ENTRIES.insert(PER_UNIT + 3, (0, None, None))
        ENTRIES.append((1, None, None))
        BUILT = [PER_UNIT + 4, S_PER_GROUP]
        NORM0 = 4 * (STEPS[0] + 1)
        QUARTER = list(range(NORM0 - 10, NORM0)) + list(range(NORM0 + 4, 4 * J_PER_GROUP))
        assert len(QUARTER) == S_PER_GROUP
        BESIDE_C0 = sum(q < NORM0 for q in QUARTER)

        S_BANKS = [psum[:, 0:2, :].rearrange("p a n -> p (a n)"), psum[:, 2:4, :].rearrange("p a n -> p (a n)")]
        ST_BANKS = [psum[:, 4, :], psum[:, 5, :]]
        O_BANK, SUM_BANK = psum[:, 6, :], psum[:, 7, :]

        def half(eng, body):
            with eng.Fori(0, NU // 2 - 1) as i:
                body(i, False)
            body(NU // 2 - 1, True)

        with nc.Block() as block:
            @block.gpsimd
            def _(pool):
                def build(n, ins):
                    ins.then_inc(const_done, 1)
                    pool.wait_ge(const_done, n)
                build(1, pool.memset(causal[:, :], 0.0))
                build(2, pool.memset(pick[:, :], 0.0))
                build(3, pool.memset(ones[:, :], 1.0))
                for s in range(2):
                    build(4 + s, pool.memset(f32(kst[s][96:128, :, :]), 1.0))
                tri = causal[:, SEQ - P:SEQ]
                build(6, pool.affine_select(out=tri, in_=tri, compare_op=ALU.is_ge, fill=FLOOR, base=0,
                                            pattern=[[-1, P]], channel_multiplier=1))
                for k in range(2):
                    build(7 + k, pool.affine_select(out=pick[:, :], in_=pick[:, :], compare_op=ALU.not_equal, fill=1.0,
                                                    base=-PER_UNIT * k, pattern=[[-1, PER_UNIT]], channel_multiplier=1))

                for n in range(2):
                    build(9 + n, pool.partition_all_reduce(bound[:, n, 0:1], w_max[:, n:n + 1], P, bass.bass_isa.ReduceOp.max))
                build(11, pool.tensor_scalar(bound[:, :, 1], bound[:, :, 0], TERN, None, ALU.mult))
                build(12, pool.tensor_scalar(bound[:, :, 2], bound[:, :, 1], -1.0, None, ALU.mult))
                tiles = lambda ap, n: ap.rearrange("p (k n) -> p k n", k=(KT, TW // D)[n])

                def load_raw(i, n):
                    pool.dma_start(tiles(raw[:, n, :], n), eighth(raw_v[n], n, i)).then_inc(raw_loaded[n], 16)

                def ternarize(i, n, last):
                    w, out = raw[:, n, :], eighth(tern[:, n, :].rearrange("p (k n) -> p k n", k=n_rows[n]), n, i)
                    before = TERN_STEPS * (2 * i + n)
                    pool.wait_ge(raw_loaded[n], 16 * i + 16)
                    pool.sem_inc(passed, 1)
                    pool.tensor_scalar(below[:, n, :], w, bound[:, n, 2:3], None, ALU.is_lt).then_inc(tern_step, 1)
                    pool.tensor_scalar(above[:, n, :], w, bound[:, n, 1:2], None, ALU.is_gt).then_inc(tern_step, 1)
                    pool.wait_ge(tern_step, before + 2)
                    pool.sem_inc(passed, 1)
                    pool.tensor_tensor(out, tiles(above[:, n, :], n), tiles(below[:, n, :], n), ALU.subtract).then_inc(tern_step, 1)
                    pool.wait_ge(tern_step, before + 3)
                    pool.sem_inc(passed, 1)
                    pool.tensor_tensor(tiles(below[:, n, :], n), tiles(w, n), f32(out), ALU.mult).then_inc(tern_step, 1)
                    pool.wait_ge(tern_step, before + 4)
                    if not last:
                        pool.sem_inc(passed, 1)
                        load_raw(i + 1, n)
                    half = TW // 2
                    for fold in range(3):
                        dst = below[:, n, 0:half] if half > KEPT else kept[:, n, bass.ds(i, 1), :].rearrange("p o k -> p (o k)")
                        pool.sem_inc(passed, 1)
                        pool.tensor_tensor(dst, below[:, n, 0:half], below[:, n, half:2 * half], ALU.add).then_inc(tern_step, 1)
                        pool.wait_ge(tern_step, before + 5 + fold)
                        half //= 2

                for n in range(2):
                    load_raw(0, n)

                def body(i, last):
                    for s in range(2):
                        for step, (c, j) in enumerate(KEY_STEPS):
                            if (c, j) == (1, 0):
                                ternarize(i, s, last)
                            for g in range(HPG):
                                if j >= CT * c:
                                    at = ST_PER_GROUP * s + HPG * step + g + 1
                                    q0 = P * j - CH * c
                                    blk = probs[:, step % 2, g, q0:q0 + P]
                                    pool.wait_ge(p_ready, 2 + 2 * ST_PER_GROUP * i + at)
                                    pool.sem_inc(passed, 1)
                                    pool.affine_select(out=blk, in_=blk, compare_op=ALU.is_ge, fill=0.0, base=0,
                                                       pattern=[[1, P]], channel_multiplier=-1).then_inc(p_masked, 1)
                half(pool, body)

            @block.sync
            def _(sp):
                def load(u, s, k):
                    for c in range(2):
                        cols = slice(c * CH, (c + 1) * CH)
                        for dst, src, rows in ((qst, q_dram, (0, 0, 1)), (kst, k_dram, (0, 1, 0))):
                            for r, part in enumerate(rows):
                                view = src[u, part].rearrange("(h d) t -> d h t", d=HD)[:, :, cols]
                                sp.dma_start(f32(dst[s][r * HD:(r + 1) * HD, :, cols]), view).then_inc(loaded[s][c], 16)
                    sp.dma_start(vs[s][:, :, :], v_dram[u].rearrange("(t p) e -> p t e", p=P)).then_inc(v_loaded[s], 16)

                def store(u, c, n):
                    sp.wait_ge(o_normed, 1 + n + 1)
                    sp.dma_start(o_dram[u, :, c * CH:(c + 1) * CH], o_out[:, c, :]).then_inc(o_stored[c], 16)

                load(0, 0, 0)
                load(1, 1, 0)

                def body(i, last):
                    for s in range(2):
                        store(2 * i + s, 0, 4 * i + 2 * s)
                        if not last:
                            sp.wait_ge(pv_done, 2 + J_PER_GROUP * (2 * i + s + 1))
                            load(2 * i + 2 + s, s, i + 1)
                        store(2 * i + s, 1, 4 * i + 2 * s + 1)
                half(sp, body)
                for c in range(2):
                    sp.wait_ge(o_stored[c], 1 + 16 * NU)

            @block.tensor
            def _(pe):
                def score_entry(u, s, m):
                    c, tile, g = ENTRIES[m]
                    bank = S_BANKS[m % 2]
                    pe.wait_ge(s_used, S_PER_GROUP * u + m + 1)
                    if tile is None:
                        pe.wait_ge(nm_ready, 2 * u + c + 1)
                        pe.transpose(bank[0:2 * PER_UNIT, 0:P], f32(negmax[:, c, :, :]).rearrange("p a n -> p (a n)"),
                                     ident[:, :]).then_inc(s_ready, 1)
                        return
                    t = CT * c + tile
                    n = P * (t + 1)
                    for k0 in range(0, n, CH):
                        k1 = min(n, k0 + CH)
                        mm = pe.matmul(bank[:, k0:k1], qst[s][0:96, g, t * P:(t + 1) * P],
                                       kst[s][0:96, g, k0:k1], start=True, stop=True)
                    mm.then_inc(s_ready, 1)

                def scores_T(u, s, c, j, st):
                    q0, g = max(0, P * j - CH * c), st % HPG
                    pe.wait_ge(p_ready, ST_PER_GROUP * u + st + 1)
                    if j == 0 and g == 0:
                        pe.wait_ge(s_used, 2 + S_PER_GROUP * u + BUILT[c])
                    pe.matmul(ST_BANKS[st % 2][:, q0:CH], kst[s][:, g, j * P:(j + 1) * P],
                              qst[s][:, g, c * CH + q0:(c + 1) * CH], start=True, stop=True).then_inc(st_ready, 1)

                def with_v(u, s, c, j, step, use_ones):
                    q0 = max(0, P * j - CH * c)
                    if not use_ones:
                        if (c, j) == (0, 0):
                            pe.wait_ge(v_loaded[s], 8 * u + 16 - 8 * s)
                        if j == 0:
                            pe.wait_ge(o_read, 2 * u + c + 1)
                        pe.wait_ge(p_ready, 2 + ST_PER_GROUP * u + HPG * (step + 1))
                        if j >= CT * c:
                            pe.wait_ge(p_masked, PER_UNIT * (2 * u + c) + HPG * (j - CT * c + 1))
                    bank = SUM_BANK if use_ones else O_BANK
                    for g in range(HPG):
                        lhsT = ones[:, :] if use_ones else vs[s][:, j, g * HD:(g + 1) * HD]
                        mm = pe.matmul(bank[g * HD:(g + 1) * HD, q0:CH], lhsT, probs[:, step % 2, g, q0:CH],
                                       start=(j == 0), stop=(j == STEPS[c] - 1))
                    if use_ones:
                        mm.then_inc(pv_done, 1)

                def second_pass(i, last):
                    before = None
                    for s in range(2):
                        u = 2 * i + s
                        entries = [] if last and s == 1 else list(range(S_PER_GROUP))
                        for step, (c, j) in enumerate(KEY_STEPS):
                            for quarter in range(4):
                                if quarter % 2 == 0:
                                    scores_T(u, s, c, j, HPG * step + quarter)
                                    scores_T(u, s, c, j, HPG * step + quarter + 1)
                                elif before:
                                    with_v(*before, use_ones=(quarter == 3))
                                if entries and QUARTER[entries[0]] == 4 * step + quarter:
                                    if entries[0] in (0, PER_UNIT):
                                        pe.wait_ge(loaded[1 - s][entries[0] // PER_UNIT], LOADS * (i + 1 + s))
                                    score_entry(u + 1, 1 - s, entries.pop(0))
                            before = (u, s, c, j, step)
                    with_v(*before, use_ones=False)
                    with_v(*before, use_ones=True)

                pe.sem_inc(pv_done, 2)
                pe.wait_ge(const_done, CONSTS)
                pe.wait_ge(loaded[0][0], LOADS)
                pe.wait_ge(loaded[0][1], LOADS)
                for m in range(S_PER_GROUP):
                    score_entry(0, 0, m)

                half(pe, second_pass)

            @block.scalar
            def _(act):
                act.sem_inc(p_ready, 2)
                act.sem_inc(o_read, 1)

                def evacuate(u, c):
                    act.wait_ge(pv_done, 2 + J_PER_GROUP * u + sum(STEPS[:c + 1]))
                    act.wait_ge(o_normed, 1 + 2 * u + c)
                    act.activation(o_raw[:, 0, :], O_BANK, ACT.Copy)
                    act.activation(o_raw[:, 1, :], SUM_BANK, ACT.Copy).then_inc(o_read, 1)

                def body(i, last):
                    before = None
                    for s in range(2):
                        u = 2 * i + s
                        for step, (c, j) in enumerate(KEY_STEPS):
                            q0 = max(0, P * j - CH * c)
                            act.wait_ge(pv_done, J_PER_GROUP * u + step + 1)
                            for g in range(HPG):
                                st = HPG * step + g
                                act.wait_ge(st_ready, ST_PER_GROUP * u + st + 1)
                                act.activation(probs[:, step % 2, g, q0:CH], ST_BANKS[st % 2][:, q0:CH], ACT.Exp,
                                               scale=SM_SCALE).then_inc(p_ready, 1)
                            if j == 0 and before:
                                evacuate(*before)
                            before = (u, c)
                    evacuate(*before)
                half(act, body)

            @block.vector
            def _(dve):
                dve.sem_inc(s_used, 2)
                dve.wait_ge(const_done, CONSTS)

                def maximum(u, s, m):
                    c, tile, g = ENTRIES[m]
                    base = S_PER_GROUP * u
                    dve.wait_ge(s_ready, base + m + 1)
                    dve.wait_ge(s_used, base + m + 1)
                    dve.sem_inc(passed, 1)
                    if tile is not None:
                        n = P * (CT * c + tile + 1)
                        col = g * CT + tile
                        dve.tensor_tensor_reduce(junk[:, m % 2, 0:n], S_BANKS[m % 2][:, 0:n], causal[:, SEQ - n:SEQ], 1.0, FLOOR,
                                                 ALU.add, ALU.max, rowmax[:, c, col:col + 1]).then_inc(s_used, 1)
                        if (tile, g) == (CT - 1, HPG - 1):
                            dve.wait_ge(s_used, 2 + base + m + 1)
                            dve.tensor_scalar(negmax[:, c, 0, :], rowmax[:, c, :], -1.0, None, ALU.mult).then_inc(rm_done, 1)
                            dve.wait_ge(rm_done, 2 * u + c + 1)
                            dve.scalar_tensor_tensor(out=negmax[:, c, 1, :], in0=rowmax[:, c, :], scalar=-1.0,
                                                     in1=f32(negmax[:, c, 0, :]), op0=ALU.mult, op1=ALU.subtract).then_inc(nm_ready, 1)
                        return
                    rows = [2 * PER_UNIT, HPG, CT, P]
                    dve.tensor_tensor(
                        qst[s][96:128, :, c * CH:(c + 1) * CH].rearrange("p g (t q) -> p g t q", q=P),
                        S_BANKS[m % 2][0:2 * PER_UNIT, 0:P][:, None, None, :].to_broadcast(rows),
                        pick[:, :].rearrange("p (g t) -> p g t", g=HPG)[:, :, :, None].to_broadcast(rows),
                        ALU.mult).then_inc(s_used, 1)

                def normalize(u, c):
                    dve.wait_ge(o_read, 1 + 2 * u + c + 1)
                    dve.wait_ge(o_stored[c], 1 + 16 * u)
                    dve.reciprocal(recip[:, :], o_raw[:, 1, :]).then_inc(rec_done, 1)
                    dve.wait_ge(rec_done, 2 * u + c + 1)
                    dve.tensor_tensor(o_out[:, c, :], o_raw[:, 0, :], recip[:, :], ALU.mult).then_inc(o_normed, 1)

                for m in range(S_PER_GROUP):
                    maximum(0, 0, m)

                def body(i, last):
                    for s in range(2):
                        u = 2 * i + s
                        if not (last and s == 1):
                            for m in range(BESIDE_C0):
                                maximum(u + 1, 1 - s, m)
                        normalize(u, 0)
                        if not (last and s == 1):
                            for m in range(BESIDE_C0, S_PER_GROUP):
                                maximum(u + 1, 1 - s, m)
                        normalize(u, 1)
                half(dve, body)


class Banks:

    def __init__(self, nc, ctx, name, psum, first, size, per_iter):
        assert per_iter % size == 0
        self.psum, self.first, self.size, self.turns = psum, first, size, per_iter // size
        self.filled = [ctx.semaphore(f"{name}_filled{k}", 1) for k in range(size)]
        self.freed = [ctx.semaphore(f"{name}_freed{k}", 1) for k in range(size)]

    def bank(self, m):
        return self.psum[:, self.first + m % self.size, :]

    def wait_free(self, pe, it, m):
        self.wait_freed(pe, m % self.size, it * self.turns + m // self.size)

    def wait_full(self, eng, it, m):
        self.wait_filled(eng, m % self.size, it * self.turns + m // self.size + 1)

    def wait_filled(self, eng, bank, n):
        eng.wait_ge(self.filled[bank], 1 + n)

    def wait_freed(self, eng, bank, n):
        eng.wait_ge(self.freed[bank], 1 + n)

    def fill(self, ins, m):
        return ins.then_inc(self.filled[m % self.size], 1)

    def free(self, ins, m):
        return ins.then_inc(self.freed[m % self.size], 1)


def partials(pe, bank, terms):
    for n, (lhsT, rhs) in enumerate(terms):
        mm = pe.matmul(bank, lhsT, rhs, start=(n == 0), stop=(n == len(terms) - 1))
    return mm


class LayerNorm:
    FROM = 2 * CT

    def __init__(self, nc, ctx, name):
        sem = lambda k: ctx.semaphore(f"{name}_{k}")
        self.stats = ctx.enter_context(nc.sbuf_tensor(f"{name}_stats", [P, CT, 6], F32))
        self.meanvar = ctx.enter_context(nc.sbuf_tensor(f"{name}_meanvar", [P, CT, 2], F32))
        self.vareps = ctx.enter_context(nc.sbuf_tensor(f"{name}_vareps", [P, CT], F32))
        self.rstd = ctx.enter_context(nc.sbuf_tensor(f"{name}_rstd", [P, CT], F32))
        self.power = ctx.enter_context(nc.sbuf_tensor(f"{name}_power", [P, CT], F32))
        self.summed, self.got_stats, self.got_mean = sem("summed"), sem("got_stats"), sem("got_mean")
        self.passed = sem("passed")
        self.ready, self.eps_added, self.got_rstd, self.normed = sem("ready"), sem("eps_added"), sem("got_rstd"), sem("normed")

    def setup(self, pool):
        pool.memset(self.power[:, :], -0.5).then_inc(self.ready, 1)
        pool.wait_ge(self.ready, 1)

    def pool_part(self, pool, n):
        pool.wait_ge(self.got_mean, n * CT + CT)
        pool.sem_inc(self.passed, 1)
        pool.tensor_scalar(self.vareps[:, :], self.meanvar[:, :, 1], LN_EPS, None, ALU.add).then_inc(self.eps_added, 1)
        pool.wait_ge(self.eps_added, n + 1)
        pool.tensor_tensor(self.rstd[:, :], self.vareps[:, :], self.power[:, :], ALU.pow).then_inc(self.got_rstd, 1)

    def vector_part(self, dve, n, src, dst):
        self.find_statistics(dve, n, src)
        self.normalize_tiles(dve, n, src, dst)

    def find_statistics(self, dve, n, src):
        for t in range(CT):
            dve.wait_ge(self.summed, self.FROM + n * CT + t + 1)
            dve.bn_stats(self.stats[:, t, :], src(t)).then_inc(self.got_stats, 1)
        dve.wait_ge(self.got_stats, n * CT + CT)
        dve.sem_inc(self.passed, 1)
        for t in range(CT):
            dve.bn_aggr(self.meanvar[:, t, :], self.stats[:, t, :]).then_inc(self.got_mean, 1)

    def normalize_tiles(self, dve, n, src, dst):
        dve.wait_ge(self.got_rstd, n + 1)
        for t in range(CT):
            dve.tensor_scalar(dst(t), src(t), self.meanvar[:, t, 0:1], self.rstd[:, t:t + 1],
                              ALU.subtract, ALU.mult).then_inc(self.normed, 1)


def batches(eng, body):
    with eng.Fori(0, BATCH - 1) as b:
        body(b, False)
    body(BATCH - 1, True)


def rows(vec):
    return vec.rearrange("(o n) -> o n", o=1).to_broadcast([P, vec.shape[0]])


def phase_out0(nc, psum, x, wo, bo, o_dram, x1_dram, tern, kept, alpha):
    NT = tern.shape[2]
    PIECES = 4
    with Phase(nc) as ctx:
        sb = lambda n, s, d: ctx.enter_context(nc.sbuf_tensor(n, s, d))
        sem = ctx.semaphore
        stage = sb("p3_stage", [P, 2, KT * D // 2], F32)
        w_hi = sb("p3_w_hi", [P, KT, D], F32R)
        w_lo = sb("p3_w_lo", [P, KT, D], F32R)
        o_in = sb("p3_o", [P, 2, GROUPS, CH], F32)
        o_hi = sb("p3_o_hi", [P, 2, GROUPS, CH], F32R)
        o_lo = sb("p3_o_lo", [P, 2, GROUPS, CH], F32R)
        xs = sb("p3_x", [P, 2, CT, D], F32)
        bias = sb("p3_bias", [P, D], F32)
        squares = sb("p3_squares", [P, NT // PIECES], F16)
        counts = sb("p3_counts", [P, 2, PIECES], F32)
        totals = sb("p3_totals", [P, 4], F32)
        totals_all = sb("p3_totals_all", [P, 4], F32)
        per_count = sb("p3_per_count", [P, 2], F32)
        load_w, split_hi, split_lo, w_done, n_w = split_loader(nc, ctx, "p3_w", stage[:, :, :], halves(wo, w_hi[:, :, :], w_lo[:, :, :]))
        ln = LayerNorm(nc, ctx, "p3_ln")
        banks = Banks(nc, ctx, "p3_bank", psum, 0, 8, 2 * CT)
        bias_loaded = sem("p3_bias_loaded")
        o_loaded = [sem(f"p3_o_loaded{c}") for c in range(2)]
        x_loaded = [sem(f"p3_x_loaded{c}") for c in range(2)]
        o_hi_done, o_lo_done = sem("p3_o_hi_done"), sem("p3_o_lo_done")
        x_biased = sem("p3_x_biased")
        stored = [sem(f"p3_stored{c}") for c in range(2)]
        counted, reduced, alpha_step = sem("p3_counted"), sem("p3_reduced"), sem("p3_alpha_step")
        x_v = x.rearrange("b (c t p) d -> b c p t d", c=2, p=P)

        def load_o(eng, b, c):
            src = o_dram[bass.ds(4 * b, GROUPS), :, c * CH:(c + 1) * CH].rearrange("g p t -> p g t")
            eng.dma_start(o_in[:, c, :, :], src).then_inc(o_loaded[c], 16)

        with nc.Block() as block:
            @block.sync
            def _(sp):
                load_w(sp)
                sp.dma_start(bias[:, :], rows(bo)).then_inc(bias_loaded, 16)
                for c in range(2):
                    sp.dma_start(xs[:, c, :, :], x_v[0, c]).then_inc(x_loaded[c], 16)

                def body(b, last):
                    for c in range(2):
                        sp.wait_ge(ln.normed, 8 * b + 4 * c + 4)
                        sp.dma_start(x1_dram[2 * b + c].rearrange("(t p) d -> p t d", p=P), xs[:, c, :, :]).then_inc(stored[c], 16)
                        sp.wait_ge(stored[c], 16 * b + 16)
                        if not last:
                            sp.dma_start(xs[:, c, :, :], x_v[b + 1, c]).then_inc(x_loaded[c], 16)
                batches(sp, body)

            @block.gpsimd
            def _(pool):
                ln.setup(pool)
                pool.wait_ge(bias_loaded, 16)

                def split(b, c):
                    pool.wait_ge(o_hi_done, 2 * b + c + 1)
                    pool.tensor_tensor(o_lo[:, c, :, :], o_in[:, c, :, :], f32(o_hi[:, c, :, :]), ALU.subtract).then_inc(o_lo_done, 1)

                def add_bias(b, c):
                    pool.wait_ge(x_loaded[c], 16 * b + 16)
                    pool.tensor_tensor(xs[:, c, :, :], xs[:, c, :, :], bias[:, None, :].to_broadcast([P, CT, D]), ALU.add).then_inc(x_biased, 1)

                split(0, 0)
                add_bias(0, 0)
                pool.wait_ge(counted, 2 * PIECES + 2)
                pool.partition_all_reduce(totals_all[:, :], totals[:, :], P, bass.bass_isa.ReduceOp.add).then_inc(reduced, 1)

                def body(b, last):
                    split(b, 1)
                    ln.pool_part(pool, 2 * b)
                    add_bias(b, 1)
                    if not last:
                        split(b + 1, 0)
                    ln.pool_part(pool, 2 * b + 1)
                    if not last:
                        add_bias(b + 1, 0)
                batches(pool, body)

            @block.scalar
            def _(act):
                for c in range(2):
                    load_o(act, 0, c)
                split_hi(act)

                def body(b, last):
                    for c in range(2):
                        act.wait_ge(o_loaded[c], 16 * b + 16)
                        banks.wait_filled(act, CT * c + CT - 1, b)
                        act.activation(o_hi[:, c, :, :], o_in[:, c, :, :], ACT.Copy).then_inc(o_hi_done, 1)
                        if not last:
                            act.wait_ge(o_lo_done, 2 * b + c + 1)
                            load_o(act, b + 1, c)
                batches(act, body)

            @block.tensor
            def _(pe):
                pe.wait_ge(w_done, n_w)

                def body(b, last):
                    for c in range(2):
                        pe.wait_ge(o_lo_done, 2 * b + c + 1)
                        for t in range(CT):
                            m = CT * c + t
                            tok = slice(t * P, (t + 1) * P)
                            pe.wait_ge(ln.summed, 8 * b + m + 1)
                            banks.fill(partials(pe, banks.bank(m), [
                                (o[:, c, k, tok], w[:, k, :]) for k in range(KT)
                                for o, w in ((o_hi, w_hi), (o_lo, w_hi), (o_hi, w_lo))]), m)
                batches(pe, body)

            @block.vector
            def _(dve):
                split_lo(dve)
                dve.sem_inc(ln.summed, ln.FROM)
                for n in range(2):
                    for q in range(PIECES):
                        part = f32(tern[:, n, q * NT // PIECES:(q + 1) * NT // PIECES])
                        if n + q > 0:
                            dve.wait_ge(counted, PIECES * n + q)
                        dve.tensor_tensor_reduce(squares[:, :], part, part, 1.0, 0.0, ALU.mult, ALU.add,
                                                 counts[:, n, q:q + 1]).then_inc(counted, 1)
                dve.wait_ge(counted, 2 * PIECES)
                dve.tensor_reduce(totals[:, 0:2], kept[:, :, :, :].rearrange("p n i k -> p n (i k)"), AX.X, ALU.add).then_inc(counted, 1)
                dve.tensor_reduce(totals[:, 2:4], counts[:, :, :], AX.X, ALU.add).then_inc(counted, 1)
                dve.wait_ge(reduced, 1)
                dve.tensor_scalar(totals_all[:, 2:4], totals_all[:, 2:4], 1.0, None, ALU.max).then_inc(alpha_step, 1)
                dve.wait_ge(alpha_step, 1)
                dve.reciprocal(per_count[:, :], totals_all[:, 2:4]).then_inc(alpha_step, 1)
                dve.wait_ge(alpha_step, 2)
                dve.tensor_tensor(alpha[:, :], totals_all[:, 0:2], per_count[:, :], ALU.mult).then_inc(alpha_step, 1)

                def body(b, last):
                    for c in range(2):
                        dve.wait_ge(x_biased, 2 * b + c + 1)
                        for t in range(CT):
                            m = CT * c + t
                            banks.wait_full(dve, b, m)
                            dve.tensor_tensor(xs[:, c, t, :], banks.bank(m), xs[:, c, t, :], ALU.add).then_inc(ln.summed, 1)
                        ln.vector_part(dve, 2 * b + c, lambda t: xs[:, c, t, :], lambda t: xs[:, c, t, :])
                batches(dve, body)


def phase_ffn0(nc, psum, ident, tern, alpha, b1, b2, x1_dram, y_dram, y_max):
    with Phase(nc) as ctx:
        sb = lambda n, s, d: ctx.enter_context(nc.sbuf_tensor(n, s, d))
        sem = ctx.semaphore
        tern1 = tern[:, 0, :].rearrange("p (k n) -> p k n", k=KT)
        tern2 = tern[:, 1, :].rearrange("p (k n) -> p k n", k=HT)
        b1c = sb("p4_b1", [P, HT], F32)
        b2r = sb("p4_b2", [P, D], F32)
        x1 = sb("p4_x1", [P, CT, D], F32)
        xT_hi = sb("p4_xT_hi", [P, 2, KT, CH], F32R)
        xT_lo = sb("p4_xT_lo", [P, 2, KT, CH], F32R)
        h = sb("p4_h", [P, 2, CH], F32)
        h_hi = sb("p4_h_hi", [P, 2, CH], F32R)
        h_lo = sb("p4_h_lo", [P, 2, CH], F32R)
        ys = sb("p4_y", [P, CT, D], F32)
        y_abs = sb("p4_y_abs", [P, CT + 2], F32)

        Y = Banks(nc, ctx, "p4_ybank", psum, 0, CT, 2 * CT)
        H = Banks(nc, ctx, "p4_hbank", psum, 4, 2, 2 * HT)
        T = Banks(nc, ctx, "p4_tbank", psum, 6, 2, 2 * KT)
        bias_loaded, x_loaded, cleared = sem("p4_bias_loaded"), sem("p4_x_loaded"), sem("p4_cleared")
        xt_hi, xt_lo = sem("p4_xt_hi"), sem("p4_xt_lo")
        hh_done, hl_done = sem("p4_h_hi_done"), sem("p4_h_lo_done", 2)
        h_used = sem("p4_h_used", 1)
        y_done, y_maxed, run_max = sem("p4_y_done"), sem("p4_y_maxed"), sem("p4_run_max")
        y_stored = sem("p4_y_stored", 1)

        with nc.Block() as block:
            @block.sync
            def _(sp):
                sp.dma_start(b1c[:, :], b1).then_inc(bias_loaded, 16)
                sp.dma_start(b2r[:, :], rows(b2)).then_inc(bias_loaded, 16)

                def load_x(b, c):
                    if not (type(b) is int and b == c == 0):
                        for k in range(2):
                            T.wait_filled(sp, k, 4 * b + 2 * c)
                    sp.dma_start(x1[:, :, :], x1_dram[2 * b + c].rearrange("(t p) d -> p t d", p=P)).then_inc(x_loaded, 16)

                load_x(0, 0)

                def body(b, last):
                    load_x(b, 1)
                    if not last:
                        load_x(b + 1, 0)
                    for c in range(2):
                        sp.wait_ge(y_maxed, 8 * b + 4 * c + 4)
                        sp.dma_start(y_dram[2 * b + c].rearrange("(t p) d -> p t d", p=P), ys[:, :, :]).then_inc(y_stored, 16)
                batches(sp, body)
                sp.wait_ge(y_stored, 1 + 16 * NCH)

            @block.scalar
            def _(act):
                act.preload_act_table(ACT.Gelu)
                act.wait_ge(bias_loaded, 32)

                def x_hi(b, c):
                    for k in range(KT):
                        T.wait_full(act, b, KT * c + k)
                        act.activation(xT_hi[:, c, k, :], T.bank(KT * c + k), ACT.Copy).then_inc(xt_hi, 1)

                x_hi(0, 0)

                def body(b, last):
                    for c in range(2):
                        for t in range(HT):
                            m = HT * c + t
                            H.wait_full(act, b, m)
                            act.wait_ge(hl_done, 2 * HT * b + m + 1)
                            H.free(act.activation(h[:, t % 2, :], H.bank(m), ACT.Gelu, bias=b1c[:, t:t + 1], scale=alpha[:, 0:1]), m)
                            if t == HT // 2 and not (c and last):
                                x_hi(b + c, 1 - c)
                batches(act, body)

            @block.tensor
            def _(pe):
                def transposes(b, c):
                    pe.wait_ge(x_loaded, 32 * b + 16 * c + 16)
                    for k in range(KT):
                        m = KT * c + k
                        pe.wait_ge(xt_lo, 8 * b + m + 1)
                        for t in range(CT):
                            mm = pe.transpose(T.bank(m)[:, t * P:(t + 1) * P], x1[:, t, k * P:(k + 1) * P], ident[:, :])
                        T.fill(mm, m)

                transposes(0, 0)

                def body(b, last):
                    def to_y(c, t):
                        pe.wait_ge(hl_done, 2 + 2 * HT * b + HT * c + t + 1)
                        for a in range(CT):
                            m = CT * c + a
                            if t == 0:
                                Y.wait_free(pe, b, m)
                            tok = slice(a * P, (a + 1) * P)
                            for part, src in enumerate((h_hi, h_lo)):
                                mm = pe.matmul(Y.bank(m), src[:, t % 2, tok], tern2[:, t, :], start=(t == 0 and part == 0),
                                               stop=(t == HT - 1 and part == 1))
                            if t == HT - 1:
                                Y.fill(mm, m)
                        if t < HT - 1:
                            mm.then_inc(h_used, 1)

                    for c in range(2):
                        pe.wait_ge(xt_lo, 2 + 8 * b + 4 * c + 4)
                        for t in range(HT + 1):
                            if t < HT:
                                m = HT * c + t
                                H.wait_free(pe, b, m)
                                H.fill(partials(pe, H.bank(m), [
                                    (tern1[:, k, t * P:(t + 1) * P], xp[:, c, k, :]) for k in range(KT) for xp in (xT_hi, xT_lo)]), m)
                            if t > 0:
                                to_y(c, t - 1)
                            if t == HT // 2 and not (c and last):
                                transposes(b + c, 1 - c)
                batches(pe, body)

            @block.vector
            def _(dve):
                dve.memset(y_abs[:, :], 0.0).then_inc(cleared, 1)
                dve.wait_ge(cleared, 1)
                dve.sem_inc(xt_lo, 2)
                dve.wait_ge(bias_loaded, 32)

                def x_lo(b, c):
                    for k in range(KT):
                        m = KT * c + k
                        dve.wait_ge(xt_hi, 8 * b + m + 1)
                        dve.tensor_tensor(xT_lo[:, c, k, :], T.bank(m), f32(xT_hi[:, c, k, :]), ALU.subtract).then_inc(xt_lo, 1)

                x_lo(0, 0)

                def body(b, last):
                    for c in range(2):
                        for t in range(HT):
                            m = HT * c + t
                            H.wait_freed(dve, m % 2, HT * b + m // 2 + 1)
                            if t == 1:
                                Y.wait_filled(dve, CT - 1, 2 * b + c)
                            else:
                                dve.wait_ge(h_used, 1 + (HT - 1) * (2 * b + c) + max(0, t - 1))
                            dve.tensor_copy(h_hi[:, t % 2, :], h[:, t % 2, :]).then_inc(hh_done, 1)
                            dve.wait_ge(hh_done, 2 * HT * b + m + 1)
                            dve.tensor_tensor(h_lo[:, t % 2, :], h[:, t % 2, :], f32(h_hi[:, t % 2, :]), ALU.subtract).then_inc(hl_done, 1)
                            if t == HT // 2 and not (c and last):
                                x_lo(b + c, 1 - c)
                        dve.wait_ge(y_stored, 1 + 32 * b + 16 * c)
                        for a in range(CT):
                            m = CT * c + a
                            Y.wait_full(dve, b, m)
                            Y.free(dve.scalar_tensor_tensor(out=ys[:, a, :], in0=Y.bank(m), scalar=alpha[:, 1:2], in1=b2r[:, :],
                                                            op0=ALU.mult, op1=ALU.add), m)
                        for a in range(CT):
                            m = CT * c + a
                            Y.wait_freed(dve, a, 2 * b + c + 1)
                            dve.tensor_reduce(y_abs[:, a:a + 1], ys[:, a, :], AX.X, ALU.max, apply_absolute_value=True).then_inc(y_maxed, 1)
                        dve.wait_ge(y_maxed, 8 * b + 4 * c + 4)
                        dve.tensor_reduce(y_abs[:, CT + c:CT + c + 1], y_abs[:, :], AX.X, ALU.max).then_inc(run_max, 1)
                        dve.wait_ge(run_max, 2 * b + c + 1)
                batches(dve, body)
                dve.tensor_copy(y_max[:, :], y_abs[:, CT + 1:CT + 2]).then_inc(run_max, 1)


def phase_linear_attention(nc, psum, ident, y_max, y_dram, x1_dram, wq, wk, wv, wo, bq, bk, bv, bo, decay_row, decay_col, residual, x3_dram):
    TT = SEQ // P
    EXT = P + HPG
    with Phase(nc) as ctx:
        sb = lambda n, s, d: ctx.enter_context(nc.sbuf_tensor(n, s, d))
        sem = ctx.semaphore
        w_hi = sb("p5_w_hi", [P, 4, KT, D], F32R)
        w_lo = sb("p5_w_lo", [P, 4, KT, D], F32R)
        ys = sb("p5_y", [P, 2, CT * D], F32)
        x1 = sb("p5_x1", [P, CT * D], F32)
        x2 = sb("p5_x2", [P, TT, D], F32)
        aT_hi = sb("p5_aT_hi", [P, 2, KT, CH], F32R)
        aT_lo = sb("p5_aT_lo", [P, 2, KT, CH], F32R)
        qT = sb("p5_qT", [P, GROUPS, SEQ], F32)
        ks = sb("p5_k", [P, TT, D], F32)
        vs = sb("p5_v", [P, TT, GROUPS, P + 2], F32)
        kv = sb("p5_kv", [P, GROUPS, EXT], F32)
        o_tok = ks
        den = sb("p5_den", [P, 2, HEADS], F32)
        rden = sb("p5_rden", [P, 2, HEADS], F32)
        same_head = sb("p5_same_head", [P, EXT], F32)
        quant = sb("p5_quant", [P, 3], F32)
        bq_c = sb("p5_bq", [P, GROUPS], F32)
        bias = sb("p5_bias", [P, 3, D], F32)
        dec_r = sb("p5_decay_row", [P, SEQ], F32)
        dec_c = sb("p5_decay_col", [P, TT], F32)

        load_w, split_hi, split_lo, w_done, n_w = split_loader(
            nc, ctx, "p5_w", qT[:, :, :], [job for n, w in enumerate((wq, wk, wv, wo)) for job in halves(w, w_hi[:, n, :, :], w_lo[:, n, :, :])])
        ln_a = LayerNorm(nc, ctx, "p5_ln_a")
        ln_b = LayerNorm(nc, ctx, "p5_ln_b")
        A = Banks(nc, ctx, "p5_abank", psum, 0, 4, 4 + 2 * TT + 4 * KT)
        B = Banks(nc, ctx, "p5_bbank", psum, 4, 4, 2 * (GROUPS + 2 * CT) + TT)
        a_x = lambda c, k: KT * c + k
        a_kv = lambda g: 2 * KT + g
        a_o = lambda t, half: 2 * KT + GROUPS + 2 * t + half
        a_oT = lambda c, k: 2 * KT + GROUPS + 2 * TT + KT * c + k
        b_q = lambda c, g: 3 * CT * c + g
        b_k = lambda c, t: 3 * CT * c + CT + t
        b_v = lambda c, t: 3 * CT * c + 2 * CT + t
        b_out = lambda t: 6 * CT + t

        built, consts_loaded = sem("p5_built"), sem("p5_consts_loaded")
        y_loaded = [sem(f"p5_y_loaded{c}") for c in range(2)]
        x1_loaded = sem("p5_x1_loaded")
        max_all, quant_ready = sem("p5_max_all"), sem("p5_quant_ready")
        rounding = sem("p5_rounding")
        t_hi, t_lo = sem("p5_t_hi"), sem("p5_t_lo", 1)
        q_relu, q_done = sem("p5_q_relu"), sem("p5_q_done")
        k_biased, k_done = sem("p5_k_biased"), sem("p5_k_done")
        v_done, kv_done = sem("p5_v_done"), sem("p5_kv_done")
        den_eps, den_inv, o_done = sem("p5_den_eps"), sem("p5_den_inv"), sem("p5_o_done")
        x2_biased = sem("p5_x2_biased")
        passed = sem("p5_passed")
        residual_stored = [sem(f"p5_residual_stored{c}") for c in range(2)]
        residual_loaded = [sem(f"p5_residual_loaded{c}") for c in range(2)]
        x3_stored = [sem(f"p5_x3_stored{c}", 1) for c in range(2)]
        tok = lambda t: slice(t * P, (t + 1) * P)

        by_tile = lambda ap: ap.rearrange("p (t d) -> p t d", t=CT)
        tiles = lambda ap: ap.rearrange("(t p) d -> p t d", p=P)
        chunk = lambda ap, c: ap[:, CT * c:CT * c + CT, :]

        def load_y(eng, b, c):
            eng.dma_start(by_tile(ys[:, c, :]), tiles(y_dram[2 * b + c])).then_inc(y_loaded[c], 16)

        def load_x1(eng, b, c):
            eng.dma_start(by_tile(x1[:, :]), tiles(x1_dram[2 * b + c])).then_inc(x1_loaded, 16)

        with nc.Block() as block:
            @block.sync
            def _(sp):
                load_y(sp, 0, 0)
                load_x1(sp, 0, 0)
                load_y(sp, 0, 1)
                load_w(sp)
                sp.dma_start(bq_c[:, :], bq).then_inc(consts_loaded, 16)
                for n, vec in enumerate((bk, bv, bo)):
                    sp.dma_start(bias[:, n, :], rows(vec)).then_inc(consts_loaded, 16)
                sp.dma_start(dec_r[:, :], rows(decay_row)).then_inc(consts_loaded, 16)
                sp.dma_start(dec_c[:, :], decay_col).then_inc(consts_loaded, 16)
                sp.wait_ge(ln_a.summed, ln_a.FROM + CT)
                load_x1(sp, 0, 1)

                def body(b, last):
                    for c in range(2):
                        sp.wait_ge(x2_biased, 2 * b + c + 1)
                        sp.dma_start(tiles(residual[2 * b + c]), chunk(x2, c)).then_inc(residual_stored[c], 16)
                    for c in range(2):
                        sp.wait_ge(residual_stored[c], 16 * b + 16)
                        sp.sem_inc(passed, 1)
                        sp.wait_ge(t_lo, 1 + 16 * b + 8 + 4 * c + 4)
                        sp.sem_inc(passed, 1)
                        sp.dma_start(chunk(ks, c), tiles(residual[2 * b + c])).then_inc(residual_loaded[c], 16)
                    for c in range(2):
                        sp.wait_ge(ln_b.normed, 8 * b + 4 * c + 4)
                        sp.dma_start(tiles(x3_dram[2 * b + c]), chunk(ks, c)).then_inc(x3_stored[c], 16)
                batches(sp, body)
                for c in range(2):
                    sp.wait_ge(x3_stored[c], 1 + 16 * BATCH)

            @block.gpsimd
            def _(pool):
                def build(n, ins):
                    ins.then_inc(built, 1)
                    pool.wait_ge(built, n)
                build(1, pool.memset(same_head[:, :], 0.0))
                for g in range(HPG):
                    build(2 + 2 * g, pool.memset(same_head[g * HD:(g + 1) * HD, g * HD:(g + 1) * HD], 1.0))
                    build(3 + 2 * g, pool.memset(same_head[g * HD:(g + 1) * HD, P + g:P + g + 1], 1.0))
                build(10, pool.memset(vs[:, :, :, P:P + 2], 1.0))
                ln_a.setup(pool)
                ln_b.setup(pool)
                pool.partition_all_reduce(quant[:, 0:1], y_max[:, :], P, bass.bass_isa.ReduceOp.max).then_inc(max_all, 1)
                for c in range(2):
                    split_lo(pool, n_w // 2 * c, n_w // 2 * (c + 1))
                    ln_a.pool_part(pool, c)
                pool.wait_ge(consts_loaded, 16 * 6)

                def body(b, last):
                    def add_bias(c):
                        pool.wait_ge(t_lo, 1 + 16 * b + 4 * c + 4)
                        part = chunk(x2, c)
                        pool.tensor_tensor(part, part, bias[:, 2:3, :].to_broadcast([P, CT, D]), ALU.add).then_inc(x2_biased, 1)

                    add_bias(0)
                    for c in range(2):
                        for g in range(GROUPS):
                            n = GROUPS * c + g
                            q = qT[:, g, c * CH:(c + 1) * CH]
                            pool.wait_ge(q_relu, 8 * b + n + 1)
                            pool.tensor_tensor(q, q, dec_r[:, c * CH:(c + 1) * CH], ALU.mult).then_inc(q_done, 1)
                        if c == 0:
                            add_bias(1)
                        for t in range(CT * c, CT * c + CT):
                            pool.wait_ge(k_biased, 8 * b + t + 1)
                            pool.sem_inc(ln_a.passed, 1)
                            pool.tensor_scalar(ks[:, t, :], ks[:, t, :], 0.0, dec_c[:, t:t + 1], ALU.max, ALU.mult).then_inc(k_done, 1)
                        if not last:
                            ln_a.pool_part(pool, 2 * b + 2 + c)
                    for c in range(2):
                        ln_b.pool_part(pool, 2 * b + c)
                batches(pool, body)

            @block.scalar
            def _(act):
                split_hi(act)
                act.wait_ge(consts_loaded, 16 * 6)

                def part_hi(b, c, entry):
                    for k in range(KT):
                        A.wait_full(act, b, entry(c, k))
                        act.activation(aT_hi[:, c, k, :], A.bank(entry(c, k)), ACT.Copy).then_inc(t_hi, 1)

                part_hi(0, 0, a_x)

                def body(b, last):
                    if not last:
                        act.wait_ge(ln_a.summed, ln_a.FROM + 8 * b + 8)
                        for c in range(2):
                            load_y(act, b + 1, c)
                        load_x1(act, b + 1, 0)
                    for c in range(2):
                        if c == 1:
                            part_hi(b, 1, a_x)
                        if c == 1 and not last:
                            act.wait_ge(ln_a.summed, ln_a.FROM + 8 * b + 12)
                            load_x1(act, b + 1, 1)
                        for g in range(GROUPS):
                            m = b_q(c, g)
                            B.wait_full(act, b, m)
                            act.activation(qT[:, g, c * CH:(c + 1) * CH], B.bank(m), ACT.Relu, bias=bq_c[:, g:g + 1]).then_inc(q_relu, 1)
                    for c in range(2):
                        part_hi(b, c, a_oT)
                    if not last:
                        part_hi(b + 1, 0, a_x)
                batches(act, body)

            @block.tensor
            def _(pe):
                def transposes(b, c, entry, src):
                    for k in range(KT):
                        m = entry(c, k)
                        free_a(b, m)
                        for t in range(CT):
                            mm = pe.transpose(A.bank(m)[:, tok(t)], src(t)[:, tok(k)], ident[:, :])
                        A.fill(mm, m)

                def free_a(b, m):
                    prev = m - 4
                    if prev < 0:
                        pe.wait_ge(t_lo, 1 + 16 * b)
                    elif prev < a_kv(0):
                        pe.wait_ge(t_lo, 1 + 16 * b + prev + 1)
                    elif prev < a_o(0, 0):
                        pe.wait_ge(kv_done, 4 * b + prev - a_kv(0) + 1)
                    elif prev < a_oT(0, 0):
                        pe.wait_ge(o_done, 16 * b + prev - a_o(0, 0) + 1)
                    else:
                        pe.wait_ge(t_lo, 1 + 16 * b + 8 + prev - a_oT(0, 0) + 1)

                def x2_transposes(b, c):
                    pe.wait_ge(ln_a.normed, 8 * b + 4 * c + 4)
                    transposes(b, c, a_x, lambda t: x2[:, CT * c + t, :])

                x2_transposes(0, 0)
                pe.wait_ge(w_done, n_w)

                def body(b, last):
                    def free_b(m):
                        prev = m - 4
                        if prev < 0:
                            pe.wait_ge(ln_b.summed, 8 * b + 4 + m + 1)
                        elif prev < b_out(0):
                            c, kind, n = prev // (3 * CT), prev % (3 * CT) // CT, prev % CT
                            pe.wait_ge((q_relu, k_biased, v_done)[kind], 8 * b + CT * c + n + 1)
                        else:
                            pe.wait_ge(ln_b.summed, ln_b.FROM + 8 * b + prev - b_out(0) + 1)

                    def product(c, n, a_cols, w_cols, a_is_lhs):
                        terms = []
                        for k in range(KT):
                            for a, w in ((aT_hi, w_hi), (aT_lo, w_hi), (aT_hi, w_lo)):
                                pair = (a[:, c, k, a_cols], w[:, n, k, w_cols])
                                terms.append(pair if a_is_lhs else pair[::-1])
                        return terms

                    everything = slice(0, D)
                    for c in range(2):
                        pe.wait_ge(t_lo, 1 + 16 * b + 4 * c + 4)
                        for g in range(GROUPS):
                            free_b(b_q(c, g))
                            B.fill(partials(pe, B.bank(b_q(c, g)), product(c, 0, everything, tok(g), False)), b_q(c, g))
                        if c == 0:
                            x2_transposes(b, 1)
                        for n, entry in ((1, b_k), (2, b_v)):
                            for t in range(CT):
                                free_b(entry(c, t))
                                B.fill(partials(pe, B.bank(entry(c, t)), product(c, n, tok(t), everything, True)), entry(c, t))
                    pe.wait_ge(k_done, 8 * b + 8)
                    pe.wait_ge(v_done, 8 * b + 8)
                    for g in range(GROUPS):
                        m = a_kv(g)
                        free_a(b, m)
                        A.fill(partials(pe, A.bank(m)[:, 0:P + 2], [(ks[:, t, tok(g)], vs[:, t, g, :]) for t in range(TT)]), m)
                    pe.wait_ge(q_done, 8 * b + 8)
                    for t in range(TT):
                        for half in range(2):
                            m = a_o(t, half)
                            free_a(b, m)
                            if t == 0:
                                pe.wait_ge(kv_done, 4 * b + 2 * half + 2)
                            for g in (2 * half, 2 * half + 1):
                                mm = pe.matmul(A.bank(m)[:, (g % 2) * EXT:(g % 2 + 1) * EXT], qT[:, g, tok(t)], kv[:, g, :],
                                               start=True, stop=True)
                            A.fill(mm, m)
                    for c in range(2):
                        pe.wait_ge(o_done, 16 * b + 8 * c + 8)
                        transposes(b, c, a_oT, lambda t: o_tok[:, CT * c + t, :])
                    for c in range(2):
                        pe.wait_ge(t_lo, 1 + 16 * b + 8 + 4 * c + 4)
                        for t in range(CT):
                            m = b_out(CT * c + t)
                            free_b(m)
                            B.fill(partials(pe, B.bank(m), product(c, 3, tok(t), everything, True)), m)
                        if c == 0 and not last:
                            x2_transposes(b + 1, 0)
                batches(pe, body)

            @block.vector
            def _(dve):
                dve.sem_inc(ln_a.summed, ln_a.FROM)
                dve.sem_inc(ln_b.summed, ln_b.FROM)
                dve.wait_ge(max_all, 1)
                dve.tensor_scalar(quant[:, 1:2], quant[:, 0:1], 1.0 / QMAX, FP4_EPS, ALU.mult, ALU.add).then_inc(quant_ready, 1)
                dve.wait_ge(quant_ready, 1)
                dve.reciprocal(quant[:, 2:3], quant[:, 1:2]).then_inc(quant_ready, 1)
                dve.wait_ge(quant_ready, 2)

                def quantize(b, c):
                    y = ys[:, c, :]
                    dve.wait_ge(y_loaded[c], 16 * b + 16)
                    dve.tensor_scalar(y, y, quant[:, 2:3], ROUND, ALU.mult, ALU.add).then_inc(rounding, 1)
                    dve.wait_ge(rounding, 6 * b + 3 * c + 1)
                    dve.tensor_scalar(y, y, -ROUND, QMAX, ALU.add, ALU.min).then_inc(rounding, 1)
                    dve.wait_ge(rounding, 6 * b + 3 * c + 2)
                    dve.tensor_scalar(y, y, -QMAX, quant[:, 1:2], ALU.max, ALU.mult).then_inc(rounding, 1)

                def add_x1(b, c, first=False):
                    dve.wait_ge(rounding, 6 * b + 3 * c + 3)
                    dve.wait_ge(x1_loaded, 32 * b + 16 * c + 16)
                    if not first:
                        dve.wait_ge(residual_stored[c], 16 * b)
                    for t in range(CT):
                        cols = slice(t * D, (t + 1) * D)
                        dve.tensor_tensor(x2[:, CT * c + t, :], ys[:, c, cols], x1[:, cols], ALU.add).then_inc(ln_a.summed, 1)

                x2_tile = lambda c: (lambda t: x2[:, CT * c + t, :])

                def part_lo(b, c, entry, first):
                    for k in range(KT):
                        dve.wait_ge(t_hi, 16 * b + first + KT * c + k + 1)
                        dve.tensor_tensor(aT_lo[:, c, k, :], A.bank(entry(c, k)), f32(aT_hi[:, c, k, :]), ALU.subtract).then_inc(t_lo, 1)

                for c in range(2):
                    quantize(0, c)
                    add_x1(0, c, True)
                    ln_a.vector_part(dve, c, x2_tile(c), x2_tile(c))
                    if c == 0:
                        part_lo(0, 0, a_x, 0)
                dve.wait_ge(built, 10)
                dve.wait_ge(consts_loaded, 16 * 6)

                def body(b, last):
                    def keys(c):
                        dve.wait_ge(x3_stored[c], 1 + 16 * b)
                        for t in range(CT):
                            B.wait_full(dve, b, b_k(c, t))
                            dve.tensor_tensor(ks[:, CT * c + t, :], B.bank(b_k(c, t)), bias[:, 0, :], ALU.add).then_inc(k_biased, 1)

                    def values(c):
                        for t in range(CT):
                            B.wait_full(dve, b, b_v(c, t))
                            heads = lambda ap: ap.rearrange("p (g e) -> p g e", g=GROUPS)
                            dve.tensor_tensor(vs[:, CT * c + t, :, 0:P], heads(B.bank(b_v(c, t))), heads(bias[:, 1, :]), ALU.add).then_inc(v_done, 1)

                    if not last:
                        quantize(b + 1, 0)
                    part_lo(b, 1, a_x, 0)
                    for c in range(2):
                        keys(c)
                        if not last:
                            add_x1(b + 1, c)
                        values(c)
                        if not last:
                            ln_a.find_statistics(dve, 2 * b + 2 + c, x2_tile(c))
                        if c == 0 and not last:
                            ln_a.normalize_tiles(dve, 2 * b + 2, x2_tile(0), x2_tile(0))
                            quantize(b + 1, 1)
                    for g in range(GROUPS):
                        bank = A.bank(a_kv(g))
                        A.wait_full(dve, b, a_kv(g))
                        dve.tensor_tensor(kv[:, g, 0:P], bank[:, 0:P], same_head[:, 0:P], ALU.mult)
                        dve.tensor_scalar(kv[:, g, P:EXT], same_head[:, P:EXT], bank[:, P:P + 1], None, ALU.mult).then_inc(kv_done, 1)
                    for t in range(TT):
                        halves = [A.bank(a_o(t, half))[:, 0:2 * EXT].rearrange("p (g e) -> p g e", g=2) for half in range(2)]
                        slot = lambda ap: ap[:, t % 2, :]
                        for half in range(2):
                            A.wait_full(dve, b, a_o(t, half))
                            dve.tensor_scalar(slot(den)[:, half * 2 * HPG:(half + 1) * 2 * HPG].rearrange("p (g h) -> p g h", g=2),
                                              halves[half][:, :, P:EXT], LIN_EPS, None, ALU.add).then_inc(den_eps, 1)
                        dve.wait_ge(den_eps, 16 * b + 2 * t + 2)
                        dve.reciprocal(slot(rden), slot(den)).then_inc(den_inv, 1)
                        dve.wait_ge(den_inv, 8 * b + t + 1)
                        for half in range(2):
                            for g in range(2):
                                at = (2 * half + g) * P
                                heads = lambda ap: ap.rearrange("p (h e) -> p h e", h=HPG)
                                inv = slot(rden)[:, (2 * half + g) * HPG:(2 * half + g + 1) * HPG]
                                ins = dve.tensor_tensor(heads(o_tok[:, t, at:at + P]), heads(halves[half][:, g, 0:P]),
                                                        inv[:, :, None].to_broadcast([P, HPG, HD]), ALU.mult)
                            ins.then_inc(o_done, 1)
                    for c in range(2):
                        part_lo(b, c, a_oT, 8)
                    if not last:
                        ln_a.normalize_tiles(dve, 2 * b + 3, x2_tile(1), x2_tile(1))
                    for c in range(2):
                        dve.wait_ge(residual_loaded[c], 16 * b + 16)
                        for t in range(CT):
                            m = b_out(CT * c + t)
                            at = ks[:, CT * c + t, :]
                            B.wait_full(dve, b, m)
                            dve.tensor_tensor(at, B.bank(m), at, ALU.add).then_inc(ln_b.summed, 1)
                        x3_tile = lambda t: ks[:, CT * c + t, :]
                        ln_b.vector_part(dve, 2 * b + c, x3_tile, x3_tile)
                        if c == 0 and not last:
                            part_lo(b + 1, 0, a_x, 0)
                batches(dve, body)


def phase_ffn1(nc, psum, w0, b0, w1, b1, x3_dram, out):
    with Phase(nc) as ctx:
        sb = lambda n, s, d: ctx.enter_context(nc.sbuf_tensor(n, s, d))
        sem = ctx.semaphore
        w0_hi = sb("p6_w0_hi", [P, KT, HID], F32R)
        w0_lo = sb("p6_w0_lo", [P, KT, HID], F32R)
        w1_hi = sb("p6_w1_hi", [P, HT, D], F32R)
        w1_lo = sb("p6_w1_lo", [P, HT, D], F32R)
        stage = sb("p6_stage", [P, 4, D * CT // 2], F32)
        x3 = sb("p6_x3", [P, 2, CT * D], F32)
        x16 = sb("p6_x16", [P, CT, D], F16)
        xT = sb("p6_xT", [P, 2, KT, CH], F32R)
        h16 = sb("p6_h16", [P, 2, CH], F16)
        h = sb("p6_h", [P, 2, CH], F32R)
        e16 = sb("p6_e16", [P, CT, D], F16)
        res = sb("p6_out", [P, CT, D], F32)
        ident16 = sb("p6_ident16", [P, P], F16)
        b0c = sb("p6_b0", [P, HT], F32)
        b1r = sb("p6_b1", [P, D], F32)
        half = HID // 2
        jobs = [(w0[k * P:(k + 1) * P, n:n + half], w0_hi[:, k, n:n + half], w0_lo[:, k, n:n + half]) for k in range(KT) for n in (0, half)]
        n_w0 = len(jobs)
        w1_v = w1.rearrange("(t p) n -> p t n", p=P)
        flat = lambda ap: ap.rearrange("p t n -> p (t n)")
        for q in range(0, HT, 2):
            jobs.append((w1_v[:, q:q + 2, :], flat(w1_hi[:, q:q + 2, :]), flat(w1_lo[:, q:q + 2, :])))
        load_w, split_hi, split_lo, w_done, n_w = split_loader(nc, ctx, "p6_w", stage[:, :, :], jobs)
        ln = LayerNorm(nc, ctx, "p6_ln")
        Y = Banks(nc, ctx, "p6_ybank", psum, 0, CT, 2 * CT)
        H = Banks(nc, ctx, "p6_hbank", psum, 4, 2, 2 * HT)
        T = Banks(nc, ctx, "p6_tbank", psum, 6, 2, 2 * KT)
        built, bias_loaded = sem("p6_built"), sem("p6_bias_loaded")
        x_loaded = [sem(f"p6_x_loaded{c}") for c in range(2)]
        x_cast, h_done, h_used = sem("p6_x_cast"), sem("p6_h_done", 2), sem("p6_h_used", 1)
        stored = sem("p6_stored", 1)

        with nc.Block() as block:
            @block.sync
            def _(sp):
                tiles = lambda ap: ap.rearrange("(t p) d -> p t d", p=P)

                def load_x(b, c):
                    sp.dma_start(x3[:, c, :].rearrange("p (t d) -> p t d", t=CT), tiles(x3_dram[2 * b + c])).then_inc(x_loaded[c], 16)

                load_x(0, 0)
                load_w(sp)
                sp.dma_start(b0c[:, :], b0).then_inc(bias_loaded, 16)
                sp.dma_start(b1r[:, :], rows(b1)).then_inc(bias_loaded, 16)
                load_x(0, 1)

                def body(b, last):
                    for c in range(2):
                        sp.wait_ge(ln.summed, ln.FROM + 8 * b + 4 * c + 4)
                        if not last:
                            load_x(b + 1, c)
                        sp.wait_ge(ln.normed, 8 * b + 4 * c + 4)
                        sp.dma_start(tiles(out[2 * b + c]), res[:, :, :]).then_inc(stored, 16)
                batches(sp, body)
                sp.wait_ge(stored, 1 + 16 * NCH)

            @block.gpsimd
            def _(pool):
                pool.memset(ident16[:, :], 0.0).then_inc(built, 1)
                pool.wait_ge(built, 1)
                pool.affine_select(out=ident16[:, :], in_=ident16[:, :], compare_op=ALU.not_equal, fill=1.0, base=0,
                                   pattern=[[-1, P]], channel_multiplier=1).then_inc(built, 1)
                pool.wait_ge(built, 2)
                ln.setup(pool)
                with pool.Fori(0, BATCH) as b:
                    for c in range(2):
                        ln.pool_part(pool, 2 * b + c)

            @block.scalar
            def _(act):
                def x_T(b, c):
                    for k in range(KT):
                        m = KT * c + k
                        T.wait_full(act, b, m)
                        T.free(act.activation(xT[:, c, k, :], T.bank(m).bitcast(F16)[:, 0:CH], ACT.Copy), m)

                x_T(0, 0)
                split_hi(act)
                act.preload_act_table(ACT.Gelu)
                act.wait_ge(bias_loaded, 32)

                def body(b, last):
                    for c in range(2):
                        for t in range(HT):
                            m = HT * c + t
                            H.wait_full(act, b, m)
                            act.wait_ge(h_done, 2 * HT * b + m + 1)
                            H.free(act.activation(h16[:, t % 2, :], H.bank(m), ACT.Gelu, bias=b0c[:, t:t + 1]), m)
                            if t == HT // 2 and not (c and last):
                                x_T(b + c, 1 - c)
                batches(act, body)

            @block.tensor
            def _(pe):
                pe.wait_ge(built, 2)

                def transposes(b, c):
                    pe.wait_ge(x_cast, 2 * b + c + 1)
                    for k in range(KT):
                        m = KT * c + k
                        T.wait_free(pe, b, m)
                        for t in range(CT):
                            mm = pe.transpose(T.bank(m).bitcast(F16)[:, t * P:(t + 1) * P], x16[:, t, k * P:(k + 1) * P], ident16[:, :])
                        T.fill(mm, m)

                transposes(0, 0)
                pe.wait_ge(w_done, n_w0)

                def body(b, last):
                    def to_y(c, t):
                        pe.wait_ge(h_done, 2 + 2 * HT * b + HT * c + t + 1)
                        pe.wait_ge(w_done, n_w0 + t // 2 + 1)
                        for a in range(CT):
                            m = CT * c + a
                            if t == 0:
                                Y.wait_free(pe, b, m)
                            for part, w in enumerate((w1_hi, w1_lo)):
                                mm = pe.matmul(Y.bank(m), h[:, t % 2, a * P:(a + 1) * P], w[:, t, :], start=(t == 0 and part == 0),
                                               stop=(t == HT - 1 and part == 1))
                            if t == HT - 1:
                                Y.fill(mm, m)
                        if t < HT - 1:
                            mm.then_inc(h_used, 1)

                    for c in range(2):
                        for k in range(2):
                            T.wait_freed(pe, k, 4 * b + 2 * c + 2)
                        for t in range(HT + 1):
                            if t < HT:
                                m = HT * c + t
                                H.wait_free(pe, b, m)
                                H.fill(partials(pe, H.bank(m), [
                                    (w[:, k, t * P:(t + 1) * P], xT[:, c, k, :]) for k in range(KT) for w in (w0_hi, w0_lo)]), m)
                            if t > 0:
                                to_y(c, t - 1)
                            if t == HT // 2 and not (c and last):
                                transposes(b + c, 1 - c)
                batches(pe, body)

            @block.vector
            def _(dve):
                dve.sem_inc(ln.summed, ln.FROM)

                def cast(b, c):
                    dve.wait_ge(x_loaded[c], 16 * b + 16)
                    for k in range(2):
                        T.wait_filled(dve, k, 4 * b + 2 * c)
                    dve.tensor_copy(x16[:, :, :].rearrange("p t d -> p (t d)"), x3[:, c, :]).then_inc(x_cast, 1)

                cast(0, 0)
                split_lo(dve)
                dve.wait_ge(bias_loaded, 32)

                def body(b, last):
                    for c in range(2):
                        for t in range(HT):
                            m = HT * c + t
                            H.wait_freed(dve, m % 2, HT * b + m // 2 + 1)
                            if t == 1:
                                Y.wait_filled(dve, CT - 1, 2 * b + c)
                            else:
                                dve.wait_ge(h_used, 1 + (HT - 1) * (2 * b + c) + max(0, t - 1))
                            dve.tensor_copy(h[:, t % 2, :], h16[:, t % 2, :]).then_inc(h_done, 1)
                            if t == HT // 2 - 1 and not (c and last):
                                cast(b + c, 1 - c)
                        for a in range(CT):
                            m = CT * c + a
                            Y.wait_full(dve, b, m)
                            Y.free(dve.tensor_tensor(e16[:, a, :], Y.bank(m), b1r[:, :], ALU.add), m)
                        dve.wait_ge(stored, 1 + 32 * b + 16 * c)
                        for a in range(CT):
                            Y.wait_freed(dve, a, 2 * b + c + 1)
                            dve.tensor_tensor(res[:, a, :], x3[:, c, a * D:(a + 1) * D], e16[:, a, :], ALU.add).then_inc(ln.summed, 1)
                        ln.vector_part(dve, 2 * b + c, lambda t: res[:, t, :], lambda t: res[:, t, :])
                batches(dve, body)


def build_program(nc, x, l0_wq, l0_wk, l0_wv, l0_wo, l0_bo, f0_w1, f0_b1, f0_w2, f0_b2,
                  l1_wq, l1_bq, l1_wk, l1_bk, l1_wv, l1_bv, l1_wo, l1_bo, f1_w0, f1_b0, f1_w1, f1_b1,
                  decay_row, decay_col, out):
    groups = BATCH * GROUPS
    q_dram = nc.dram_tensor("q_parts", [groups, 2, P, SEQ], F32)
    k_dram = nc.dram_tensor("k_parts", [groups, 2, P, SEQ], F32)
    v_dram = nc.dram_tensor("v_rows", [groups, SEQ, P], F32)
    o_dram = nc.dram_tensor("attention_out", [groups, P, SEQ], F32)
    x1_dram = nc.dram_tensor("x1", [NCH, CH, D], F32)
    y_dram = nc.dram_tensor("ffn0_out", [NCH, CH, D], F32)
    residual = nc.dram_tensor("residual", [NCH, CH, D], F32)
    x3_dram = nc.dram_tensor("x3", [NCH, CH, D], F32)
    with Phase(nc) as ctx:
        psum = ctx.enter_context(nc.psum_tensor("psum", [P, 8, CH], F32))
        y_max = ctx.enter_context(nc.sbuf_tensor("y_max", [P, 1], F32))
        ident = build_constants(nc, ctx)
        with ExitStack() as layer0:
            sb = lambda n, s, d: layer0.enter_context(nc.sbuf_tensor(n, s, d))
            w_max = sb("w_max", [P, 2], F32)
            ffn_w = (f0_w1, f0_w2)
            phase_qkv0(nc, psum, ident, x, l0_wq, l0_wk, l0_wv, q_dram, k_dram, v_dram, ffn_w, w_max)
            tern = sb("tern", [P, 2, KT * HID], F32R)
            kept = sb("kept", [P, 2, 8, KT * HID // 64], F32)
            alpha = sb("alpha", [P, 2], F32)
            phase_attention(nc, psum, ident, q_dram, k_dram, v_dram, o_dram, ffn_w, w_max, tern, kept)
            phase_out0(nc, psum, x, l0_wo, l0_bo, o_dram, x1_dram, tern, kept, alpha)
            phase_ffn0(nc, psum, ident, tern, alpha, f0_b1, f0_b2, x1_dram, y_dram, y_max)
        phase_linear_attention(nc, psum, ident, y_max, y_dram, x1_dram, l1_wq, l1_wk, l1_wv, l1_wo,
                               l1_bq, l1_bk, l1_bv, l1_bo, decay_row, decay_col, residual, x3_dram)
        phase_ffn1(nc, psum, f1_w0, f1_b0, f1_w1, f1_b1, x3_dram, out.rearrange("b (c t) d -> (b c) t d", c=2))


def kernel(**inputs):
    import concourse.bacc as bacc
    from concourse.bass_utils import run_bass_kernel_spmd

    i = {k: np.ascontiguousarray(v) for k, v in inputs.items()}
    by_partition = lambda v: np.ascontiguousarray(v.reshape(-1, P).T)
    transposed = lambda w: np.ascontiguousarray(w.T)
    decay = np.exp(-np.arange(SEQ, dtype=np.float32) / np.float32(SEQ)).astype(np.float32)
    arrays = {
        "x": i["L0_attn_x"], "l0_wq": i["L0_attn_wq"], "l0_wk": i["L0_attn_wk"], "l0_wv": i["L0_attn_wv"],
        "l0_wo": i["L0_attn_wo"], "l0_bo": i["L0_attn_bo"],
        "f0_w1": transposed(i["L0_ffn_W1"]), "f0_b1": by_partition(i["L0_ffn_b1"]),
        "f0_w2": transposed(i["L0_ffn_W2"]), "f0_b2": i["L0_ffn_b2"],
        "l1_wq": transposed(i["L1_attn_Wq"]), "l1_bq": by_partition(i["L1_attn_bq"]),
        "l1_wk": transposed(i["L1_attn_Wk"]), "l1_bk": i["L1_attn_bk"],
        "l1_wv": transposed(i["L1_attn_Wv"]), "l1_bv": i["L1_attn_bv"],
        "l1_wo": transposed(i["L1_attn_Wo"]), "l1_bo": i["L1_attn_bo"],
        "f1_w0": transposed(i["L1_ffn_W0"]), "f1_b0": by_partition(i["L1_ffn_bias0"]),
        "f1_w1": transposed(i["L1_ffn_W1"]), "f1_b1": i["L1_ffn_bias1"],
        "decay_row": decay, "decay_col": by_partition(decay),
    }
    nc = bacc.Bacc("TRN2", target_bir_lowering=False, num_devices=1)
    args = [nc.dram_tensor(f"in_{n}", a.shape, mybir.dt.from_np(a.dtype), kind="ExternalInput").ap() for n, a in arrays.items()]
    out = nc.dram_tensor("out", (BATCH, SEQ, D), F32, kind="ExternalOutput").ap()
    build_program(nc, *args, out)
    result = run_bass_kernel_spmd(nc, [{f"in_{n}": a for n, a in arrays.items()}], core_ids=[0])
    return result.results[0]["out"]
```

```python
from contextlib import ExitStack

import numpy as np

import concourse.bass as bass
from concourse import mybir

F32 = mybir.dt.float32
F32R = mybir.dt.float32r
F16 = mybir.dt.float16
ALU = mybir.AluOpType
ACT = mybir.ActivationFunctionType
AX = mybir.AxisListType

P = 128
BATCH, SEQ, D, HID = 4, 1024, 512, 2048
HEADS = 16
HD = D // HEADS
KT = D // P
HT = HID // P
CH = 512
NCH = BATCH * SEQ // CH
CT = CH // P
GROUPS = D // P
HPG = P // HD
SM_SCALE = 1.0 / float(np.sqrt(np.float32(HD)))
LN_EPS = 1e-5
FP4_EPS = 1e-8
QMAX = 7.0
LIN_EPS = 1e-6
TERN = 0.05
ROUND = 12582912.0
FLOOR = -3.0e38


class Phase(ExitStack):

    def __init__(self, nc):
        super().__init__()
        self.nc, self.semaphores = nc, []

    def semaphore(self, name, start=0):
        handle = self.nc.alloc_semaphore(name=name)
        self.semaphores.append(handle)
        if start:
            self.nc.gpsimd.sem_inc(handle, start)
        return handle

    def __exit__(self, *exc):
        self.nc.clear_and_free_semaphores(self.semaphores)
        self.nc.all_engine_barrier()
        return super().__exit__(*exc)


def f32(ap):
    return ap.bitcast(F32)


def split_loader(nc, ctx, name, stage, jobs):
    slots = stage.shape[1]
    loaded = [ctx.semaphore(f"{name}_loaded{k}") for k in range(slots)]
    hi_done = ctx.semaphore(f"{name}_hi")
    lo_done = ctx.semaphore(f"{name}_lo")

    def load(sp, first=0, last=len(jobs)):
        for n, (src, _, _) in list(enumerate(jobs))[first:last]:
            if n >= slots:
                sp.wait_ge(lo_done, n - slots + 1)
            sp.dma_start(stage[:, n % slots, :], src).then_inc(loaded[n % slots], 16)

    def split_hi(act):
        for n, (_, hi, _) in enumerate(jobs):
            act.wait_ge(loaded[n % slots], 16 * (n // slots + 1))
            act.activation(hi, stage[:, n % slots, :], ACT.Copy).then_inc(hi_done, 1)

    def split_lo(dve, first=0, last=len(jobs)):
        for n, (_, hi, lo) in list(enumerate(jobs))[first:last]:
            dve.wait_ge(hi_done, n + 1)
            dve.tensor_tensor(lo, stage[:, n % slots, :], f32(hi), ALU.subtract).then_inc(lo_done, 1)

    return load, split_hi, split_lo, lo_done, len(jobs)


def batches(eng, body):
    with eng.Fori(0, BATCH - 1) as b:
        body(b, False)
    body(BATCH - 1, True)


def halves(w, hi, lo):
    flat = lambda ap: ap.rearrange("p k n -> p (k n)")
    view = w.rearrange("(k p) n -> p k n", p=P)
    return [(view[:, k:k + KT // 2, :], flat(hi[:, k:k + KT // 2, :]), flat(lo[:, k:k + KT // 2, :])) for k in (0, KT // 2)]


def build_constants(nc, ctx):
    ident = ctx.enter_context(nc.sbuf_tensor("ident", [P, P], F32))
    zeroed = ctx.semaphore("ident_zeroed")
    with nc.Block() as block:
        @block.gpsimd
        def _(pool):
            pool.memset(ident[:, :], 0.0).then_inc(zeroed, 1)
            pool.wait_ge(zeroed, 1)
            pool.affine_select(out=ident[:, :], in_=ident[:, :], compare_op=ALU.not_equal, fill=1.0,
                               base=0, pattern=[[-1, P]], channel_multiplier=1).then_inc(zeroed, 1)
            pool.wait_ge(zeroed, 2)
    return ident


def phase_qkv0(nc, psum, ident, x, wq, wk, wv, q_dram, k_dram, v_dram, ffn_w, w_max):
    OUTS = 2 * GROUPS + CT
    with Phase(nc) as ctx:
        sb = lambda n, s, d: ctx.enter_context(nc.sbuf_tensor(n, s, d))
        sem = ctx.semaphore
        stage = sb("p1_stage", [P, 4, KT * D // 2], F32)
        w_hi = sb("p1_w_hi", [P, 3, KT, D], F32R)
        w_lo = sb("p1_w_lo", [P, 3, KT, D], F32R)
        xs = sb("p1_x", [P, CT, D], F32)
        xT_hi = sb("p1_xT_hi", [P, 2, KT, CH], F32R)
        xT_lo = sb("p1_xT_lo", [P, 2, KT, CH], F32R)
        qk_out = sb("p1_qk_out", [P, 4, 2, CH], F32R)
        v_out = sb("p1_v_out", [P, CT, D], F32)
        raw = sb("p1_raw", [P, 2, KT * D], F32)
        piece_max = sb("p1_piece_max", [P, 2, BATCH], F32)
        jobs = [job for n, w in enumerate((wq, wk, wv)) for job in halves(w, w_hi[:, n, :, :], w_lo[:, n, :, :])]
        stage_v = stage[:, :, :]
        load_w, split_hi, split_lo, w_done, n_w = split_loader(nc, ctx, "p1_w", stage_v, jobs)
        x_loaded = sem("p1_x_loaded")
        xt_ready = sem("p1_xt_ready", 1)
        xt_hi = sem("p1_xt_hi")
        xt_lo = sem("p1_xt_lo")
        proj = sem("p1_proj")
        qk_hi = sem("p1_qk_hi")
        qk_lo = sem("p1_qk_lo")
        v_copied = sem("p1_v_copied")
        qk_stored = [sem(f"p1_qk_stored{k}", 1) for k in range(4)]
        v_stored = [sem(f"p1_v_stored{t}", 1) for t in range(CT)]
        raw_loaded = [sem(f"p1_raw_loaded{n}") for n in range(2)]
        passed = sem("p1_passed")
        piece_done = sem("p1_piece_done", 2)
        x_v = x.rearrange("b (c t p) d -> b c p t d", c=2, p=P)
        raw_v = [w.rearrange("(q k p) n -> q p k n", q=BATCH, p=P) for w in ffn_w]

        with nc.Block() as block:
            @block.gpsimd
            def _(pool):
                def load_x(b, c):
                    pool.dma_start(xs[:, :, :], x_v[b, c]).then_inc(x_loaded, 16)

                load_x(0, 0)

                def body(b, last):
                    for c in range(2):
                        pool.wait_ge(piece_done, 2 * b + c + 1)
                        pool.sem_inc(passed, 1)
                        n = raw_v[c].shape[2]
                        pool.dma_start(raw[:, c, :].rearrange("p (k n) -> p k n", k=n), raw_v[c][b]).then_inc(raw_loaded[c], 16)
                        if not (c and last):
                            pool.wait_ge(xt_ready, 1 + 8 * b + 4 * c + 4)
                            pool.sem_inc(passed, 1)
                            load_x(b + c, 1 - c)
                batches(pool, body)

            @block.sync
            def _(sp):
                load_w(sp)
                with sp.Fori(0, BATCH) as b:
                    for c in range(2):
                        for j in range(2 * GROUPS):
                            dst = (q_dram, k_dram)[j % 2]
                            dst_v = dst[bass.ds(4 * b + j // 2, 1), :, :, c * CH:(c + 1) * CH].rearrange("o s p t -> p (o s) t")
                            sp.wait_ge(qk_lo, 8 + 16 * b + 8 * c + j + 1)
                            sp.dma_start(dst_v, f32(qk_out[:, j % 4, :, :])).then_inc(qk_stored[j % 4], 16)
                        for t in range(CT):
                            r0 = c * CH + t * P
                            dst_v = v_dram[bass.ds(4 * b, 4), r0:r0 + P, :].rearrange("g p e -> p g e")
                            sp.wait_ge(v_copied, 4 + 8 * b + 4 * c + t + 1)
                            sp.dma_start(dst_v, v_out[:, t, :].rearrange("p (g e) -> p g e", g=GROUPS)).then_inc(v_stored[t], 16)
                for k in range(4):
                    sp.wait_ge(qk_stored[k], 1 + 16 * 4 * BATCH)
                for t in range(CT):
                    sp.wait_ge(v_stored[t], 1 + 16 * 2 * BATCH)

            @block.tensor
            def _(pe):
                pe.sem_inc(proj, 2 * OUTS)

                def transposes(b, c, k):
                    pe.wait_ge(x_loaded, 32 * b + 16 * c + 16)
                    pe.wait_ge(xt_lo, 8 * b + 4 * c + k + 1)
                    for t in range(CT):
                        mm = pe.transpose(psum[:, k % 2, t * P:(t + 1) * P], xs[:, t, k * P:(k + 1) * P], ident[:, :])
                    mm.then_inc(xt_ready, 1)

                for k in range(KT):
                    transposes(0, 0, k)

                def body(b, last):
                    for c in range(2):
                        pe.wait_ge(xt_lo, 2 + 8 * b + 4 * c + 4)
                        for o in range(OUTS):
                            pe.wait_ge(w_done, n_w if o >= 2 * GROUPS else 2 * (o % 2) + 2)
                            if o < 2:
                                pe.wait_ge(qk_lo, 16 * b + 8 * c + 7 + o)
                            elif o < 6:
                                pe.wait_ge(v_copied, 8 * b + 4 * c + o - 1)
                            else:
                                pe.wait_ge(qk_lo, 8 + 16 * b + 8 * c + o - 5)
                            bank = psum[:, 2 + o % 6, :]
                            n = 0
                            for kt in range(KT):
                                for part in range(3):
                                    xp = (xT_hi, xT_lo, xT_hi)[part]
                                    wp = (w_hi, w_hi, w_lo)[part]
                                    if o < 2 * GROUPS:
                                        g = o // 2
                                        lhsT, rhs = wp[:, o % 2, kt, g * P:(g + 1) * P], xp[:, c, kt, :]
                                    else:
                                        t = o - 2 * GROUPS
                                        lhsT, rhs = xp[:, c, kt, t * P:(t + 1) * P], wp[:, 2, kt, :]
                                    mm = pe.matmul(bank, lhsT, rhs, start=(n == 0), stop=(n == 3 * KT - 1))
                                    n += 1
                            mm.then_inc(proj, 1)
                            if 4 <= o < 4 + KT and not (c and last):
                                transposes(b + c, 1 - c, o - 4)
                batches(pe, body)

            @block.scalar
            def _(act):
                act.sem_inc(v_copied, 4)

                def x_hi(b, c, k):
                    act.wait_ge(xt_ready, 1 + 8 * b + 4 * c + k + 1)
                    act.activation(xT_hi[:, c, k, :], psum[:, k % 2, :], ACT.Copy).then_inc(xt_hi, 1)

                for k in range(KT):
                    x_hi(0, 0, k)
                split_hi(act)

                def body(b, last):
                    for c in range(2):
                        for o in range(OUTS):
                            bank = psum[:, 2 + o % 6, :]
                            act.wait_ge(proj, 2 * OUTS + 24 * b + 12 * c + o + 1)
                            if o < 2 * GROUPS:
                                act.wait_ge(qk_stored[o % 4], 1 + 64 * b + 32 * c + 16 * (o // 4))
                                act.activation(qk_out[:, o % 4, 0, :], bank, ACT.Copy).then_inc(qk_hi, 1)
                            else:
                                t = o - 2 * GROUPS
                                act.wait_ge(v_stored[t], 1 + 32 * b + 16 * c)
                                act.activation(v_out[:, t, :], bank, ACT.Copy).then_inc(v_copied, 1)
                            if 4 <= o < 4 + KT and not (c and last):
                                x_hi(b + c, 1 - c, o - 4)
                batches(act, body)

            @block.vector
            def _(dve):
                dve.sem_inc(xt_lo, 2)
                dve.sem_inc(qk_lo, 8)

                def x_lo(b, c, k):
                    dve.wait_ge(xt_hi, 8 * b + 4 * c + k + 1)
                    dve.tensor_tensor(xT_lo[:, c, k, :], psum[:, k % 2, :], f32(xT_hi[:, c, k, :]),
                                      ALU.subtract).then_inc(xt_lo, 1)

                for k in range(KT):
                    x_lo(0, 0, k)
                split_lo(dve)

                def body(b, last):
                    for c in range(2):
                        for j in range(2 * GROUPS):
                            dve.wait_ge(qk_hi, 16 * b + 8 * c + j + 1)
                            dve.tensor_tensor(qk_out[:, j % 4, 1, :], psum[:, 2 + j % 6, :], f32(qk_out[:, j % 4, 0, :]),
                                              ALU.subtract).then_inc(qk_lo, 1)
                            if 4 <= j < 4 + KT and not (c and last):
                                x_lo(b + c, 1 - c, j - 4)
                        dve.wait_ge(raw_loaded[c], 16 * b + 16)
                        dve.tensor_reduce(piece_max[:, c, bass.ds(b, 1)], raw[:, c, :], AX.X, ALU.max,
                                          apply_absolute_value=True).then_inc(piece_done, 1)
                batches(dve, body)
                dve.wait_ge(piece_done, 2 + 2 * BATCH)
                dve.tensor_reduce(w_max[:, :], piece_max[:, :, :], AX.X, ALU.max).then_inc(piece_done, 1)


def phase_attention(nc, psum, ident, q_dram, k_dram, v_dram, o_dram, ffn_w, w_max, tern, kept):
    NU = BATCH * GROUPS
    DOWN = SEQ // P
    PER_UNIT = HPG * CT
    S_PER_GROUP = 2 * (PER_UNIT + 1)
    STEPS = [CT, 2 * CT]
    ST_PER_GROUP = HPG * sum(STEPS)
    J_PER_GROUP = sum(STEPS)
    KEY_STEPS = [(0, j) for j in range(STEPS[0])] + [(1, j) for j in range(STEPS[1])]
    LOADS = 6 * 16
    with Phase(nc) as ctx:
        sb = lambda n, s, d: ctx.enter_context(nc.sbuf_tensor(n, s, d))
        sem = ctx.semaphore
        kst = [sb(f"p2_kst{s}", [P, HPG, SEQ], F32R) for s in range(2)]
        qst = [sb(f"p2_qst{s}", [P, HPG, SEQ], F32R) for s in range(2)]
        vs = [sb(f"p2_v{s}", [P, DOWN, P], F32) for s in range(2)]
        probs = sb("p2_probs", [P, 2, HPG, CH], F32)
        junk = sb("p2_junk", [P, 2, SEQ], F32)
        rowmax = sb("p2_rowmax", [P, 2, PER_UNIT], F32)
        negmax = sb("p2_negmax", [P, 2, 2, PER_UNIT], F32R)
        causal = sb("p2_causal", [P, SEQ], F32)
        pick = sb("p2_pick", [2 * PER_UNIT, PER_UNIT], F32)
        ones = sb("p2_ones", [P, HD], F32)
        o_raw = sb("p2_o_raw", [P, 2, CH], F32)
        recip = sb("p2_recip", [P, CH], F32)
        o_out = sb("p2_o_out", [P, 2, CH], F32)

        TW = tern.shape[2] // (NU // 2)
        KEPT = kept.shape[3]
        raw = sb("p2_raw", [P, 2, TW], F32)
        below = sb("p2_below", [P, 2, TW], F32)
        above = sb("p2_above", [P, 2, TW], F32)
        bound = sb("p2_bound", [P, 2, 3], F32)
        raw_loaded = [sem(f"p2_raw_loaded{n}") for n in range(2)]
        bound_done = sem("p2_bound_done")
        tern_step = sem("p2_tern_step")
        TERN_STEPS = 7
        raw_v = [ffn_w[0].rearrange("(k p) n -> p k n", p=P), ffn_w[1].rearrange("(k p) n -> p k n", p=P)]
        n_rows = [v.shape[1] for v in raw_v]

        def eighth(ap, n, i):
            if n == 0:
                return ap[:, :, bass.ds(TW // KT * i, TW // KT)]
            return ap[:, bass.ds(TW // D * i, TW // D), :]

        const_done = sem("p2_const_done")
        MASKS, CONSTS = 5, 8
        loaded = [[sem(f"p2_loaded{s}_{c}") for c in range(2)] for s in range(2)]
        v_loaded = [sem(f"p2_v_loaded{s}") for s in range(2)]
        s_ready = sem("p2_s_ready")
        s_used = sem("p2_s_used")
        rm_done = sem("p2_rm_done")
        nm_ready = sem("p2_nm_ready")
        st_ready = sem("p2_st_ready")
        p_ready = sem("p2_p_ready")
        p_masked = sem("p2_p_masked")
        pv_done = sem("p2_pv_done")
        rec_done = sem("p2_rec_done")
        o_read = sem("p2_o_read")
        o_normed = sem("p2_o_normed", 1)
        passed = sem("p2_passed")
        o_stored = [sem(f"p2_o_stored{c}", 1) for c in range(2)]

        SHORT = [(0, e // HPG, e % HPG) for e in range(PER_UNIT)]
        LONG = [(1, CT - 1 - e // HPG, e % HPG) for e in range(PER_UNIT)]
        LEAD = 9
        ENTRIES = SHORT[:LEAD] + [e for pair in zip(SHORT[LEAD:], LONG) for e in pair] + LONG[PER_UNIT - LEAD:]
        LAST = [ENTRIES.index(SHORT[-1]), S_PER_GROUP - 2]
        ENTRIES.insert(LAST[0] + 4, (0, None, None))
        ENTRIES.append((1, None, None))
        FIRST = [0, ENTRIES.index(LONG[0])]
        BUILT = [ENTRIES.index((c, None, None)) + 1 for c in range(2)]
        NORM0 = 4 * (STEPS[0] + 1)
        QUARTER = list(range(NORM0 - 11, NORM0)) + list(range(NORM0 + 4, 4 * J_PER_GROUP - 2)) + [4 * J_PER_GROUP - 1]
        assert len(QUARTER) == S_PER_GROUP
        BESIDE_C0 = sum(q < NORM0 for q in QUARTER)

        S_BANKS = [psum[:, 0:2, :].rearrange("p a n -> p (a n)"), psum[:, 2:4, :].rearrange("p a n -> p (a n)")]
        ST_BANKS = [psum[:, 4, :], psum[:, 5, :]]
        O_BANK, SUM_BANK = psum[:, 6, :], psum[:, 7, :]

        def half(eng, body):
            with eng.Fori(0, NU // 2 - 1) as i:
                body(i, False)
            body(NU // 2 - 1, True)

        with nc.Block() as block:
            @block.gpsimd
            def _(pool):
                def build(n, ins):
                    ins.then_inc(const_done, 1)
                    pool.wait_ge(const_done, n)
                build(1, pool.memset(causal[:, :], 0.0))
                tri = causal[:, SEQ - P:SEQ]
                build(2, pool.affine_select(out=tri, in_=tri, compare_op=ALU.is_ge, fill=FLOOR, base=0,
                                            pattern=[[-1, P]], channel_multiplier=1))
                build(3, pool.memset(pick[:, :], 0.0))
                for k in range(2):
                    build(4 + k, pool.affine_select(out=pick[:, :], in_=pick[:, :], compare_op=ALU.not_equal, fill=1.0,
                                                    base=-PER_UNIT * k, pattern=[[-1, PER_UNIT]], channel_multiplier=1))
                build(6, pool.memset(ones[:, :], 1.0))
                for s in range(2):
                    build(7 + s, pool.memset(f32(kst[s][96:128, :, :]), 1.0))
                for n in range(2):
                    build(9 + n, pool.partition_all_reduce(bound[:, n, 0:1], w_max[:, n:n + 1], P, bass.bass_isa.ReduceOp.max))
                build(11, pool.tensor_scalar(bound[:, :, 1], bound[:, :, 0], TERN, None, ALU.mult))
                build(12, pool.tensor_scalar(bound[:, :, 2], bound[:, :, 1], -1.0, None, ALU.mult))
                tiles = lambda ap, n: ap.rearrange("p (k n) -> p k n", k=(KT, TW // D)[n])

                def load_raw(i, n):
                    pool.dma_start(tiles(raw[:, n, :], n), eighth(raw_v[n], n, i)).then_inc(raw_loaded[n], 16)

                def ternarize(i, n, last):
                    w, out = raw[:, n, :], eighth(tern[:, n, :].rearrange("p (k n) -> p k n", k=n_rows[n]), n, i)
                    before = TERN_STEPS * (2 * i + n)
                    pool.wait_ge(raw_loaded[n], 16 * i + 16)
                    pool.sem_inc(passed, 1)
                    pool.tensor_scalar(below[:, n, :], w, bound[:, n, 2:3], None, ALU.is_lt).then_inc(tern_step, 1)
                    pool.tensor_scalar(above[:, n, :], w, bound[:, n, 1:2], None, ALU.is_gt).then_inc(tern_step, 1)
                    pool.wait_ge(tern_step, before + 2)
                    pool.sem_inc(passed, 1)
                    pool.tensor_tensor(out, tiles(above[:, n, :], n), tiles(below[:, n, :], n), ALU.subtract).then_inc(tern_step, 1)
                    pool.wait_ge(tern_step, before + 3)
                    pool.sem_inc(passed, 1)
                    pool.tensor_tensor(tiles(below[:, n, :], n), tiles(w, n), f32(out), ALU.mult).then_inc(tern_step, 1)
                    pool.wait_ge(tern_step, before + 4)
                    if not last:
                        pool.sem_inc(passed, 1)
                        load_raw(i + 1, n)
                    half = TW // 2
                    for fold in range(3):
                        dst = below[:, n, 0:half] if half > KEPT else kept[:, n, bass.ds(i, 1), :].rearrange("p o k -> p (o k)")
                        pool.sem_inc(passed, 1)
                        pool.tensor_tensor(dst, below[:, n, 0:half], below[:, n, half:2 * half], ALU.add).then_inc(tern_step, 1)
                        pool.wait_ge(tern_step, before + 5 + fold)
                        half //= 2

                for n in range(2):
                    load_raw(0, n)

                def body(i, last):
                    for s in range(2):
                        for step, (c, j) in enumerate(KEY_STEPS):
                            if (c, j) == (1, 0):
                                ternarize(i, s, last)
                            for g in range(HPG):
                                if j >= CT * c:
                                    at = ST_PER_GROUP * s + HPG * step + g + 1
                                    q0 = P * j - CH * c
                                    blk = probs[:, step % 2, g, q0:q0 + P]
                                    pool.wait_ge(p_ready, 2 + 2 * ST_PER_GROUP * i + at)
                                    pool.sem_inc(passed, 1)
                                    pool.affine_select(out=blk, in_=blk, compare_op=ALU.is_ge, fill=0.0, base=0,
                                                       pattern=[[1, P]], channel_multiplier=-1).then_inc(p_masked, 1)
                half(pool, body)

            @block.sync
            def _(sp):
                def load(u, s, k):
                    for c in range(2):
                        cols = slice(c * CH, (c + 1) * CH)
                        for dst, src, rows in ((qst, q_dram, (0, 0, 1)), (kst, k_dram, (0, 1, 0))):
                            for r, part in enumerate(rows):
                                view = src[u, part].rearrange("(h d) t -> d h t", d=HD)[:, :, cols]
                                sp.dma_start(f32(dst[s][r * HD:(r + 1) * HD, :, cols]), view).then_inc(loaded[s][c], 16)
                    sp.dma_start(vs[s][:, :, :], v_dram[u].rearrange("(t p) e -> p t e", p=P)).then_inc(v_loaded[s], 16)

                def store(u, c, n):
                    sp.wait_ge(o_normed, 1 + n + 1)
                    sp.dma_start(o_dram[u, :, c * CH:(c + 1) * CH], o_out[:, c, :]).then_inc(o_stored[c], 16)

                load(0, 0, 0)
                load(1, 1, 0)

                def body(i, last):
                    for s in range(2):
                        store(2 * i + s, 0, 4 * i + 2 * s)
                        if not last:
                            sp.wait_ge(pv_done, 2 + J_PER_GROUP * (2 * i + s + 1))
                            load(2 * i + 2 + s, s, i + 1)
                        store(2 * i + s, 1, 4 * i + 2 * s + 1)
                half(sp, body)
                for c in range(2):
                    sp.wait_ge(o_stored[c], 1 + 16 * NU)

            @block.tensor
            def _(pe):
                def score_entry(u, s, m):
                    c, tile, g = ENTRIES[m]
                    bank = S_BANKS[m % 2]
                    pe.wait_ge(s_used, S_PER_GROUP * u + m + 1)
                    if tile is None:
                        pe.wait_ge(nm_ready, 2 * u + c + 1)
                        pe.transpose(bank[0:2 * PER_UNIT, 0:P], f32(negmax[:, c, :, :]).rearrange("p a n -> p (a n)"),
                                     ident[:, :]).then_inc(s_ready, 1)
                        return
                    t = CT * c + tile
                    n = P * (t + 1)
                    for k0 in range(0, n, CH):
                        k1 = min(n, k0 + CH)
                        mm = pe.matmul(bank[:, k0:k1], qst[s][0:96, g, t * P:(t + 1) * P],
                                       kst[s][0:96, g, k0:k1], start=True, stop=True)
                    mm.then_inc(s_ready, 1)

                def scores_T(u, s, c, j, st):
                    q0, g = max(0, P * j - CH * c), st % HPG
                    pe.wait_ge(p_ready, ST_PER_GROUP * u + st + 1)
                    if j == 0 and g == 0:
                        pe.wait_ge(s_used, 2 + S_PER_GROUP * u + BUILT[c])
                    pe.matmul(ST_BANKS[st % 2][:, q0:CH], kst[s][:, g, j * P:(j + 1) * P],
                              qst[s][:, g, c * CH + q0:(c + 1) * CH], start=True, stop=True).then_inc(st_ready, 1)

                def with_v(u, s, c, j, step, use_ones):
                    q0 = max(0, P * j - CH * c)
                    if not use_ones:
                        if (c, j) == (0, 0):
                            pe.wait_ge(v_loaded[s], 8 * u + 16 - 8 * s)
                        if j == 0:
                            pe.wait_ge(o_read, 2 * u + c + 1)
                        pe.wait_ge(p_ready, 2 + ST_PER_GROUP * u + HPG * (step + 1))
                        if j >= CT * c:
                            pe.wait_ge(p_masked, PER_UNIT * (2 * u + c) + HPG * (j - CT * c + 1))
                    bank = SUM_BANK if use_ones else O_BANK
                    for g in range(HPG):
                        lhsT = ones[:, :] if use_ones else vs[s][:, j, g * HD:(g + 1) * HD]
                        mm = pe.matmul(bank[g * HD:(g + 1) * HD, q0:CH], lhsT, probs[:, step % 2, g, q0:CH],
                                       start=(j == 0), stop=(j == STEPS[c] - 1))
                    if use_ones:
                        mm.then_inc(pv_done, 1)

                def second_pass(i, last):
                    before = None
                    for s in range(2):
                        u = 2 * i + s
                        entries = [] if last and s == 1 else list(range(S_PER_GROUP))
                        for step, (c, j) in enumerate(KEY_STEPS):
                            for quarter in range(4):
                                if quarter % 2 == 0:
                                    scores_T(u, s, c, j, HPG * step + quarter)
                                    scores_T(u, s, c, j, HPG * step + quarter + 1)
                                elif before:
                                    with_v(*before, use_ones=(quarter == 3))
                                if entries and QUARTER[entries[0]] == 4 * step + quarter:
                                    if entries[0] in FIRST:
                                        pe.wait_ge(loaded[1 - s][FIRST.index(entries[0])], LOADS * (i + 1 + s))
                                    score_entry(u + 1, 1 - s, entries.pop(0))
                            before = (u, s, c, j, step)
                    with_v(*before, use_ones=False)
                    with_v(*before, use_ones=True)

                pe.sem_inc(pv_done, 2)
                for m in range(S_PER_GROUP):
                    if m in FIRST:
                        pe.wait_ge(loaded[0][FIRST.index(m)], LOADS)
                    score_entry(0, 0, m)
                pe.wait_ge(const_done, CONSTS)

                half(pe, second_pass)

            @block.scalar
            def _(act):
                act.sem_inc(p_ready, 2)
                act.sem_inc(o_read, 1)

                def evacuate(u, c):
                    act.wait_ge(pv_done, 2 + J_PER_GROUP * u + sum(STEPS[:c + 1]))
                    act.wait_ge(o_normed, 1 + 2 * u + c)
                    act.activation(o_raw[:, 0, :], O_BANK, ACT.Copy)
                    act.activation(o_raw[:, 1, :], SUM_BANK, ACT.Copy).then_inc(o_read, 1)

                def body(i, last):
                    before = None
                    for s in range(2):
                        u = 2 * i + s
                        for step, (c, j) in enumerate(KEY_STEPS):
                            q0 = max(0, P * j - CH * c)
                            act.wait_ge(pv_done, J_PER_GROUP * u + step + 1)
                            for g in range(HPG):
                                st = HPG * step + g
                                act.wait_ge(st_ready, ST_PER_GROUP * u + st + 1)
                                act.activation(probs[:, step % 2, g, q0:CH], ST_BANKS[st % 2][:, q0:CH], ACT.Exp,
                                               scale=SM_SCALE).then_inc(p_ready, 1)
                            if j == 0 and before:
                                evacuate(*before)
                            before = (u, c)
                    evacuate(*before)
                half(act, body)

            @block.vector
            def _(dve):
                dve.sem_inc(s_used, 2)
                dve.wait_ge(const_done, MASKS)

                def maximum(u, s, m):
                    c, tile, g = ENTRIES[m]
                    base = S_PER_GROUP * u
                    dve.wait_ge(s_ready, base + m + 1)
                    dve.wait_ge(s_used, base + m + 1)
                    dve.sem_inc(passed, 1)
                    if tile is not None:
                        n = P * (CT * c + tile + 1)
                        col = g * CT + tile
                        dve.tensor_tensor_reduce(junk[:, m % 2, 0:n], S_BANKS[m % 2][:, 0:n], causal[:, SEQ - n:SEQ], 1.0, FLOOR,
                                                 ALU.add, ALU.max, rowmax[:, c, col:col + 1]).then_inc(s_used, 1)
                        if m in LAST:
                            dve.wait_ge(s_used, 2 + base + m + 1)
                            dve.tensor_scalar(negmax[:, c, 0, :], rowmax[:, c, :], -1.0, None, ALU.mult).then_inc(rm_done, 1)
                            dve.wait_ge(rm_done, 2 * u + c + 1)
                            dve.scalar_tensor_tensor(out=negmax[:, c, 1, :], in0=rowmax[:, c, :], scalar=-1.0,
                                                     in1=f32(negmax[:, c, 0, :]), op0=ALU.mult, op1=ALU.subtract).then_inc(nm_ready, 1)
                        return
                    rows = [2 * PER_UNIT, HPG, CT, P]
                    dve.tensor_tensor(
                        qst[s][96:128, :, c * CH:(c + 1) * CH].rearrange("p g (t q) -> p g t q", q=P),
                        S_BANKS[m % 2][0:2 * PER_UNIT, 0:P][:, None, None, :].to_broadcast(rows),
                        pick[:, :].rearrange("p (g t) -> p g t", g=HPG)[:, :, :, None].to_broadcast(rows),
                        ALU.mult).then_inc(s_used, 1)

                def normalize(u, c):
                    dve.wait_ge(o_read, 1 + 2 * u + c + 1)
                    dve.wait_ge(o_stored[c], 1 + 16 * u)
                    dve.reciprocal(recip[:, :], o_raw[:, 1, :]).then_inc(rec_done, 1)
                    dve.wait_ge(rec_done, 2 * u + c + 1)
                    dve.tensor_tensor(o_out[:, c, :], o_raw[:, 0, :], recip[:, :], ALU.mult).then_inc(o_normed, 1)

                for m in range(S_PER_GROUP):
                    maximum(0, 0, m)

                def body(i, last):
                    for s in range(2):
                        u = 2 * i + s
                        if not (last and s == 1):
                            for m in range(BESIDE_C0):
                                maximum(u + 1, 1 - s, m)
                        normalize(u, 0)
                        if not (last and s == 1):
                            for m in range(BESIDE_C0, S_PER_GROUP):
                                maximum(u + 1, 1 - s, m)
                        normalize(u, 1)
                half(dve, body)


class Banks:

    def __init__(self, nc, ctx, name, psum, first, size, per_iter):
        assert per_iter % size == 0
        self.psum, self.first, self.size, self.turns = psum, first, size, per_iter // size
        self.filled = [ctx.semaphore(f"{name}_filled{k}", 1) for k in range(size)]
        self.freed = [ctx.semaphore(f"{name}_freed{k}", 1) for k in range(size)]

    def bank(self, m):
        return self.psum[:, self.first + m % self.size, :]

    def wait_free(self, pe, it, m):
        self.wait_freed(pe, m % self.size, it * self.turns + m // self.size)

    def wait_full(self, eng, it, m):
        self.wait_filled(eng, m % self.size, it * self.turns + m // self.size + 1)

    def wait_filled(self, eng, bank, n):
        eng.wait_ge(self.filled[bank], 1 + n)

    def wait_freed(self, eng, bank, n):
        eng.wait_ge(self.freed[bank], 1 + n)

    def fill(self, ins, m):
        return ins.then_inc(self.filled[m % self.size], 1)

    def free(self, ins, m):
        return ins.then_inc(self.freed[m % self.size], 1)


def partials(pe, bank, terms):
    for n, (lhsT, rhs) in enumerate(terms):
        mm = pe.matmul(bank, lhsT, rhs, start=(n == 0), stop=(n == len(terms) - 1))
    return mm


class LayerNorm:
    FROM = 2 * CT

    def __init__(self, nc, ctx, name):
        sem = lambda k: ctx.semaphore(f"{name}_{k}")
        self.stats = ctx.enter_context(nc.sbuf_tensor(f"{name}_stats", [P, CT, 6], F32))
        self.meanvar = ctx.enter_context(nc.sbuf_tensor(f"{name}_meanvar", [P, CT, 2], F32))
        self.vareps = ctx.enter_context(nc.sbuf_tensor(f"{name}_vareps", [P, CT], F32))
        self.rstd = ctx.enter_context(nc.sbuf_tensor(f"{name}_rstd", [P, CT], F32))
        self.power = ctx.enter_context(nc.sbuf_tensor(f"{name}_power", [P, CT], F32))
        self.summed, self.got_stats, self.got_mean = sem("summed"), sem("got_stats"), sem("got_mean")
        self.passed = sem("passed")
        self.ready, self.eps_added, self.got_rstd, self.normed = sem("ready"), sem("eps_added"), sem("got_rstd"), sem("normed")

    def setup(self, pool):
        pool.memset(self.power[:, :], -0.5).then_inc(self.ready, 1)
        pool.wait_ge(self.ready, 1)

    def pool_part(self, pool, n):
        pool.wait_ge(self.got_mean, n * CT + CT)
        pool.sem_inc(self.passed, 1)
        pool.tensor_scalar(self.vareps[:, :], self.meanvar[:, :, 1], LN_EPS, None, ALU.add).then_inc(self.eps_added, 1)
        pool.wait_ge(self.eps_added, n + 1)
        pool.tensor_tensor(self.rstd[:, :], self.vareps[:, :], self.power[:, :], ALU.pow).then_inc(self.got_rstd, 1)

    def vector_part(self, dve, n, src, dst):
        self.find_statistics(dve, n, src)
        self.normalize_tiles(dve, n, src, dst)

    def find_statistics(self, dve, n, src):
        for t in range(CT):
            dve.wait_ge(self.summed, self.FROM + n * CT + t + 1)
            dve.bn_stats(self.stats[:, t, :], src(t)).then_inc(self.got_stats, 1)
        dve.wait_ge(self.got_stats, n * CT + CT)
        dve.sem_inc(self.passed, 1)
        for t in range(CT):
            dve.bn_aggr(self.meanvar[:, t, :], self.stats[:, t, :]).then_inc(self.got_mean, 1)

    def normalize_tiles(self, dve, n, src, dst):
        dve.wait_ge(self.got_rstd, n + 1)
        for t in range(CT):
            dve.tensor_scalar(dst(t), src(t), self.meanvar[:, t, 0:1], self.rstd[:, t:t + 1],
                              ALU.subtract, ALU.mult).then_inc(self.normed, 1)


def rows(vec):
    return vec.rearrange("(o n) -> o n", o=1).to_broadcast([P, vec.shape[0]])


def phase_out0(nc, psum, x, wo, bo, o_dram, x1_dram, tern, kept, alpha, next_x1):
    NT = tern.shape[2]
    PIECES = 4
    with Phase(nc) as ctx:
        sb = lambda n, s, d: ctx.enter_context(nc.sbuf_tensor(n, s, d))
        sem = ctx.semaphore
        stage = sb("p3_stage", [P, 2, KT * D // 2], F32)
        w_hi = sb("p3_w_hi", [P, KT, D], F32R)
        w_lo = sb("p3_w_lo", [P, KT, D], F32R)
        o_in = sb("p3_o", [P, 2, GROUPS, CH], F32)
        o_hi = sb("p3_o_hi", [P, 2, GROUPS, CH], F32R)
        o_lo = sb("p3_o_lo", [P, 2, GROUPS, CH], F32R)
        xs = sb("p3_x", [P, 2, CT, D], F32)
        x1 = sb("p3_x1", [P, 2, CT, D], F32)
        bias = sb("p3_bias", [P, D], F32)
        squares = sb("p3_squares", [P, NT // PIECES], F16)
        counts = sb("p3_counts", [P, 2, PIECES], F32)
        totals = sb("p3_totals", [P, 4], F32)
        totals_all = sb("p3_totals_all", [P, 4], F32)
        per_count = sb("p3_per_count", [P, 2], F32)
        load_w, split_hi, split_lo, w_done, n_w = split_loader(nc, ctx, "p3_w", stage[:, :, :], halves(wo, w_hi[:, :, :], w_lo[:, :, :]))
        ln = LayerNorm(nc, ctx, "p3_ln")
        banks = Banks(nc, ctx, "p3_bank", psum, 0, 8, 2 * CT)
        bias_loaded, next_loaded = sem("p3_bias_loaded"), sem("p3_next_loaded")
        o_loaded = [sem(f"p3_o_loaded{c}") for c in range(2)]
        x_loaded = [sem(f"p3_x_loaded{c}") for c in range(2)]
        o_hi_done, o_lo_done = sem("p3_o_hi_done"), sem("p3_o_lo_done")
        x_biased = sem("p3_x_biased")
        stored = [sem(f"p3_stored{c}", 1) for c in range(2)]
        counted, reduced, alpha_step = sem("p3_counted"), sem("p3_reduced"), sem("p3_alpha_step")
        x_v = x.rearrange("b (c t p) d -> b c p t d", c=2, p=P)

        def load_o(eng, b, c):
            src = o_dram[bass.ds(4 * b, GROUPS), :, c * CH:(c + 1) * CH].rearrange("g p t -> p g t")
            eng.dma_start(o_in[:, c, :, :], src).then_inc(o_loaded[c], 16)

        with nc.Block() as block:
            @block.sync
            def _(sp):
                load_w(sp)
                sp.wait_ge(o_loaded[0], 16)
                sp.dma_start(bias[:, :], rows(bo)).then_inc(bias_loaded, 16)
                for c in range(2):
                    sp.dma_start(xs[:, c, :, :], x_v[0, c]).then_inc(x_loaded[c], 16)

                def body(b, last):
                    for c in range(2):
                        if not last:
                            sp.wait_ge(ln.summed, ln.FROM + 8 * b + 4 * c + 4)
                            sp.dma_start(xs[:, c, :, :], x_v[b + 1, c]).then_inc(x_loaded[c], 16)
                        elif c == 0:
                            sp.wait_ge(stored[0], 1 + 16 * b)
                            sp.dma_start(next_x1[:, :, :], x1_dram[0].rearrange("(t p) d -> p t d", p=P)).then_inc(next_loaded, 16)
                        sp.wait_ge(ln.normed, 8 * b + 4 * c + 4)
                        sp.dma_start(x1_dram[2 * b + c].rearrange("(t p) d -> p t d", p=P), x1[:, c, :, :]).then_inc(stored[c], 16)
                batches(sp, body)
                sp.wait_ge(next_loaded, 16)
                for c in range(2):
                    sp.wait_ge(stored[c], 1 + 16 * BATCH)

            @block.gpsimd
            def _(pool):
                ln.setup(pool)
                pool.wait_ge(bias_loaded, 16)

                def add_bias(b, c):
                    pool.wait_ge(x_loaded[c], 16 * b + 16)
                    pool.tensor_tensor(xs[:, c, :, :], xs[:, c, :, :], bias[:, None, :].to_broadcast([P, CT, D]), ALU.add).then_inc(x_biased, 1)

                for c in range(2):
                    add_bias(0, c)

                def body(b, last):
                    for c in range(2):
                        ln.pool_part(pool, 2 * b + c)
                        if not last:
                            add_bias(b + 1, c)
                batches(pool, body)
                pool.wait_ge(counted, 2 * PIECES + 2)
                pool.partition_all_reduce(totals_all[:, :], totals[:, :], P, bass.bass_isa.ReduceOp.add).then_inc(reduced, 1)

            @block.scalar
            def _(act):
                load_o(act, 0, 0)
                split_hi(act)
                load_o(act, 0, 1)

                def body(b, last):
                    for c in range(2):
                        act.wait_ge(o_loaded[c], 16 * b + 16)
                        banks.wait_filled(act, CT * c + CT - 1, b)
                        act.activation(o_hi[:, c, :, :], o_in[:, c, :, :], ACT.Copy).then_inc(o_hi_done, 1)
                        if not last:
                            act.wait_ge(o_lo_done, 2 * b + c + 1)
                            load_o(act, b + 1, c)
                batches(act, body)

            @block.tensor
            def _(pe):
                pe.wait_ge(w_done, n_w)

                def body(b, last):
                    for c in range(2):
                        pe.wait_ge(o_lo_done, 2 * b + c + 1)
                        for t in range(CT):
                            m = CT * c + t
                            tok = slice(t * P, (t + 1) * P)
                            pe.wait_ge(ln.summed, 8 * b + m + 1)
                            banks.fill(partials(pe, banks.bank(m), [
                                (o[:, c, k, tok], w[:, k, :]) for k in range(KT)
                                for o, w in ((o_hi, w_hi), (o_lo, w_hi), (o_hi, w_lo))]), m)
                batches(pe, body)

            @block.vector
            def _(dve):
                def count(n):
                    for q in range(PIECES):
                        part = f32(tern[:, n, q * NT // PIECES:(q + 1) * NT // PIECES])
                        if n + q > 0:
                            dve.wait_ge(counted, PIECES * n + q)
                        dve.tensor_tensor_reduce(squares[:, :], part, part, 1.0, 0.0, ALU.mult, ALU.add,
                                                 counts[:, n, q:q + 1]).then_inc(counted, 1)

                def o_split(b, c):
                    dve.wait_ge(o_hi_done, 2 * b + c + 1)
                    dve.tensor_tensor(o_lo[:, c, :, :], o_in[:, c, :, :], f32(o_hi[:, c, :, :]), ALU.subtract).then_inc(o_lo_done, 1)

                dve.sem_inc(ln.summed, ln.FROM)
                count(0)
                split_lo(dve)
                o_split(0, 0)
                count(1)
                o_split(0, 1)
                dve.wait_ge(counted, 2 * PIECES)
                dve.tensor_reduce(totals[:, 0:2], kept[:, :, :, :].rearrange("p n i k -> p n (i k)"), AX.X, ALU.add).then_inc(counted, 1)
                dve.tensor_reduce(totals[:, 2:4], counts[:, :, :], AX.X, ALU.add).then_inc(counted, 1)

                def body(b, last):
                    for c in range(2):
                        dve.wait_ge(x_biased, 2 * b + c + 1)
                        dve.wait_ge(stored[c], 1 + 16 * b)
                        for t in range(CT):
                            m = CT * c + t
                            banks.wait_full(dve, b, m)
                            dve.tensor_tensor(x1[:, c, t, :], banks.bank(m), xs[:, c, t, :], ALU.add).then_inc(ln.summed, 1)
                        tile = lambda t: x1[:, c, t, :]
                        ln.find_statistics(dve, 2 * b + c, tile)
                        if not last:
                            o_split(b + 1, c)
                        ln.normalize_tiles(dve, 2 * b + c, tile, tile)
                batches(dve, body)
                dve.wait_ge(reduced, 1)
                dve.tensor_scalar(totals_all[:, 2:4], totals_all[:, 2:4], 1.0, None, ALU.max).then_inc(alpha_step, 1)
                dve.wait_ge(alpha_step, 1)
                dve.reciprocal(per_count[:, :], totals_all[:, 2:4]).then_inc(alpha_step, 1)
                dve.wait_ge(alpha_step, 2)
                dve.tensor_tensor(alpha[:, :], totals_all[:, 0:2], per_count[:, :], ALU.mult).then_inc(alpha_step, 1)


def phase_ffn0(nc, psum, ident, tern, alpha, b1, b2, x1, x1_dram, y_dram, y_max):
    with Phase(nc) as ctx:
        sb = lambda n, s, d: ctx.enter_context(nc.sbuf_tensor(n, s, d))
        sem = ctx.semaphore
        tern1 = tern[:, 0, :].rearrange("p (k n) -> p k n", k=KT)
        tern2 = tern[:, 1, :].rearrange("p (k n) -> p k n", k=HT)
        b1c = sb("p4_b1", [P, HT], F32)
        b2r = sb("p4_b2", [P, D], F32)
        xT_hi = sb("p4_xT_hi", [P, 2, KT, CH], F32R)
        xT_lo = sb("p4_xT_lo", [P, 2, KT, CH], F32R)
        h = sb("p4_h", [P, 2, CH], F32)
        h_hi = sb("p4_h_hi", [P, 2, CH], F32R)
        h_lo = sb("p4_h_lo", [P, 2, CH], F32R)
        ys = sb("p4_y", [P, CT, D], F32)
        y_abs = sb("p4_y_abs", [P, CT + 2], F32)

        Y = Banks(nc, ctx, "p4_ybank", psum, 0, CT, 2 * CT)
        H = Banks(nc, ctx, "p4_hbank", psum, 4, 2, 2 * HT)
        T = Banks(nc, ctx, "p4_tbank", psum, 6, 2, 2 * KT)
        passed = sem("p4_passed")
        bias_loaded, x_loaded, cleared = sem("p4_bias_loaded"), sem("p4_x_loaded", 16), sem("p4_cleared")
        xt_hi, xt_lo = sem("p4_xt_hi"), sem("p4_xt_lo")
        hh_done, hl_done = sem("p4_h_hi_done"), sem("p4_h_lo_done", 2)
        h_used = sem("p4_h_used", 1)
        y_done, y_maxed, run_max = sem("p4_y_done"), sem("p4_y_maxed"), sem("p4_run_max")
        y_stored = sem("p4_y_stored", 1)

        with nc.Block() as block:
            @block.sync
            def _(sp):
                sp.dma_start(b1c[:, :], b1).then_inc(bias_loaded, 16)
                sp.dma_start(b2r[:, :], rows(b2)).then_inc(bias_loaded, 16)

                def load_x(b, c):
                    for k in range(2):
                        T.wait_filled(sp, k, 4 * b + 2 * c)
                    sp.dma_start(x1[:, :, :], x1_dram[2 * b + c].rearrange("(t p) d -> p t d", p=P)).then_inc(x_loaded, 16)

                def body(b, last):
                    load_x(b, 1)
                    if not last:
                        load_x(b + 1, 0)
                    for c in range(2):
                        sp.wait_ge(y_maxed, 8 * b + 4 * c + 4)
                        sp.dma_start(y_dram[2 * b + c].rearrange("(t p) d -> p t d", p=P), ys[:, :, :]).then_inc(y_stored, 16)
                batches(sp, body)
                sp.wait_ge(y_stored, 1 + 16 * NCH)

            @block.gpsimd
            def _(pool):
                def body(b, last):
                    for m in range(2 * HT):
                        pool.wait_ge(hh_done, 2 * HT * b + m + 1)
                        pool.tensor_tensor(h_lo[:, m % 2, :], h[:, m % 2, :], f32(h_hi[:, m % 2, :]), ALU.subtract).then_inc(hl_done, 1)
                batches(pool, body)

            @block.scalar
            def _(act):
                act.preload_act_table(ACT.Gelu)
                act.wait_ge(bias_loaded, 32)

                def x_hi(b, c, k):
                    T.wait_full(act, b, KT * c + k)
                    act.activation(xT_hi[:, c, k, :], T.bank(KT * c + k), ACT.Copy).then_inc(xt_hi, 1)

                for k in range(KT):
                    x_hi(0, 0, k)

                def body(b, last):
                    for c in range(2):
                        for t in range(HT):
                            m = HT * c + t
                            H.wait_full(act, b, m)
                            act.wait_ge(hl_done, 2 * HT * b + m + 1)
                            H.free(act.activation(h[:, t % 2, :], H.bank(m), ACT.Gelu, bias=b1c[:, t:t + 1], scale=alpha[:, 0:1]), m)
                            if t == 1:
                                Y.wait_filled(act, CT - 1, 2 * b + c)
                            else:
                                act.wait_ge(h_used, 1 + (HT - 1) * (2 * b + c) + max(0, t - 1))
                            act.sem_inc(passed, 1)
                            H.wait_freed(act, m % 2, HT * b + m // 2 + 1)
                            act.activation(h_hi[:, t % 2, :], h[:, t % 2, :], ACT.Copy).then_inc(hh_done, 1)
                            if HT // 2 < t <= HT // 2 + KT and not (c and last):
                                x_hi(b + c, 1 - c, t - HT // 2 - 1)
                batches(act, body)

            @block.tensor
            def _(pe):
                def transposes(b, c, k):
                    pe.wait_ge(x_loaded, 32 * b + 16 * c + 16)
                    m = KT * c + k
                    pe.wait_ge(xt_lo, 8 * b + m + 1)
                    for t in range(CT):
                        mm = pe.transpose(T.bank(m)[:, t * P:(t + 1) * P], x1[:, t, k * P:(k + 1) * P], ident[:, :])
                    T.fill(mm, m)

                def hidden(b, c, t):
                    if t == 0:
                        pe.wait_ge(xt_lo, 2 + 8 * b + 4 * c + 4)
                    m = HT * c + t
                    H.wait_free(pe, b, m)
                    H.fill(partials(pe, H.bank(m), [
                        (tern1[:, k, t * P:(t + 1) * P], xp[:, c, k, :]) for k in range(KT) for xp in (xT_hi, xT_lo)]), m)

                for k in range(KT):
                    transposes(0, 0, k)
                hidden(0, 0, 0)

                def body(b, last):
                    def to_y(c, t):
                        pe.wait_ge(hl_done, 2 + 2 * HT * b + HT * c + t + 1)
                        for a in range(CT):
                            m = CT * c + a
                            if t == 0:
                                Y.wait_free(pe, b, m)
                            tok = slice(a * P, (a + 1) * P)
                            for part, src in enumerate((h_hi, h_lo)):
                                mm = pe.matmul(Y.bank(m), src[:, t % 2, tok], tern2[:, t, :], start=(t == 0 and part == 0),
                                               stop=(t == HT - 1 and part == 1))
                            if t == HT - 1:
                                Y.fill(mm, m)
                        if t < HT - 1:
                            mm.then_inc(h_used, 1)

                    for c in range(2):
                        for t in range(HT):
                            if t < HT - 1:
                                hidden(b, c, t + 1)
                            elif not (c and last):
                                hidden(b + c, 1 - c, 0)
                            to_y(c, t)
                            if HT // 2 <= t < HT // 2 + KT and not (c and last):
                                transposes(b + c, 1 - c, t - HT // 2)
                batches(pe, body)

            @block.vector
            def _(dve):
                dve.memset(y_abs[:, :], 0.0).then_inc(cleared, 1)
                dve.wait_ge(cleared, 1)
                dve.sem_inc(xt_lo, 2)
                dve.wait_ge(bias_loaded, 32)

                def x_lo(b, c, k):
                    m = KT * c + k
                    dve.wait_ge(xt_hi, 8 * b + m + 1)
                    dve.tensor_tensor(xT_lo[:, c, k, :], T.bank(m), f32(xT_hi[:, c, k, :]), ALU.subtract).then_inc(xt_lo, 1)

                for k in range(KT):
                    x_lo(0, 0, k)

                def body(b, last):
                    for c in range(2):
                        if not (c and last):
                            for k in range(KT):
                                x_lo(b + c, 1 - c, k)
                        dve.wait_ge(y_stored, 1 + 32 * b + 16 * c)
                        for a in range(CT):
                            m = CT * c + a
                            Y.wait_full(dve, b, m)
                            Y.free(dve.scalar_tensor_tensor(out=ys[:, a, :], in0=Y.bank(m), scalar=alpha[:, 1:2], in1=b2r[:, :],
                                                            op0=ALU.mult, op1=ALU.add), m)
                        for a in range(CT):
                            m = CT * c + a
                            Y.wait_freed(dve, a, 2 * b + c + 1)
                            dve.tensor_reduce(y_abs[:, a:a + 1], ys[:, a, :], AX.X, ALU.max, apply_absolute_value=True).then_inc(y_maxed, 1)
                        dve.wait_ge(y_maxed, 8 * b + 4 * c + 4)
                        dve.tensor_reduce(y_abs[:, CT + c:CT + c + 1], y_abs[:, :], AX.X, ALU.max).then_inc(run_max, 1)
                        dve.wait_ge(run_max, 2 * b + c + 1)
                batches(dve, body)
                dve.tensor_copy(y_max[:, :], y_abs[:, CT + 1:CT + 2]).then_inc(run_max, 1)


def phase_linear_attention(nc, psum, ident, y_max, y_dram, x1_dram, wq, wk, wv, wo, bq, bk, bv, bo, decay_row, decay_col, residual, x3_dram, next_x3):
    TT = SEQ // P
    EXT = P + HPG
    with Phase(nc) as ctx:
        sb = lambda n, s, d: ctx.enter_context(nc.sbuf_tensor(n, s, d))
        sem = ctx.semaphore
        w_hi = sb("p5_w_hi", [P, 4, KT, D], F32R)
        w_lo = sb("p5_w_lo", [P, 4, KT, D], F32R)
        ys = sb("p5_y", [P, 2, CT * D], F32)
        x1 = sb("p5_x1", [P, CT * D], F32)
        x2 = sb("p5_x2", [P, TT, D], F32)
        aT_hi = sb("p5_aT_hi", [P, 2, KT, CH], F32R)
        aT_lo = sb("p5_aT_lo", [P, 2, KT, CH], F32R)
        qT = sb("p5_qT", [P, GROUPS, SEQ], F32)
        ks = sb("p5_k", [P, TT, D], F32)
        vs = sb("p5_v", [P, TT, GROUPS, P + 2], F32)
        kv = sb("p5_kv", [P, GROUPS, EXT], F32)
        o_tok = ks
        den = sb("p5_den", [P, 2, HEADS], F32)
        rden = sb("p5_rden", [P, 2, HEADS], F32)
        same_head = sb("p5_same_head", [P, EXT], F32)
        quant = sb("p5_quant", [P, 3], F32)
        bq_c = sb("p5_bq", [P, GROUPS], F32)
        bias = sb("p5_bias", [P, 3, D], F32)
        dec_r = sb("p5_decay_row", [P, SEQ], F32)
        dec_c = sb("p5_decay_col", [P, TT], F32)

        load_w, split_hi, split_lo, w_done, n_w = split_loader(
            nc, ctx, "p5_w", qT[:, :, :], [job for n, w in enumerate((wq, wk, wv, wo)) for job in halves(w, w_hi[:, n, :, :], w_lo[:, n, :, :])])
        ln_a = LayerNorm(nc, ctx, "p5_ln_a")
        ln_b = LayerNorm(nc, ctx, "p5_ln_b")
        A = Banks(nc, ctx, "p5_abank", psum, 0, 4, 4 + 2 * TT + 4 * KT)
        B = Banks(nc, ctx, "p5_bbank", psum, 4, 4, 2 * (GROUPS + 2 * CT) + TT)
        a_x = lambda c, k: KT * c + k
        a_kv = lambda g: 2 * KT + g
        a_o = lambda t, half: 2 * KT + GROUPS + 2 * t + half
        a_oT = lambda c, k: 2 * KT + GROUPS + 2 * TT + KT * c + k
        b_q = lambda c, g: 3 * CT * c + g
        b_k = lambda c, t: 3 * CT * c + CT + t
        b_v = lambda c, t: 3 * CT * c + 2 * CT + t
        b_out = lambda t: 6 * CT + t

        built, consts_loaded = sem("p5_built"), sem("p5_consts_loaded")
        y_loaded = [sem(f"p5_y_loaded{c}") for c in range(2)]
        x1_loaded = sem("p5_x1_loaded")
        max_all, quant_ready = sem("p5_max_all"), sem("p5_quant_ready")
        rounding = sem("p5_rounding")
        t_hi, t_lo = sem("p5_t_hi"), sem("p5_t_lo", 1)
        q_relu, q_done = sem("p5_q_relu"), sem("p5_q_done")
        k_biased, k_done = sem("p5_k_biased"), sem("p5_k_done")
        v_done, kv_done = sem("p5_v_done"), sem("p5_kv_done")
        den_eps, den_inv, o_done = sem("p5_den_eps"), sem("p5_den_inv"), sem("p5_o_done")
        x2_biased, next_loaded = sem("p5_x2_biased"), sem("p5_next_loaded")
        passed = sem("p5_passed")
        residual_stored = [sem(f"p5_residual_stored{c}") for c in range(2)]
        residual_loaded = [sem(f"p5_residual_loaded{c}") for c in range(2)]
        x3_stored = [sem(f"p5_x3_stored{c}", 1) for c in range(2)]
        tok = lambda t: slice(t * P, (t + 1) * P)

        by_tile = lambda ap: ap.rearrange("p (t d) -> p t d", t=CT)
        tiles = lambda ap: ap.rearrange("(t p) d -> p t d", p=P)
        chunk = lambda ap, c: ap[:, CT * c:CT * c + CT, :]

        def load_y(eng, b, c):
            eng.dma_start(by_tile(ys[:, c, :]), tiles(y_dram[2 * b + c])).then_inc(y_loaded[c], 16)

        def load_x1(eng, b, c):
            eng.dma_start(by_tile(x1[:, :]), tiles(x1_dram[2 * b + c])).then_inc(x1_loaded, 16)

        with nc.Block() as block:
            @block.sync
            def _(sp):
                load_y(sp, 0, 0)
                load_x1(sp, 0, 0)
                load_y(sp, 0, 1)
                load_w(sp)
                sp.dma_start(bq_c[:, :], bq).then_inc(consts_loaded, 16)
                for n, vec in enumerate((bk, bv, bo)):
                    sp.dma_start(bias[:, n, :], rows(vec)).then_inc(consts_loaded, 16)
                sp.dma_start(dec_r[:, :], rows(decay_row)).then_inc(consts_loaded, 16)
                sp.dma_start(dec_c[:, :], decay_col).then_inc(consts_loaded, 16)
                sp.wait_ge(ln_a.summed, ln_a.FROM + CT)
                load_x1(sp, 0, 1)

                def body(b, last):
                    for c in range(2):
                        sp.wait_ge(x2_biased, 2 * b + c + 1)
                        sp.dma_start(tiles(residual[2 * b + c]), chunk(x2, c)).then_inc(residual_stored[c], 16)
                    for c in range(2):
                        sp.wait_ge(residual_stored[c], 16 * b + 16)
                        sp.sem_inc(passed, 1)
                        sp.wait_ge(t_lo, 1 + 16 * b + 8 + 4 * c + 4)
                        sp.sem_inc(passed, 1)
                        sp.dma_start(chunk(ks, c), tiles(residual[2 * b + c])).then_inc(residual_loaded[c], 16)
                    if last:
                        sp.wait_ge(x3_stored[0], 1 + 16 * b)
                        sp.dma_start(by_tile(next_x3[:, :]), tiles(x3_dram[0])).then_inc(next_loaded, 16)
                    for c in range(2):
                        sp.wait_ge(ln_b.normed, 8 * b + 4 * c + 4)
                        sp.dma_start(tiles(x3_dram[2 * b + c]), chunk(ks, c)).then_inc(x3_stored[c], 16)
                batches(sp, body)
                for c in range(2):
                    sp.wait_ge(x3_stored[c], 1 + 16 * BATCH)
                sp.wait_ge(next_loaded, 16)

            @block.gpsimd
            def _(pool):
                def build(n, ins):
                    ins.then_inc(built, 1)
                    pool.wait_ge(built, n)
                build(1, pool.memset(same_head[:, :], 0.0))
                for g in range(HPG):
                    build(2 + 2 * g, pool.memset(same_head[g * HD:(g + 1) * HD, g * HD:(g + 1) * HD], 1.0))
                    build(3 + 2 * g, pool.memset(same_head[g * HD:(g + 1) * HD, P + g:P + g + 1], 1.0))
                build(10, pool.memset(vs[:, :, :, P:P + 2], 1.0))
                ln_a.setup(pool)
                ln_b.setup(pool)
                pool.partition_all_reduce(quant[:, 0:1], y_max[:, :], P, bass.bass_isa.ReduceOp.max).then_inc(max_all, 1)
                split_lo(pool, 0, 2)
                ln_a.pool_part(pool, 0)
                split_lo(pool, 2)
                ln_a.pool_part(pool, 1)
                pool.wait_ge(consts_loaded, 16 * 6)

                def body(b, last):
                    def add_bias(c):
                        pool.wait_ge(t_lo, 1 + 16 * b + 4 * c + 4)
                        part = chunk(x2, c)
                        pool.tensor_tensor(part, part, bias[:, 2:3, :].to_broadcast([P, CT, D]), ALU.add).then_inc(x2_biased, 1)

                    add_bias(0)
                    for c in range(2):
                        for g in range(GROUPS):
                            n = GROUPS * c + g
                            q = qT[:, g, c * CH:(c + 1) * CH]
                            pool.wait_ge(q_relu, 8 * b + n + 1)
                            pool.tensor_tensor(q, q, dec_r[:, c * CH:(c + 1) * CH], ALU.mult).then_inc(q_done, 1)
                        if c == 0:
                            add_bias(1)
                        for t in range(CT * c, CT * c + CT):
                            pool.wait_ge(k_biased, 8 * b + t + 1)
                            pool.sem_inc(ln_a.passed, 1)
                            pool.tensor_scalar(ks[:, t, :], ks[:, t, :], 0.0, dec_c[:, t:t + 1], ALU.max, ALU.mult).then_inc(k_done, 1)
                        if not last:
                            ln_a.pool_part(pool, 2 * b + 2 + c)
                    for c in range(2):
                        ln_b.pool_part(pool, 2 * b + c)
                batches(pool, body)

            @block.scalar
            def _(act):
                split_hi(act)
                act.wait_ge(consts_loaded, 16 * 6)

                def part_hi(b, c, entry):
                    for k in range(KT):
                        A.wait_full(act, b, entry(c, k))
                        act.activation(aT_hi[:, c, k, :], A.bank(entry(c, k)), ACT.Copy).then_inc(t_hi, 1)

                part_hi(0, 0, a_x)
                act.wait_ge(w_done, n_w)

                def body(b, last):
                    if not last:
                        act.wait_ge(ln_a.summed, ln_a.FROM + 8 * b + 8)
                        for c in range(2):
                            load_y(act, b + 1, c)
                        load_x1(act, b + 1, 0)
                    for c in range(2):
                        if c == 1:
                            part_hi(b, 1, a_x)
                        if c == 1 and not last:
                            act.wait_ge(ln_a.summed, ln_a.FROM + 8 * b + 12)
                            load_x1(act, b + 1, 1)
                        for g in range(GROUPS):
                            m = b_q(c, g)
                            B.wait_full(act, b, m)
                            act.activation(qT[:, g, c * CH:(c + 1) * CH], B.bank(m), ACT.Relu, bias=bq_c[:, g:g + 1]).then_inc(q_relu, 1)
                    for c in range(2):
                        part_hi(b, c, a_oT)
                    if not last:
                        part_hi(b + 1, 0, a_x)
                batches(act, body)

            @block.tensor
            def _(pe):
                def transposes(b, c, entry, src):
                    for k in range(KT):
                        m = entry(c, k)
                        free_a(b, m)
                        for t in range(CT):
                            mm = pe.transpose(A.bank(m)[:, tok(t)], src(t)[:, tok(k)], ident[:, :])
                        A.fill(mm, m)

                def free_a(b, m):
                    prev = m - 4
                    if prev < 0:
                        pe.wait_ge(t_lo, 1 + 16 * b)
                    elif prev < a_kv(0):
                        pe.wait_ge(t_lo, 1 + 16 * b + prev + 1)
                    elif prev < a_o(0, 0):
                        pe.wait_ge(kv_done, 4 * b + prev - a_kv(0) + 1)
                    elif prev < a_oT(0, 0):
                        pe.wait_ge(o_done, 16 * b + prev - a_o(0, 0) + 1)
                    else:
                        pe.wait_ge(t_lo, 1 + 16 * b + 8 + prev - a_oT(0, 0) + 1)

                def x2_transposes(b, c):
                    pe.wait_ge(ln_a.normed, 8 * b + 4 * c + 4)
                    transposes(b, c, a_x, lambda t: x2[:, CT * c + t, :])

                x2_transposes(0, 0)

                def body(b, last):
                    def free_b(m):
                        prev = m - 4
                        if prev < 0:
                            pe.wait_ge(ln_b.summed, 8 * b + 4 + m + 1)
                        elif prev < b_out(0):
                            c, kind, n = prev // (3 * CT), prev % (3 * CT) // CT, prev % CT
                            pe.wait_ge((q_relu, k_biased, v_done)[kind], 8 * b + CT * c + n + 1)
                        else:
                            pe.wait_ge(ln_b.summed, ln_b.FROM + 8 * b + prev - b_out(0) + 1)

                    def product(c, n, a_cols, w_cols, a_is_lhs):
                        pe.wait_ge(w_done, 2 * n + 2)
                        terms = []
                        for k in range(KT):
                            for a, w in ((aT_hi, w_hi), (aT_lo, w_hi), (aT_hi, w_lo)):
                                pair = (a[:, c, k, a_cols], w[:, n, k, w_cols])
                                terms.append(pair if a_is_lhs else pair[::-1])
                        return terms

                    everything = slice(0, D)
                    for c in range(2):
                        pe.wait_ge(t_lo, 1 + 16 * b + 4 * c + 4)
                        for g in range(GROUPS):
                            free_b(b_q(c, g))
                            B.fill(partials(pe, B.bank(b_q(c, g)), product(c, 0, everything, tok(g), False)), b_q(c, g))
                        if c == 0:
                            x2_transposes(b, 1)
                        for n, entry in ((1, b_k), (2, b_v)):
                            for t in range(CT):
                                free_b(entry(c, t))
                                B.fill(partials(pe, B.bank(entry(c, t)), product(c, n, tok(t), everything, True)), entry(c, t))
                    pe.wait_ge(k_done, 8 * b + 8)
                    pe.wait_ge(v_done, 8 * b + 8)
                    for g in range(GROUPS):
                        m = a_kv(g)
                        free_a(b, m)
                        A.fill(partials(pe, A.bank(m)[:, 0:P + 2], [(ks[:, t, tok(g)], vs[:, t, g, :]) for t in range(TT)]), m)
                    pe.wait_ge(q_done, 8 * b + 8)
                    for t in range(TT):
                        for half in range(2):
                            m = a_o(t, half)
                            free_a(b, m)
                            if t == 0:
                                pe.wait_ge(kv_done, 4 * b + 2 * half + 2)
                            for g in (2 * half, 2 * half + 1):
                                mm = pe.matmul(A.bank(m)[:, (g % 2) * EXT:(g % 2 + 1) * EXT], qT[:, g, tok(t)], kv[:, g, :],
                                               start=True, stop=True)
                            A.fill(mm, m)
                    for c in range(2):
                        pe.wait_ge(o_done, 16 * b + 8 * c + 8)
                        transposes(b, c, a_oT, lambda t: o_tok[:, CT * c + t, :])
                    for c in range(2):
                        pe.wait_ge(t_lo, 1 + 16 * b + 8 + 4 * c + 4)
                        for t in range(CT):
                            m = b_out(CT * c + t)
                            free_b(m)
                            B.fill(partials(pe, B.bank(m), product(c, 3, tok(t), everything, True)), m)
                        if c == 0 and not last:
                            x2_transposes(b + 1, 0)
                batches(pe, body)

            @block.vector
            def _(dve):
                dve.sem_inc(ln_a.summed, ln_a.FROM)
                dve.sem_inc(ln_b.summed, ln_b.FROM)
                dve.wait_ge(max_all, 1)
                dve.tensor_scalar(quant[:, 1:2], quant[:, 0:1], 1.0 / QMAX, FP4_EPS, ALU.mult, ALU.add).then_inc(quant_ready, 1)
                dve.wait_ge(quant_ready, 1)
                dve.reciprocal(quant[:, 2:3], quant[:, 1:2]).then_inc(quant_ready, 1)
                dve.wait_ge(quant_ready, 2)

                def quantize(b, c):
                    y = ys[:, c, :]
                    dve.wait_ge(y_loaded[c], 16 * b + 16)
                    dve.tensor_scalar(y, y, quant[:, 2:3], ROUND, ALU.mult, ALU.add).then_inc(rounding, 1)
                    dve.wait_ge(rounding, 6 * b + 3 * c + 1)
                    dve.tensor_scalar(y, y, -ROUND, QMAX, ALU.add, ALU.min).then_inc(rounding, 1)
                    dve.wait_ge(rounding, 6 * b + 3 * c + 2)
                    dve.tensor_scalar(y, y, -QMAX, quant[:, 1:2], ALU.max, ALU.mult).then_inc(rounding, 1)

                def add_x1(b, c, first=False):
                    dve.wait_ge(rounding, 6 * b + 3 * c + 3)
                    dve.wait_ge(x1_loaded, 32 * b + 16 * c + 16)
                    if not first:
                        dve.wait_ge(residual_stored[c], 16 * b)
                    for t in range(CT):
                        cols = slice(t * D, (t + 1) * D)
                        dve.tensor_tensor(x2[:, CT * c + t, :], ys[:, c, cols], x1[:, cols], ALU.add).then_inc(ln_a.summed, 1)

                x2_tile = lambda c: (lambda t: x2[:, CT * c + t, :])

                def part_lo(b, c, entry, first):
                    for k in range(KT):
                        dve.wait_ge(t_hi, 16 * b + first + KT * c + k + 1)
                        dve.tensor_tensor(aT_lo[:, c, k, :], A.bank(entry(c, k)), f32(aT_hi[:, c, k, :]), ALU.subtract).then_inc(t_lo, 1)

                for c in range(2):
                    quantize(0, c)
                    add_x1(0, c, True)
                    ln_a.vector_part(dve, c, x2_tile(c), x2_tile(c))
                    if c == 0:
                        part_lo(0, 0, a_x, 0)
                dve.wait_ge(built, 10)
                dve.wait_ge(consts_loaded, 16 * 6)

                def body(b, last):
                    def keys(c):
                        dve.wait_ge(x3_stored[c], 1 + 16 * b)
                        for t in range(CT):
                            B.wait_full(dve, b, b_k(c, t))
                            dve.tensor_tensor(ks[:, CT * c + t, :], B.bank(b_k(c, t)), bias[:, 0, :], ALU.add).then_inc(k_biased, 1)

                    def values(c):
                        for t in range(CT):
                            B.wait_full(dve, b, b_v(c, t))
                            heads = lambda ap: ap.rearrange("p (g e) -> p g e", g=GROUPS)
                            dve.tensor_tensor(vs[:, CT * c + t, :, 0:P], heads(B.bank(b_v(c, t))), heads(bias[:, 1, :]), ALU.add).then_inc(v_done, 1)

                    if not last:
                        quantize(b + 1, 0)
                    part_lo(b, 1, a_x, 0)
                    for c in range(2):
                        keys(c)
                        if not last:
                            add_x1(b + 1, c)
                        values(c)
                        if not last:
                            ln_a.find_statistics(dve, 2 * b + 2 + c, x2_tile(c))
                        if c == 0 and not last:
                            ln_a.normalize_tiles(dve, 2 * b + 2, x2_tile(0), x2_tile(0))
                            quantize(b + 1, 1)
                    for g in range(GROUPS):
                        bank = A.bank(a_kv(g))
                        A.wait_full(dve, b, a_kv(g))
                        dve.tensor_tensor(kv[:, g, 0:P], bank[:, 0:P], same_head[:, 0:P], ALU.mult)
                        dve.tensor_scalar(kv[:, g, P:EXT], same_head[:, P:EXT], bank[:, P:P + 1], None, ALU.mult).then_inc(kv_done, 1)
                    for t in range(TT):
                        halves = [A.bank(a_o(t, half))[:, 0:2 * EXT].rearrange("p (g e) -> p g e", g=2) for half in range(2)]
                        slot = lambda ap: ap[:, t % 2, :]
                        for half in range(2):
                            A.wait_full(dve, b, a_o(t, half))
                            dve.tensor_scalar(slot(den)[:, half * 2 * HPG:(half + 1) * 2 * HPG].rearrange("p (g h) -> p g h", g=2),
                                              halves[half][:, :, P:EXT], LIN_EPS, None, ALU.add).then_inc(den_eps, 1)
                        dve.wait_ge(den_eps, 16 * b + 2 * t + 2)
                        dve.reciprocal(slot(rden), slot(den)).then_inc(den_inv, 1)
                        dve.wait_ge(den_inv, 8 * b + t + 1)
                        for half in range(2):
                            for g in range(2):
                                at = (2 * half + g) * P
                                heads = lambda ap: ap.rearrange("p (h e) -> p h e", h=HPG)
                                inv = slot(rden)[:, (2 * half + g) * HPG:(2 * half + g + 1) * HPG]
                                ins = dve.tensor_tensor(heads(o_tok[:, t, at:at + P]), heads(halves[half][:, g, 0:P]),
                                                        inv[:, :, None].to_broadcast([P, HPG, HD]), ALU.mult)
                            ins.then_inc(o_done, 1)
                    for c in range(2):
                        part_lo(b, c, a_oT, 8)
                    if not last:
                        ln_a.normalize_tiles(dve, 2 * b + 3, x2_tile(1), x2_tile(1))
                    for c in range(2):
                        dve.wait_ge(residual_loaded[c], 16 * b + 16)
                        for t in range(CT):
                            m = b_out(CT * c + t)
                            at = ks[:, CT * c + t, :]
                            B.wait_full(dve, b, m)
                            dve.tensor_tensor(at, B.bank(m), at, ALU.add).then_inc(ln_b.summed, 1)
                        x3_tile = lambda t: ks[:, CT * c + t, :]
                        ln_b.vector_part(dve, 2 * b + c, x3_tile, x3_tile)
                        if c == 0 and not last:
                            part_lo(b + 1, 0, a_x, 0)
                batches(dve, body)


def phase_ffn1(nc, psum, w0, b0, w1, b1, x3_first, x3_dram, out):
    with Phase(nc) as ctx:
        sb = lambda n, s, d: ctx.enter_context(nc.sbuf_tensor(n, s, d))
        sem = ctx.semaphore
        w0_hi = sb("p6_w0_hi", [P, KT, HID], F32R)
        w0_lo = sb("p6_w0_lo", [P, KT, HID], F32R)
        w1_hi = sb("p6_w1_hi", [P, HT, D], F32R)
        w1_lo = sb("p6_w1_lo", [P, HT, D], F32R)
        stage = sb("p6_stage", [P, 4, D * CT // 2], F32)
        x3 = (x3_first, sb("p6_x3", [P, CT * D], F32))
        x16 = sb("p6_x16", [P, CT, D], F16)
        xT = sb("p6_xT", [P, 2, KT, CH], F32R)
        h16 = sb("p6_h16", [P, 2, CH], F16)
        h = sb("p6_h", [P, 2, CH], F32R)
        e16 = sb("p6_e16", [P, CT, D], F16)
        res = sb("p6_out", [P, CT, D], F32)
        ident16 = sb("p6_ident16", [P, P], F16)
        b0c = sb("p6_b0", [P, HT], F32)
        b1r = sb("p6_b1", [P, D], F32)
        w0_v = w0.rearrange("(k p) n -> p k n", p=P)
        w1_v = w1.rearrange("(t p) n -> p t n", p=P)
        blocks = [("w0", 0)]
        for n in range(1, HT // 2):
            blocks += [("w0", n), ("w1", n - 1)]
        blocks.append(("w1", HT // 2 - 1))
        n_w = len(blocks)
        n_slots = stage.shape[1]
        w_loaded = [sem(f"p6_w_loaded{k}") for k in range(n_slots)]
        w_hi_done, w_done = sem("p6_w_hi_done"), sem("p6_w_done")

        def block_views(which, n):
            if which == "w0":
                cols = slice(2 * P * n, 2 * P * (n + 1))
                return w0_v[:, :, cols], w0_hi[:, :, cols], w0_lo[:, :, cols]
            tiles = slice(2 * n, 2 * n + 2)
            return w1_v[:, tiles, :], w1_hi[:, tiles, :], w1_lo[:, tiles, :]

        ln = LayerNorm(nc, ctx, "p6_ln")
        Y = Banks(nc, ctx, "p6_ybank", psum, 0, CT, 2 * CT)
        H = Banks(nc, ctx, "p6_hbank", psum, 4, 2, 2 * HT)
        T = Banks(nc, ctx, "p6_tbank", psum, 6, 2, 2 * KT)
        built, b0_loaded, bias_loaded = sem("p6_built"), sem("p6_b0_loaded"), sem("p6_bias_loaded")
        x_loaded = [sem("p6_x_loaded0", 16), sem("p6_x_loaded1")]
        passed = sem("p6_passed")
        x_cast = sem("p6_x_cast")
        h_done, h_used = sem("p6_h_done", 2), sem("p6_h_used", 1)
        stored = sem("p6_stored", 1)

        with nc.Block() as block:
            @block.sync
            def _(sp):
                tiles = lambda ap: ap.rearrange("(t p) d -> p t d", p=P)

                def load_x(b, c):
                    sp.dma_start(x3[c][:, :].rearrange("p (t d) -> p t d", t=CT), tiles(x3_dram[2 * b + c])).then_inc(x_loaded[c], 16)

                for i, (which, n) in enumerate(blocks):
                    src, hi, _ = block_views(which, n)
                    if i >= n_slots:
                        sp.wait_ge(w_done, i - n_slots + 1)
                    sp.dma_start(stage[:, i % n_slots, :].rearrange("p (k n) -> p k n", k=hi.shape[1]), src).then_inc(w_loaded[i % n_slots], 16)
                    if i == 0:
                        sp.dma_start(b0c[:, :], b0).then_inc(b0_loaded, 16)
                sp.dma_start(b1r[:, :], rows(b1)).then_inc(bias_loaded, 16)
                load_x(0, 1)

                def body(b, last):
                    for c in range(2):
                        sp.wait_ge(ln.summed, ln.FROM + CT + 8 * b + 4 * c + 4)
                        if not last:
                            load_x(b + 1, c)
                        sp.wait_ge(ln.normed, 8 * b + 4 * c + 4)
                        sp.dma_start(tiles(out[2 * b + c]), res[:, :, :]).then_inc(stored, 16)
                batches(sp, body)
                sp.wait_ge(stored, 1 + 16 * NCH)

            @block.gpsimd
            def _(pool):
                pool.memset(ident16[:, :], 0.0).then_inc(built, 1)
                pool.wait_ge(built, 1)
                pool.affine_select(out=ident16[:, :], in_=ident16[:, :], compare_op=ALU.not_equal, fill=1.0, base=0,
                                   pattern=[[-1, P]], channel_multiplier=1).then_inc(built, 1)
                pool.wait_ge(built, 2)
                ln.setup(pool)

                def body(b, last):
                    for c in range(2):
                        for t in range(HT):
                            m = HT * c + t
                            H.wait_freed(pool, m % 2, HT * b + m // 2 + 1)
                            pool.sem_inc(passed, 1)
                            if t == 1:
                                Y.wait_filled(pool, CT - 1, 2 * b + c)
                            else:
                                pool.wait_ge(h_used, 1 + (HT - 1) * (2 * b + c) + max(0, t - 1))
                            pool.sem_inc(passed, 1)
                            pool.tensor_copy(h[:, t % 2, :], h16[:, t % 2, :]).then_inc(h_done, 1)
                            if t == HT // 4:
                                ln.pool_part(pool, 2 * b + c)
                batches(pool, body)
                ln.pool_part(pool, NCH)

            @block.scalar
            def _(act):
                def x_T(b, c, k):
                    m = KT * c + k
                    T.wait_full(act, b, m)
                    T.free(act.activation(xT[:, c, k, :], T.bank(m).bitcast(F16)[:, 0:CH], ACT.Copy), m)

                for k in range(KT):
                    x_T(0, 0, k)
                act.preload_act_table(ACT.Gelu)
                act.wait_ge(b0_loaded, 16)

                def body(b, last):
                    for c in range(2):
                        for t in range(HT):
                            m = HT * c + t
                            H.wait_full(act, b, m)
                            act.wait_ge(h_done, 2 * HT * b + m + 1)
                            H.free(act.activation(h16[:, t % 2, :], H.bank(m), ACT.Gelu, bias=b0c[:, t:t + 1]), m)
                            if HT // 2 < t <= HT // 2 + KT and not (c and last):
                                x_T(b + c, 1 - c, t - HT // 2 - 1)
                batches(act, body)

            @block.tensor
            def _(pe):
                pe.wait_ge(built, 2)

                def transposes(b, c, k):
                    pe.wait_ge(x_cast, 2 * b + c + 1)
                    m = KT * c + k
                    T.wait_free(pe, b, m)
                    for t in range(CT):
                        mm = pe.transpose(T.bank(m).bitcast(F16)[:, t * P:(t + 1) * P], x16[:, t, k * P:(k + 1) * P], ident16[:, :])
                    T.fill(mm, m)

                def hidden(b, c, t):
                    if t == 0:
                        for k in range(2):
                            T.wait_freed(pe, k, 4 * b + 2 * c + 2)
                    pe.wait_ge(w_done, blocks.index(("w0", t // 2)) + 1)
                    m = HT * c + t
                    H.wait_free(pe, b, m)
                    H.fill(partials(pe, H.bank(m), [
                        (w[:, k, t * P:(t + 1) * P], xT[:, c, k, :]) for k in range(KT) for w in (w0_hi, w0_lo)]), m)

                for k in range(KT):
                    transposes(0, 0, k)
                hidden(0, 0, 0)

                def body(b, last):
                    def to_y(c, t):
                        pe.wait_ge(h_done, 2 + 2 * HT * b + HT * c + t + 1)
                        pe.wait_ge(w_done, blocks.index(("w1", t // 2)) + 1)
                        for a in range(CT):
                            m = CT * c + a
                            if t == 0:
                                Y.wait_free(pe, b, m)
                            for part, w in enumerate((w1_hi, w1_lo)):
                                mm = pe.matmul(Y.bank(m), h[:, t % 2, a * P:(a + 1) * P], w[:, t, :], start=(t == 0 and part == 0),
                                               stop=(t == HT - 1 and part == 1))
                            if t == HT - 1:
                                Y.fill(mm, m)
                        if t < HT - 1:
                            mm.then_inc(h_used, 1)

                    for c in range(2):
                        for t in range(HT):
                            if t < HT - 1:
                                hidden(b, c, t + 1)
                            elif not (c and last):
                                hidden(b + c, 1 - c, 0)
                            to_y(c, t)
                            if HT // 2 <= t < HT // 2 + KT and not (c and last):
                                transposes(b + c, 1 - c, t - HT // 2)
                batches(pe, body)

            @block.vector
            def _(dve):
                dve.sem_inc(ln.summed, ln.FROM + CT)
                dve.sem_inc(ln.got_stats, CT)
                dve.memset(ln.meanvar[:, :, :], 1.0).then_inc(ln.got_mean, CT)

                def cast(b, c):
                    dve.wait_ge(x_loaded[c], 16 * b + 16)
                    for k in range(2):
                        T.wait_filled(dve, k, 4 * b + 2 * c)
                    dve.tensor_copy(x16[:, :, :].rearrange("p t d -> p (t d)"), x3[c][:, :]).then_inc(x_cast, 1)

                cast(0, 0)
                for i, (which, n) in enumerate(blocks):
                    _, hi, lo = block_views(which, n)
                    w = stage[:, i % n_slots, :].rearrange("p (k n) -> p k n", k=hi.shape[1])
                    dve.wait_ge(w_loaded[i % n_slots], 16 * (i // n_slots + 1))
                    dve.tensor_copy(hi, w).then_inc(w_hi_done, 1)
                    dve.wait_ge(w_hi_done, i + 1)
                    dve.tensor_tensor(lo, w, f32(hi), ALU.subtract).then_inc(w_done, 1)
                dve.wait_ge(bias_loaded, 16)

                def body(b, last):
                    for c in range(2):
                        if not (c and last):
                            cast(b + c, 1 - c)
                        for a in range(CT):
                            m = CT * c + a
                            Y.wait_full(dve, b, m)
                            Y.free(dve.tensor_tensor(e16[:, a, :], Y.bank(m), b1r[:, :], ALU.add), m)
                        dve.wait_ge(stored, 1 + 32 * b + 16 * c)
                        for a in range(CT):
                            Y.wait_freed(dve, a, 2 * b + c + 1)
                            dve.tensor_tensor(res[:, a, :], x3[c][:, a * D:(a + 1) * D], e16[:, a, :], ALU.add).then_inc(ln.summed, 1)
                        ln.vector_part(dve, 2 * b + c + 1, lambda t: res[:, t, :], lambda t: res[:, t, :])
                batches(dve, body)


def build_program(nc, x, l0_wq, l0_wk, l0_wv, l0_wo, l0_bo, f0_w1, f0_b1, f0_w2, f0_b2,
                  l1_wq, l1_bq, l1_wk, l1_bk, l1_wv, l1_bv, l1_wo, l1_bo, f1_w0, f1_b0, f1_w1, f1_b1,
                  decay_row, decay_col, out):
    groups = BATCH * GROUPS
    q_dram = nc.dram_tensor("q_parts", [groups, 2, P, SEQ], F32)
    k_dram = nc.dram_tensor("k_parts", [groups, 2, P, SEQ], F32)
    v_dram = nc.dram_tensor("v_rows", [groups, SEQ, P], F32)
    o_dram = nc.dram_tensor("attention_out", [groups, P, SEQ], F32)
    x1_dram = nc.dram_tensor("x1", [NCH, CH, D], F32)
    y_dram = nc.dram_tensor("ffn0_out", [NCH, CH, D], F32)
    residual = nc.dram_tensor("residual", [NCH, CH, D], F32)
    x3_dram = nc.dram_tensor("x3", [NCH, CH, D], F32)
    with Phase(nc) as ctx:
        psum = ctx.enter_context(nc.psum_tensor("psum", [P, 8, CH], F32))
        y_max = ctx.enter_context(nc.sbuf_tensor("y_max", [P, 1], F32))
        ident = build_constants(nc, ctx)
        with ExitStack() as layer0:
            sb = lambda n, s, d: layer0.enter_context(nc.sbuf_tensor(n, s, d))
            w_max = sb("w_max", [P, 2], F32)
            ffn_w = (f0_w1, f0_w2)
            phase_qkv0(nc, psum, ident, x, l0_wq, l0_wk, l0_wv, q_dram, k_dram, v_dram, ffn_w, w_max)
            tern = sb("tern", [P, 2, KT * HID], F32R)
            kept = sb("kept", [P, 2, 8, KT * HID // 64], F32)
            alpha = sb("alpha", [P, 2], F32)
            phase_attention(nc, psum, ident, q_dram, k_dram, v_dram, o_dram, ffn_w, w_max, tern, kept)
            ffn0_x1 = sb("ffn0_x1", [P, CT, D], F32)
            phase_out0(nc, psum, x, l0_wo, l0_bo, o_dram, x1_dram, tern, kept, alpha, ffn0_x1)
            phase_ffn0(nc, psum, ident, tern, alpha, f0_b1, f0_b2, ffn0_x1, x1_dram, y_dram, y_max)
        x3_first = ctx.enter_context(nc.sbuf_tensor("ffn1_x3", [P, CT * D], F32))
        phase_linear_attention(nc, psum, ident, y_max, y_dram, x1_dram, l1_wq, l1_wk, l1_wv, l1_wo,
                               l1_bq, l1_bk, l1_bv, l1_bo, decay_row, decay_col, residual, x3_dram, x3_first)
        phase_ffn1(nc, psum, f1_w0, f1_b0, f1_w1, f1_b1, x3_first, x3_dram, out.rearrange("b (c t) d -> (b c) t d", c=2))


def kernel(**inputs):
    import concourse.bacc as bacc
    from concourse.bass_utils import run_bass_kernel_spmd

    i = {k: np.ascontiguousarray(v) for k, v in inputs.items()}
    by_partition = lambda v: np.ascontiguousarray(v.reshape(-1, P).T)
    transposed = lambda w: np.ascontiguousarray(w.T)
    decay = np.exp(-np.arange(SEQ, dtype=np.float32) / np.float32(SEQ)).astype(np.float32)
    arrays = {
        "x": i["L0_attn_x"], "l0_wq": i["L0_attn_wq"], "l0_wk": i["L0_attn_wk"], "l0_wv": i["L0_attn_wv"],
        "l0_wo": i["L0_attn_wo"], "l0_bo": i["L0_attn_bo"],
        "f0_w1": transposed(i["L0_ffn_W1"]), "f0_b1": by_partition(i["L0_ffn_b1"]),
        "f0_w2": transposed(i["L0_ffn_W2"]), "f0_b2": i["L0_ffn_b2"],
        "l1_wq": transposed(i["L1_attn_Wq"]), "l1_bq": by_partition(i["L1_attn_bq"]),
        "l1_wk": transposed(i["L1_attn_Wk"]), "l1_bk": i["L1_attn_bk"],
        "l1_wv": transposed(i["L1_attn_Wv"]), "l1_bv": i["L1_attn_bv"],
        "l1_wo": transposed(i["L1_attn_Wo"]), "l1_bo": i["L1_attn_bo"],
        "f1_w0": transposed(i["L1_ffn_W0"]), "f1_b0": by_partition(i["L1_ffn_bias0"]),
        "f1_w1": transposed(i["L1_ffn_W1"]), "f1_b1": i["L1_ffn_bias1"],
        "decay_row": decay, "decay_col": by_partition(decay),
    }
    nc = bacc.Bacc("TRN2", target_bir_lowering=False, num_devices=1)
    args = [nc.dram_tensor(f"in_{n}", a.shape, mybir.dt.from_np(a.dtype), kind="ExternalInput").ap() for n, a in arrays.items()]
    out = nc.dram_tensor("out", (BATCH, SEQ, D), F32, kind="ExternalOutput").ap()
    build_program(nc, *args, out)
    result = run_bass_kernel_spmd(nc, [{f"in_{n}": a for n, a in arrays.items()}], core_ids=[0])
    return result.results[0]["out"]
```
